# Optimizing a Trainium2 kernel written in Bass

```python
import numpy as np
import jax
import jax.numpy as jnp

def _softmax(x, axis=-1):
    return jax.nn.softmax(x, axis=axis)

def _gelu(x):
    return jax.nn.gelu(x, approximate=True)

def _silu(x):
    return jax.nn.silu(x)

def _sigmoid(x):
    return jax.nn.sigmoid(x)

def _layernorm(x, axis=-1, eps=1e-05):
    m = jnp.mean(x, axis=axis, keepdims=True)
    v = jnp.var(x, axis=axis, keepdims=True)
    return (x - m) / jnp.sqrt(v + eps)

def _scatter_add(tgt, idx, src, axis=0):
    return tgt.at[idx].add(src)

def _segment_sum(src, seg, n):
    return jax.ops.segment_sum(src, seg, n)
kernel_name = 'mk_gnn_preln_d4_gnn_r8_54a30b'

def setup_inputs(seed: int=0):
    np.random.seed(seed)
    _w = jnp.asarray

    def _rec_inputs():
        import jax
        import jax.numpy as jnp
        _gk = jax.random.key(seed)
        x = -0.0003713 + 1 * jax.random.normal(jax.random.fold_in(_gk, 1), (6250, 128), jnp.float32)
        src = jax.random.randint(jax.random.fold_in(_gk, 2), (200000,), 0, 6250, jnp.int32)
        dst = jax.random.randint(jax.random.fold_in(_gk, 3), (200000,), 0, 6250, jnp.int32)
        _o = jnp.argsort(dst, stable=True)
        src = src[_o]
        dst = dst[_o]
        edge_attr_32 = -5.3897e-05 + 0.999841 * jax.random.normal(jax.random.fold_in(_gk, 12), (200000, 32), jnp.float32)
        edge_attr_50 = 0.000154925 + 1.00009 * jax.random.normal(jax.random.fold_in(_gk, 13), (200000, 50), jnp.float32)
        edge_weight = jax.random.uniform(jax.random.fold_in(_gk, 15), (200000,), jnp.float32, 0.0, 1)
        node_vec1 = jax.random.uniform(jax.random.fold_in(_gk, 16), (6250, 1), jnp.float32, 0.0, 1)
        return (x, src, dst, edge_attr_32, edge_attr_50, edge_weight, node_vec1)
    x, src, dst, edge_attr_32, edge_attr_50, edge_weight, node_vec1 = _rec_inputs()

    def _L0_gnn_setup():
        import jax, jax.numpy as jnp
        import numpy as np
        N = 12500
        E = 80000
        D = 128

        def _weighted_mean_agg(ft, w, src, dst, n_nodes):
            m = ft[src] * w[:, None]
            msum = jax.ops.segment_sum(m, dst, num_segments=n_nodes)
            wsum = jax.ops.segment_sum(w, dst, num_segments=n_nodes)
            safe = jnp.where(wsum > 0, wsum, 1.0)
            return jnp.where((wsum > 0)[:, None], msum / safe[:, None], 0.0)
        key = jax.random.key(seed)
        ks = jax.random.split(key, 10)
        s = 1.0 / np.sqrt(D)
        feat = jax.random.normal(ks[0], (N, D), jnp.float32)
        w = jax.random.uniform(ks[1], (E,), jnp.float32)
        src = jax.random.randint(ks[2], (E,), 0, N, dtype=jnp.int32)
        dst = jax.random.randint(ks[3], (E,), 0, N, dtype=jnp.int32)
        W1 = jax.random.uniform(ks[4], (D, D), jnp.float32, -s, s)
        W2 = jax.random.uniform(ks[5], (D, D), jnp.float32, -s, s)
        sg = 1.0 / np.sqrt(D)
        w_ih = jax.random.uniform(ks[6], (3 * D, 2 * D), jnp.float32, -sg, sg)
        w_hh = jax.random.uniform(ks[7], (3 * D, D), jnp.float32, -sg, sg)
        b_ih = jax.random.uniform(ks[8], (3 * D,), jnp.float32, -sg, sg)
        b_hh = jax.random.uniform(ks[9], (3 * D,), jnp.float32, -sg, sg)
        return {'feat': feat, 'w': w, 'src': src, 'dst': dst, 'W1': W1, 'W2': W2, 'w_ih': w_ih, 'w_hh': w_hh, 'b_ih': b_ih, 'b_hh': b_hh}
    _L0_gnn_all = _L0_gnn_setup()
    _L0_gnn_in = {k: v for k, v in _L0_gnn_all.items() if k in ('W1', 'W2', 'w_ih', 'w_hh', 'b_ih', 'b_hh')}
    del _L0_gnn_all

    def _L1_gnn_setup():
        import jax, jax.numpy as jnp
        import numpy as np
        N = 12500
        E = 200000
        D_IN = 128
        D_HID = 128
        D_OUT = 128
        EPS = 1e-05

        def _gcn_conv(x, W, b, src, dst, edge_norm, num_nodes):
            h = x @ W
            msg = h[src] * edge_norm[:, None]
            agg = jax.ops.segment_sum(msg, dst, num_segments=num_nodes)
            return agg + b

        def _batch_norm(x, gamma, beta):
            m = jnp.mean(x, axis=0)
            v = jnp.mean(jnp.square(x - m), axis=0)
            return (x - m) * jax.lax.rsqrt(v + EPS) * gamma + beta
        key = jax.random.key(seed)
        ks = jax.random.split(key, 8)
        x = jax.random.normal(ks[0], (N, D_IN), dtype=jnp.float32)
        edge_index = jax.random.randint(ks[1], (2, E), 0, N, dtype=jnp.int64)
        W1 = jax.random.normal(ks[2], (D_IN, D_HID), dtype=jnp.float32) / np.sqrt(D_IN)
        b1 = jnp.zeros((D_HID,), dtype=jnp.float32)
        g1 = jnp.ones((D_HID,), dtype=jnp.float32)
        bt1 = jnp.zeros((D_HID,), dtype=jnp.float32)
        W2 = jax.random.normal(ks[3], (D_HID, D_OUT), dtype=jnp.float32) / np.sqrt(D_HID)
        b2 = jnp.zeros((D_OUT,), dtype=jnp.float32)
        g2 = jnp.ones((D_OUT,), dtype=jnp.float32)
        bt2 = jnp.zeros((D_OUT,), dtype=jnp.float32)
        return {'x': x, 'edge_index': edge_index, 'W1': W1, 'b1': b1, 'g1': g1, 'bt1': bt1, 'W2': W2, 'b2': b2, 'g2': g2, 'bt2': bt2}
    _L1_gnn_all = _L1_gnn_setup()
    _L1_gnn_in = {k: v for k, v in _L1_gnn_all.items() if k in ('W1', 'b1', 'g1', 'bt1', 'W2', 'b2', 'g2', 'bt2')}
    del _L1_gnn_all

    def _L2_gnn_setup():
        import jax, jax.numpy as jnp
        import numpy as np
        N = 6250
        DEG = 16
        E = N * DEG
        DIM = 128
        EDGE_DIM = 32
        EPS = 1e-05

        def _ln(x, scale, offset, mask):
            m = jnp.mean(x, axis=-1, keepdims=True)
            v = jnp.mean(jnp.square(x - m), axis=-1, keepdims=True)
            return ((x - m) * jax.lax.rsqrt(v + EPS) * scale + offset) * mask
        key = jax.random.key(seed)
        ks = jax.random.split(key, 12)
        node_inp = jax.random.normal(ks[0], (N, DIM), jnp.float32)
        edge_feat = jax.random.normal(ks[1], (E, EDGE_DIM), jnp.float32)
        node_mask = jnp.ones((N, 1), jnp.float32)
        senders = jax.random.randint(ks[2], (E,), 0, N, jnp.int32)
        receivers = jnp.repeat(jnp.arange(N, dtype=jnp.int32), DEG)
        din_e = 2 * DIM + EDGE_DIM
        s = lambda d: 1.0 / np.sqrt(d)
        We1 = jax.random.normal(ks[3], (din_e, 2 * DIM), jnp.float32) * s(din_e)
        be1 = jnp.zeros((2 * DIM,), jnp.float32)
        We2 = jax.random.normal(ks[4], (2 * DIM, DIM), jnp.float32) * s(2 * DIM)
        be2 = jnp.zeros((DIM,), jnp.float32)
        g_msg = jnp.ones((DIM,), jnp.float32)
        b_msg = jnp.zeros((DIM,), jnp.float32)
        Wn1 = jax.random.normal(ks[5], (2 * DIM, 2 * DIM), jnp.float32) * s(2 * DIM)
        bn1 = jnp.zeros((2 * DIM,), jnp.float32)
        Wn2 = jax.random.normal(ks[6], (2 * DIM, DIM), jnp.float32) * s(2 * DIM)
        bn2 = jnp.zeros((DIM,), jnp.float32)
        g_node = jnp.ones((DIM,), jnp.float32)
        b_node = jnp.zeros((DIM,), jnp.float32)
        return dict(node_inp=node_inp, edge_feat=edge_feat, node_mask=node_mask, We1=We1, be1=be1, We2=We2, be2=be2, g_msg=g_msg, b_msg=b_msg, Wn1=Wn1, bn1=bn1, Wn2=Wn2, bn2=bn2, g_node=g_node, b_node=b_node, senders=senders, receivers=receivers)
    _L2_gnn_all = _L2_gnn_setup()
    _L2_gnn_in = {k: v for k, v in _L2_gnn_all.items() if k in ('We1', 'be1', 'We2', 'be2', 'g_msg', 'b_msg', 'Wn1', 'bn1', 'Wn2', 'bn2', 'g_node', 'b_node')}
    del _L2_gnn_all

    def _L3_gnn_setup():
        import jax, jax.numpy as jnp
        import numpy as np
        PI = float(np.pi)
        CUTOFF = 10.0
        LOG2 = float(np.log(2.0))

        def ssp(x):
            return jax.nn.softplus(x) - LOG2
        key = jax.random.key(seed)
        ks = jax.random.split(key, 12)
        N, E, H, G, Fw = (6250, 100000, 128, 50, 128)
        x = jax.random.normal(ks[0], (N, H), dtype=jnp.float32)
        edge_index = jax.random.randint(ks[1], (2, E), 0, N, dtype=jnp.int64)
        edge_weight = jax.random.uniform(ks[2], (E,), dtype=jnp.float32) * CUTOFF
        edge_attr = jax.random.normal(ks[3], (E, G), dtype=jnp.float32)

        def xavier(k, shape):
            fan_in, fan_out = (shape[1], shape[0])
            s = float(np.sqrt(6.0 / (fan_in + fan_out)))
            return jax.random.uniform(k, shape, dtype=jnp.float32, minval=-s, maxval=s)
        mlp_w1 = xavier(ks[4], (Fw, G))
        mlp_b1 = jnp.zeros((Fw,), dtype=jnp.float32)
        mlp_w2 = xavier(ks[5], (Fw, Fw))
        mlp_b2 = jnp.zeros((Fw,), dtype=jnp.float32)
        lin1_w = xavier(ks[6], (Fw, H))
        lin2_w = xavier(ks[7], (H, Fw))
        lin2_b = jnp.zeros((H,), dtype=jnp.float32)
        return {'x': x, 'edge_index': edge_index, 'edge_weight': edge_weight, 'edge_attr': edge_attr, 'mlp_w1': mlp_w1, 'mlp_b1': mlp_b1, 'mlp_w2': mlp_w2, 'mlp_b2': mlp_b2, 'lin1_w': lin1_w, 'lin2_w': lin2_w, 'lin2_b': lin2_b}
    _L3_gnn_all = _L3_gnn_setup()
    _L3_gnn_in = {k: v for k, v in _L3_gnn_all.items() if k in ('mlp_w1', 'mlp_b1', 'mlp_w2', 'mlp_b2', 'lin1_w', 'lin2_w', 'lin2_b')}
    del _L3_gnn_all
    return {'x': x, 'src': src, 'dst': dst, 'edge_attr_32': edge_attr_32, 'edge_attr_50': edge_attr_50, 'edge_weight': edge_weight, 'node_vec1': node_vec1, 'L0_gnn_W1': _L0_gnn_in['W1'], 'L0_gnn_W2': _L0_gnn_in['W2'], 'L0_gnn_w_ih': _L0_gnn_in['w_ih'], 'L0_gnn_w_hh': _L0_gnn_in['w_hh'], 'L0_gnn_b_ih': _L0_gnn_in['b_ih'], 'L0_gnn_b_hh': _L0_gnn_in['b_hh'], 'L1_gnn_W1': _L1_gnn_in['W1'], 'L1_gnn_b1': _L1_gnn_in['b1'], 'L1_gnn_g1': _L1_gnn_in['g1'], 'L1_gnn_bt1': _L1_gnn_in['bt1'], 'L1_gnn_W2': _L1_gnn_in['W2'], 'L1_gnn_b2': _L1_gnn_in['b2'], 'L1_gnn_g2': _L1_gnn_in['g2'], 'L1_gnn_bt2': _L1_gnn_in['bt2'], 'L2_gnn_We1': _L2_gnn_in['We1'], 'L2_gnn_be1': _L2_gnn_in['be1'], 'L2_gnn_We2': _L2_gnn_in['We2'], 'L2_gnn_be2': _L2_gnn_in['be2'], 'L2_gnn_g_msg': _L2_gnn_in['g_msg'], 'L2_gnn_b_msg': _L2_gnn_in['b_msg'], 'L2_gnn_Wn1': _L2_gnn_in['Wn1'], 'L2_gnn_bn1': _L2_gnn_in['bn1'], 'L2_gnn_Wn2': _L2_gnn_in['Wn2'], 'L2_gnn_bn2': _L2_gnn_in['bn2'], 'L2_gnn_g_node': _L2_gnn_in['g_node'], 'L2_gnn_b_node': _L2_gnn_in['b_node'], 'L3_gnn_mlp_w1': _L3_gnn_in['mlp_w1'], 'L3_gnn_mlp_b1': _L3_gnn_in['mlp_b1'], 'L3_gnn_mlp_w2': _L3_gnn_in['mlp_w2'], 'L3_gnn_mlp_b2': _L3_gnn_in['mlp_b2'], 'L3_gnn_lin1_w': _L3_gnn_in['lin1_w'], 'L3_gnn_lin2_w': _L3_gnn_in['lin2_w'], 'L3_gnn_lin2_b': _L3_gnn_in['lin2_b']}

def reference(x, src, dst, edge_attr_32, edge_attr_50, edge_weight, node_vec1, L0_gnn_W1, L0_gnn_W2, L0_gnn_w_ih, L0_gnn_w_hh, L0_gnn_b_ih, L0_gnn_b_hh, L1_gnn_W1, L1_gnn_b1, L1_gnn_g1, L1_gnn_bt1, L1_gnn_W2, L1_gnn_b2, L1_gnn_g2, L1_gnn_bt2, L2_gnn_We1, L2_gnn_be1, L2_gnn_We2, L2_gnn_be2, L2_gnn_g_msg, L2_gnn_b_msg, L2_gnn_Wn1, L2_gnn_bn1, L2_gnn_Wn2, L2_gnn_bn2, L2_gnn_g_node, L2_gnn_b_node, L3_gnn_mlp_w1, L3_gnn_mlp_b1, L3_gnn_mlp_w2, L3_gnn_mlp_b2, L3_gnn_lin1_w, L3_gnn_lin2_w, L3_gnn_lin2_b):
    import jax
    import jax.numpy as jnp

    def _L0_gnn_ref(feat, w, src, dst, W1, W2, w_ih, w_hh, b_ih, b_hh):
        import jax, jax.numpy as jnp
        import numpy as np
        N = 12500
        E = 80000
        D = 128

        def _weighted_mean_agg(ft, w, src, dst, n_nodes):
            m = ft[src] * w[:, None]
            msum = jax.ops.segment_sum(m, dst, num_segments=n_nodes)
            wsum = jax.ops.segment_sum(w, dst, num_segments=n_nodes)
            safe = jnp.where(wsum > 0, wsum, 1.0)
            return jnp.where((wsum > 0)[:, None], msum / safe[:, None], 0.0)
        n = feat.shape[0]
        neigh1 = _weighted_mean_agg(feat, w, src, dst, n)
        neigh2 = _weighted_mean_agg(feat, w, dst, src, n)
        hn = jnp.concatenate([neigh1 @ W1.T, neigh2 @ W2.T], axis=1)
        gi = hn @ w_ih.T + b_ih
        gh = feat @ w_hh.T + b_hh
        i_r, i_z, i_n = jnp.split(gi, 3, axis=1)
        h_r, h_z, h_n = jnp.split(gh, 3, axis=1)
        r = jax.nn.sigmoid(i_r + h_r)
        z = jax.nn.sigmoid(i_z + h_z)
        nn_ = jnp.tanh(i_n + r * h_n)
        return nn_ + z * (feat - nn_)

    def _L1_gnn_ref(x, edge_index, W1, b1, g1, bt1, W2, b2, g2, bt2):
        import jax, jax.numpy as jnp
        import numpy as np
        N = 12500
        E = 200000
        D_IN = 128
        D_HID = 128
        D_OUT = 128
        EPS = 1e-05

        def _gcn_conv(x, W, b, src, dst, edge_norm, num_nodes):
            h = x @ W
            msg = h[src] * edge_norm[:, None]
            agg = jax.ops.segment_sum(msg, dst, num_segments=num_nodes)
            return agg + b

        def _batch_norm(x, gamma, beta):
            m = jnp.mean(x, axis=0)
            v = jnp.mean(jnp.square(x - m), axis=0)
            return (x - m) * jax.lax.rsqrt(v + EPS) * gamma + beta
        num_nodes = x.shape[0]
        loops = jnp.arange(num_nodes, dtype=edge_index.dtype)
        src = jnp.concatenate([edge_index[0], loops])
        dst = jnp.concatenate([edge_index[1], loops])
        deg = jax.ops.segment_sum(jnp.ones_like(dst, dtype=x.dtype), dst, num_segments=num_nodes)
        inv_sqrt_deg = jax.lax.rsqrt(deg)
        edge_norm = inv_sqrt_deg[src] * inv_sqrt_deg[dst]
        h = _gcn_conv(x, W1, b1, src, dst, edge_norm, num_nodes)
        h = _batch_norm(h, g1, bt1)
        h = jax.nn.relu(h)
        h = _gcn_conv(h, W2, b2, src, dst, edge_norm, num_nodes)
        h = _batch_norm(h, g2, bt2)
        return h

    def _L2_gnn_ref(node_inp, edge_feat, node_mask, We1, be1, We2, be2, g_msg, b_msg, Wn1, bn1, Wn2, bn2, g_node, b_node, senders, receivers):
        import jax, jax.numpy as jnp
        import numpy as np
        N = 6250
        DEG = 16
        E = N * DEG
        DIM = 128
        EDGE_DIM = 32
        EPS = 1e-05

        def _ln(x, scale, offset, mask):
            m = jnp.mean(x, axis=-1, keepdims=True)
            v = jnp.mean(jnp.square(x - m), axis=-1, keepdims=True)
            return ((x - m) * jax.lax.rsqrt(v + EPS) * scale + offset) * mask
        msg_input = jnp.concatenate([node_inp[senders], node_inp[receivers], edge_feat], axis=-1)
        h = jax.nn.swish(msg_input @ We1 + be1)
        messages = h @ We2 + be2
        agg = jax.ops.segment_sum(messages, receivers, num_segments=node_inp.shape[0], indices_are_sorted=True) / DEG
        agg = _ln(agg, g_msg, b_msg, node_mask)
        nf = jnp.concatenate([node_inp, agg], axis=-1)
        nf = jax.nn.swish(nf @ Wn1 + bn1) @ Wn2 + bn2
        nf = node_inp + nf
        return _ln(nf, g_node, b_node, node_mask)

    def _L3_gnn_ref(x, edge_index, edge_weight, edge_attr, mlp_w1, mlp_b1, mlp_w2, mlp_b2, lin1_w, lin2_w, lin2_b):
        import jax, jax.numpy as jnp
        import numpy as np
        PI = float(np.pi)
        CUTOFF = 10.0
        LOG2 = float(np.log(2.0))

        def ssp(x):
            return jax.nn.softplus(x) - LOG2
        N = x.shape[0]
        src, dst = (edge_index[0], edge_index[1])
        C = 0.5 * (jnp.cos(edge_weight * (PI / CUTOFF)) + 1.0)
        h = ssp(edge_attr @ mlp_w1.T + mlp_b1)
        W = (h @ mlp_w2.T + mlp_b2) * C[:, None]
        xh = x @ lin1_w.T
        msg = xh[src] * W
        agg = jax.ops.segment_sum(msg, dst, num_segments=N)
        out = ssp(agg @ lin2_w.T + lin2_b)
        return out
    edge_index = jnp.stack([src, dst])
    h = jnp.maximum(_layernorm(x, axis=-1), 0.0)
    x = x + _L0_gnn_ref(h, edge_weight, src, dst, L0_gnn_W1, L0_gnn_W2, L0_gnn_w_ih, L0_gnn_w_hh, L0_gnn_b_ih, L0_gnn_b_hh)
    h = jnp.maximum(_layernorm(x, axis=-1), 0.0)
    x = x + _L1_gnn_ref(h, edge_index, L1_gnn_W1, L1_gnn_b1, L1_gnn_g1, L1_gnn_bt1, L1_gnn_W2, L1_gnn_b2, L1_gnn_g2, L1_gnn_bt2)
    h = jnp.maximum(_layernorm(x, axis=-1), 0.0)
    x = x + _L2_gnn_ref(h, edge_attr_32, node_vec1, L2_gnn_We1, L2_gnn_be1, L2_gnn_We2, L2_gnn_be2, L2_gnn_g_msg, L2_gnn_b_msg, L2_gnn_Wn1, L2_gnn_bn1, L2_gnn_Wn2, L2_gnn_bn2, L2_gnn_g_node, L2_gnn_b_node, src, dst)
    h = jnp.maximum(_layernorm(x, axis=-1), 0.0)
    x = x + _L3_gnn_ref(h, edge_index, edge_weight, edge_attr_50, L3_gnn_mlp_w1, L3_gnn_mlp_b1, L3_gnn_mlp_w2, L3_gnn_mlp_b2, L3_gnn_lin1_w, L3_gnn_lin2_w, L3_gnn_lin2_b)
    return x

_drawn_inputs = setup_inputs


def setup_inputs(seed=0):
    import zlib

    import numpy as np

    out = dict(_drawn_inputs(seed))
    spreads = {'L1_gnn_b1': (0.0, 2.0),
     'L1_gnn_g1': (1.0, 0.2),
     'L1_gnn_bt1': (0.0, 0.1),
     'L1_gnn_b2': (0.0, 2.0),
     'L1_gnn_g2': (1.0, 0.2),
     'L1_gnn_bt2': (0.0, 0.1),
     'L2_gnn_be1': (0.0, 0.397),
     'L2_gnn_be2': (0.0, 0.374),
     'L2_gnn_g_msg': (1.0, 0.58),
     'L2_gnn_b_msg': (0.0, 0.784),
     'L2_gnn_bn1': (0.0, 0.393),
     'L2_gnn_bn2': (0.0, 0.1),
     'L2_gnn_g_node': (1.0, 0.2),
     'L2_gnn_b_node': (0.0, 0.303),
     'L3_gnn_mlp_b1': (0.0, 0.1),
     'L3_gnn_mlp_b2': (0.0, 0.1),
     'L3_gnn_lin2_b': (0.0, 0.352)}
    factors = {'edge_attr_32': 5.334, 'edge_weight': 4.508, 'L0_gnn_b_hh': 4.239}
    for name, (base, spread) in spreads.items():
        noise = np.random.default_rng([zlib.crc32(name.encode()), seed]).standard_normal(out[name].shape)
        drawn = base * np.exp(spread * noise) if base else spread * noise
        out[name] = jnp.asarray(drawn.astype(out[name].dtype))
    for name, factor in factors.items():
        out[name] = (out[name] * factor).astype(out[name].dtype)
    return out
```

```python
from contextlib import ExitStack

import numpy as np
import concourse.bass as bass
from concourse import mybir

F32 = mybir.dt.float32
I32 = mybir.dt.int32
ALU = mybir.AluOpType
ACT = mybir.ActivationFunctionType
AX_X = mybir.AxisListType.X

P = 128
N = 6250
D = 128
E = 200000
ET = -(-E // P)
BUCKETS = -(-N // P)
CH = 512
CT = CH // P
NCH = -(-N // CH)
NT = NCH * CT
NP = NT * P
PAD_NODE = BUCKETS * P - 1
U = 8
H = 4
NI = -(-(ET + BUCKETS - 1) // U)
PAIRS = NI * U
PG = -(-PAIRS // P)
SUMS = 4
EPS = 1e-5
DE2 = 32
DE3 = 50
PI = float(np.pi)
CUTOFF = 10.0
LOG2 = float(np.log(2.0))


class Steps:

    def __init__(self, sem, names):
        self.sem, self.names = sem, names.split()

    def start(self, eng):
        eng.sem_inc(self.sem, len(self.names))

    def now(self, name, c):
        return self.sem, (c + 1) * len(self.names) + self.names.index(name) + 1

    def before(self, name, c):
        return self.sem, c * len(self.names) + self.names.index(name) + 1


def build(nc, a, out_x):
    es = ExitStack()

    def sb(name, shape, dt=F32, ctx=None):
        return (ctx or es).enter_context(nc.sbuf_tensor(name, shape, dt))

    def ps(name, ctx, shape=(P, 512)):
        return ctx.enter_context(nc.psum_tensor(name, list(shape), F32))

    stage_sems = []

    def sem(name):
        stage_sems.append(nc.alloc_semaphore(name))
        return stage_sems[-1]

    def stage_done():
        nc.clear_and_free_semaphores(stage_sems)
        stage_sems.clear()
        nc.all_engine_barrier()

    def dram(name, shape, dt=F32):
        return nc.dram_tensor(name, shape, dt, kind="Internal").ap()

    def tiles(ap):
        return ap.rearrange("(t p) w -> p t w", p=P)

    table = dram("table", (NP, D))
    table2 = dram("table2", (NP, 2 * D))
    srcsum = [dram(f"srcsum{q}", (NP + P, D + 1)) for q in range(SUMS)]
    row_scratch = dram("row_scratch", (2, PG * P), I32)

    with es:
        x = sb("x", [P, NT, D])
        h = sb("h", [P, NT, D + 1])
        ident = sb("ident", [P, P])
        iota = sb("iota", [P, P])
        earlier = sb("earlier", [P, P])
        trash_row = sb("trash_row", [P, 1])
        edge_tab = sb("edge_tab", [P, PG * P, 3])
        tile_row = sb("tile_row", [1, PG * P], I32)
        bucket_row = sb("bucket_row", [1, PG * P // H], I32)
        deg = sb("deg", [P, NT, 2])
        stat = sb("stat", [P, NT, 6])
        mv = sb("mv", [P, NT, 2])
        rstd = sb("rstd", [P, NT])
        nmr = sb("nmr", [P, NT])
        eps = sb("eps", [P, 1])

        def stage_tables():
            with ExitStack() as ctx:
                lo_i = sb("lo_i", [P, 2, ET], I32, ctx)
                lo = sb("lo", [P, ET], F32, ctx)
                hi = sb("hi", [P, ET], F32, ctx)
                extra = sb("extra", [P, ET], F32, ctx)
                one = sb("one", [P, ET], F32, ctx)
                incl = sb("incl", [P, ET], F32, ctx)
                first = sb("first", [P, ET], F32, ctx)
                off = sb("off", [P, ET], F32, ctx)
                doff = sb("doff", [P, ET], F32, ctx)
                tno = sb("tno", [P, ET], F32, ctx)
                mask = sb("mask", [P, ET], F32, ctx)
                prod = sb("prod", [P, ET], F32, ctx)
                pair_no = sb("pair_no", [P, PG], F32, ctx)
                cnt = sb("cnt", [P, PG], F32, ctx)
                tix = sb("tix", [P, PG], F32, ctx)
                tix_i = sb("tix_i", [P, PG], I32, ctx)
                tfe_i = sb("tfe_i", [P, PG], I32, ctx)
                bno = sb("bno", [P, PG], F32, ctx)
                bst = sb("bst", [P, PG], F32, ctx)
                bcl_i = sb("bcl_i", [P, PG], I32, ctx)
                buckets = sb("buckets", [1, PG * P], I32, ctx)
                rows = [sb(f"rows{k}", [P, PG, P], dt, ctx) for k, dt in enumerate((I32, I32, F32))]
                rowf = sb("rowf", [P, 2, PG, P], F32, ctx)
                pt = [ps(f"pt{k}", ctx) for k in range(2)]
                loaded, x_loaded = sem("loaded"), sem("x_loaded")
                consts, vec = sem("consts"), sem("vec")
                pairs_known, rows_in, rows_ready = sem("pairs_known"), sem("rows_in"), sem("rows_ready")
                turned, taken, rows_out, rows_back = sem("turned"), sem("taken"), sem("rows_out"), sem("rows_back")

                with nc.Block() as block:
                    @block.sync
                    def _(sp):
                        sp.dma_start(lo_i[:, :, :], a["tile_ends"].rearrange("(o k) t -> o k t", o=1).to_broadcast([P, 2, ET])).then_inc(loaded, 16)
                        sp.dma_start(x[:, :, :], a["x"]).then_inc(x_loaded, 16)
                        sp.wait_ge(pairs_known, 1)
                        with nc.allow_non_contiguous_dma(reason="two columns of 13 values a partition"):
                            sp.dma_start(row_scratch[0].rearrange("(g p) -> p g", p=P), tfe_i[:, :]).then_inc(rows_out, 16)
                            sp.dma_start(row_scratch[1].rearrange("(g p) -> p g", p=P), bcl_i[:, :]).then_inc(rows_out, 16)
                        sp.wait_ge(rows_out, 32)
                        sp.dma_start(tile_row[:, :], row_scratch[0:1, :]).then_inc(rows_back, 16)
                        sp.dma_start(buckets[:, :], row_scratch[1:2, :]).then_inc(rows_back, 16)
                        sp.wait_ge(rows_back, 32)
                        sp.wait_ge(x_loaded, 16)

                    @block.gpsimd
                    def _(g):
                        g.memset(ident[:, :], 0.0).then_inc(consts, 1)
                        g.memset(earlier[:, :], 1.0).then_inc(consts, 1)
                        g.iota(iota[:, :], [[1, P]], 0, 0, allow_small_or_imprecise_dtypes=True).then_inc(consts, 1)
                        g.iota(pair_no[:, :], [[P, PG]], 0, 1, allow_small_or_imprecise_dtypes=True).then_inc(consts, 1)
                        g.iota(tno[:, :], [[1, ET]], 0, 0, allow_small_or_imprecise_dtypes=True).then_inc(consts, 1)
                        g.iota(trash_row[:, :], [[0, 1]], NP, 1, allow_small_or_imprecise_dtypes=True).then_inc(consts, 1)
                        g.wait_ge(consts, 6)
                        g.affine_select(out=ident[:, :], in_=ident[:, :], compare_op=ALU.not_equal, fill=1.0, base=0,
                                        pattern=[[-1, P]], channel_multiplier=1).then_inc(consts, 1)
                        g.affine_select(out=earlier[:, :], in_=earlier[:, :], compare_op=ALU.is_gt, fill=0.0, base=0,
                                        pattern=[[-1, P]], channel_multiplier=1).then_inc(consts, 1)
                        g.wait_ge(pairs_known, 1)
                        for k, name in enumerate(("src", "dst", "edge_weight")):
                            for gr in range(PG):
                                g.indirect_dma_start(rows[k][:, gr, :], None, a[name],
                                                     bass.IndirectOffsetOnAxis(ap=tix_i[:, gr:gr + 1], axis=0)).then_inc(rows_in, 16)
                        g.wait_ge(rows_in, 16 * 3 * PG)

                    @block.vector
                    def _(v):
                        n = [0]

                        def then(ins):
                            n[0] += 1
                            ins.then_inc(vec, 1)
                            v.wait_ge(vec, n[0])

                        v.memset(one[:, :], 1.0)
                        v.memset(eps[:, :], EPS)
                        v.memset(deg[:, :, :], 0.0)
                        v.memset(h[:, :, D:D + 1], 1.0)
                        v.wait_ge(loaded, 16)
                        then(v.tensor_scalar(lo_i[:, :, :], lo_i[:, :, :], 7, None, ALU.arith_shift_right))
                        v.tensor_copy(lo[:, :], lo_i[:, 0, :])
                        then(v.tensor_copy(hi[:, :], lo_i[:, 1, :]))
                        then(v.tensor_tensor(extra[:, :], hi[:, :], lo[:, :], ALU.subtract))
                        then(v.tensor_tensor_scan(incl[:, :], one[:, :], extra[:, :], 0.0, ALU.mult, ALU.add))
                        then(v.tensor_tensor(first[:, :], incl[:, :], extra[:, :], ALU.subtract))
                        v.wait_ge(consts, 8)
                        then(v.tensor_tensor(first[:, :], first[:, :], tno[:, :], ALU.add))
                        then(v.tensor_tensor(off[:, :], lo[:, :], first[:, :], ALU.subtract))
                        v.tensor_copy(doff[:, 0:1], off[:, 0:1])
                        then(v.tensor_tensor(doff[:, 1:ET], off[:, 1:ET], off[:, 0:ET - 1], ALU.subtract))
                        for gr in range(PG):
                            then(v.tensor_scalar(mask[:, :], first[:, :], pair_no[:, gr:gr + 1], None, ALU.is_le, ALU.add,
                                                 accum_out=cnt[:, gr:gr + 1]))
                            then(v.tensor_tensor_reduce(prod[:, :], mask[:, :], doff[:, :], 1.0, 0.0, ALU.mult, ALU.add,
                                                        bno[:, gr:gr + 1]))
                        v.tensor_scalar(tix_i[:, :], cnt[:, :], -1.0, None, ALU.add)
                        then(v.tensor_scalar(tix[:, :], cnt[:, :], -1.0, None, ALU.add))
                        v.tensor_scalar(tfe_i[:, :], tix[:, :], float(P), None, ALU.mult)
                        then(v.tensor_tensor(bno[:, :], bno[:, :], pair_no[:, :], ALU.add))
                        v.tensor_scalar(bst[:, :], bno[:, :], float(P), None, ALU.mult)
                        v.tensor_scalar(bcl_i[:, :], bno[:, :], float(BUCKETS - 1), None, ALU.min).then_inc(pairs_known, 1)
                        v.wait_ge(rows_in, 16 * 3 * PG)
                        v.tensor_copy(rowf[:, 0, :, :], rows[0][:, :, :])
                        for gr in range(PG):
                            last = v.tensor_scalar(rowf[:, 1, gr, :], rows[1][:, gr, :], bst[:, gr:gr + 1], None, ALU.subtract)
                        last.then_inc(rows_ready, 1)
                        v.wait_ge(rows_back, 32)
                        four = buckets[:, :].rearrange("o (n q) -> o q n", q=H)
                        for q in range(1, H):
                            last = v.tensor_scalar(four[:, q, :], four[:, q, :], 8 * q, None, ALU.logical_shift_left)
                        then(last)
                        then(v.tensor_tensor(bucket_row[:, :], four[:, 0, :], four[:, 1, :], ALU.bitwise_or))
                        then(v.tensor_tensor(bucket_row[:, :], bucket_row[:, :], four[:, 2, :], ALU.bitwise_or))
                        v.tensor_tensor(bucket_row[:, :], bucket_row[:, :], four[:, 3, :], ALU.bitwise_or)

                    @block.tensor
                    def _(pe):
                        pe.wait_ge(consts, 8)
                        pe.wait_ge(rows_ready, 1)
                        for gr in range(PG):
                            if gr >= 2:
                                pe.wait_ge(taken, gr - 1)
                            for k, r in enumerate((rowf[:, 0, gr, :], rowf[:, 1, gr, :], rows[2][:, gr, :])):
                                last = pe.transpose(pt[gr % 2][:, k * P:(k + 1) * P], r, ident[:, :])
                            last.then_inc(turned, 1)

                    @block.scalar
                    def _(s):
                        for gr in range(PG):
                            s.wait_ge(turned, gr + 1)
                            last = s.copy(edge_tab[:, gr * P:(gr + 1) * P, :].rearrange("p t k -> p k t"),
                                          pt[gr % 2][:, 0:3 * P].rearrange("p (k t) -> p k t", k=3))
                            last.then_inc(taken, 1)

        def buckets_of(eng, n):
            word = eng.value_load(bucket_row[0:1, bass.ds(n, 1)], min_val=0, max_val=(1 << 30) - 1)
            return [nc.s_assert_within(eng.snap((word >> (8 * q)) & 127), 0, BUCKETS - 1,
                                       skip_runtime_bounds_check_because="buckets are held to this range when the words are made") for q in range(H)]

        def stage_norm(name, to_table):
            stats_in, merged, std_in, scaled, normed, stored = (
                sem(f"{name}_{k}") for k in ("stats", "merged", "std", "scaled", "normed", "stored"))
            with nc.Block() as block:
                @block.vector
                def _(v):
                    with v.Fori(0, NCH) as c:
                        for k in range(CT):
                            v.bn_stats(stat[:, bass.ds(c * CT + k, 1), :].rearrange("p t s -> p (t s)"),
                                       x[:, bass.ds(c * CT + k, 1), :].rearrange("p t d -> p (t d)")).then_inc(stats_in, 1)
                    v.wait_ge(stats_in, NT)
                    v.tensor_tensor(mv[:, :, 0], stat[:, :, 1], stat[:, :, 4], ALU.add).then_inc(merged, 1)
                    v.tensor_tensor(nmr[:, :], stat[:, :, 1], stat[:, :, 4], ALU.subtract).then_inc(merged, 1)
                    v.tensor_tensor(mv[:, :, 1], stat[:, :, 2], stat[:, :, 5], ALU.add).then_inc(merged, 1)
                    v.wait_ge(merged, 3)
                    v.tensor_scalar(mv[:, :, 1], mv[:, :, 1], 1.0 / D, None, ALU.mult).then_inc(merged, 1)
                    v.tensor_tensor(nmr[:, :], nmr[:, :], nmr[:, :], ALU.mult).then_inc(merged, 1)
                    v.wait_ge(merged, 5)
                    v.tensor_scalar(mv[:, :, 0], mv[:, :, 0], 0.5, None, ALU.mult).then_inc(merged, 1)
                    v.scalar_tensor_tensor(out=mv[:, :, 1], in0=nmr[:, :], scalar=0.25, in1=mv[:, :, 1],
                                           op0=ALU.mult, op1=ALU.add).then_inc(merged, 1)
                    v.wait_ge(std_in, 1)
                    v.reciprocal(rstd[:, :], rstd[:, :]).then_inc(scaled, 1)
                    v.wait_ge(scaled, 1)
                    v.scalar_tensor_tensor(out=nmr[:, :], in0=mv[:, :, 0], scalar=-1.0, in1=rstd[:, :],
                                           op0=ALU.mult, op1=ALU.mult).then_inc(scaled, 1)

                @block.scalar
                def _(s):
                    s.wait_ge(merged, 7)
                    s.activation(rstd[:, :], mv[:, :, 1], ACT.Sqrt, bias=eps[:, :]).then_inc(std_in, 1)
                    s.wait_ge(scaled, 2)
                    with s.Fori(0, NCH) as c:
                        for k in range(CT):
                            t = c * CT + k
                            s.activation(h[:, bass.ds(t, 1), 0:D], x[:, bass.ds(t, 1), :], ACT.Relu,
                                         bias=nmr[:, bass.ds(t, 1)], scale=rstd[:, bass.ds(t, 1)]).then_inc(normed, 1)

                @block.sync
                def _(sp):
                    if to_table:
                        sp.wait_ge(normed, NT)
                        sp.dma_start(tiles(table), h[:, :, 0:D]).then_inc(stored, 16)
                        sp.wait_ge(stored, 16)

        def stage_gru_edges(sum_dst):
            with ExitStack() as ctx:
                cur = sb("g_cur", [P, 2, H, 4], F32, ctx)
                gidx = sb("g_gidx", [P, 2, H], I32, ctx)
                sidx = sb("g_sidx", [P, 2, H], I32, ctx)
                dup = sb("g_dup", [P, H], F32, ctx)
                away = sb("g_away", [P, H], F32, ctx)
                G = sb("g_G", [P, U, D], F32, ctx)
                oh = sb("g_oh", [P, 2, H, P], F32, ctx)
                ohw = sb("g_ohw", [P, 2, H, P], F32, ctx)
                same = sb("g_same", [P, 2, H, P], F32, ctx)
                junk = sb("g_junk", [P, H, P], F32, ctx)
                mix = sb("g_mix", [P, 2, H, P], F32, ctx)
                rows = sb("g_rows", [P, H, D + 1], F32, ctx)
                zero = sb("g_zero", [P, (NP + P) * (D + 1) // P], F32, ctx)
                ps_src = ps("g_ps_src", ctx)
                ps_sum = [ps(f"g_ps_sum{k}", ctx) for k in range(2)]
                ps_deg = [ps(f"g_ps_deg{k}", ctx) for k in range(2)]
                ps_mix = ps("g_ps_mix", ctx)
                ps_rows = [ps(f"g_ps_rows{k}", ctx) for k in range(2)]
                zeroed, cur_ready, gidx_ready = sem("g_zeroed"), sem("g_cur_ready"), sem("g_gidx_ready")
                oh_ready, ohw_ready = sem("g_oh_ready"), sem("g_ohw_ready")
                srcrow_ready, same_ready = sem("g_srcrow_ready"), sem("g_same_ready")
                mix_made, mix_ready = sem("g_mix_made"), sem("g_mix_ready")
                dup_step, sidx_ready = sem("g_dup_step"), sem("g_sidx_ready")
                rows_made, row_ready = sem("g_rows_made"), sem("g_row_ready")
                gathered = [sem(f"g_gathered{s}") for s in range(U)]
                src_added = [sem(f"g_src_added{q}") for q in range(SUMS)]
                summed, dst_added, deg_added = sem("g_summed"), sem("g_dst_added"), sem("g_deg_added")

                with nc.Block() as block:
                    @block.gpsimd
                    def _(g):
                        g.memset(zero[:, :], 0.0).then_inc(zeroed, 1)
                        g.wait_ge(zeroed, 1)
                        for q in range(SUMS):
                            g.dma_start(srcsum[q].rearrange("(p r) c -> p (r c)", p=P), zero[:, :]).then_inc(src_added[q], 16)

                        def half(i, b):
                            g.wait_ge(gidx_ready, 2 * i + b + 1)
                            g.nop(nofuse=True)
                            for q in range(H):
                                s = H * b + q
                                g.indirect_dma_start(G[:, s, :], None, table,
                                                     bass.IndirectOffsetOnAxis(ap=gidx[:, b, q:q + 1], axis=0)).then_inc(gathered[s], 16)
                                g.wait_ge(row_ready, H * (2 * i + b) + q + 1 + H)
                                g.wait_ge(sidx_ready, 2 * i + b + 1)
                                g.nop(nofuse=True)
                                g.indirect_dma_start(srcsum[q], bass.IndirectOffsetOnAxis(ap=sidx[:, b, q:q + 1], axis=0),
                                                     rows[:, q, :], None, compute_op=ALU.add).then_inc(src_added[q], 16)

                        with g.Fori(0, NI) as i:
                            half(i, 0)
                            half(i, 1)
                        for q in range(SUMS):
                            g.wait_ge(src_added[q], 16 * (2 * NI + 1))

                    @block.vector
                    def _(v):
                        v.memset(sum_dst[:, :, :], 0.0).then_inc(dst_added, 2 * H)
                        v.memset(cur[:, :, :, 3:4], 1.0).then_inc(deg_added, 2 * H)
                        v.wait_ge(dst_added, 2 * H)
                        v.wait_ge(deg_added, 2 * H)

                        def front(i, b):
                            n = 2 * i + b
                            v.wait_ge(summed, n + 1)
                            v.tensor_copy(cur[:, b, :, 0:3], edge_tab[:, bass.ds(i * U + H * b, H), :]).then_inc(cur_ready, 1)
                            v.wait_ge(cur_ready, n + 1)
                            v.tensor_copy(gidx[:, b, :], cur[:, b, :, 0]).then_inc(gidx_ready, 1)
                            for q in range(H):
                                last = v.tensor_scalar(oh[:, b, q, :], iota[:, :], cur[:, b, q, 1:2], None, ALU.is_equal)
                            last.then_inc(oh_ready, 1)
                            v.wait_ge(srcrow_ready, n + 1)
                            for q in range(H):
                                last = v.tensor_scalar(same[:, b, q, :], ps_src[:, q * P:(q + 1) * P], cur[:, b, q, 0:1], None,
                                                       ALU.is_equal)
                            last.then_inc(same_ready, 1)
                            v.tensor_scalar(away[:, :], cur[:, b, :, 0], -1.0, trash_row[:, :], ALU.mult, ALU.add).then_inc(dup_step, 1)
                            v.wait_ge(same_ready, n + 1)
                            for q in range(H):
                                last = v.tensor_tensor_reduce(junk[:, q, :], same[:, b, q, :], earlier[:, :], 1.0, 0.0,
                                                              ALU.mult, ALU.add, dup[:, q:q + 1])
                            last.then_inc(dup_step, 1)
                            v.wait_ge(dup_step, 3 * n + 2)
                            v.scalar_tensor_tensor(out=away[:, :], in0=dup[:, :], scalar=0.5, in1=away[:, :],
                                                   op0=ALU.is_gt, op1=ALU.mult).then_inc(dup_step, 1)
                            v.wait_ge(dup_step, 3 * n + 3)
                            v.wait_ge(row_ready, H * n + H)
                            v.tensor_tensor(sidx[:, b, :], away[:, :], cur[:, b, :, 0], ALU.add).then_inc(sidx_ready, 1)

                        def back(i, b):
                            n = 2 * i + b
                            bucket = buckets_of(v, n)
                            v.wait_ge(summed, n + 3)
                            for q in range(H):
                                at = bass.ds(bucket[q], 1)
                                v.wait_ge(dst_added, H * n + q + 2 * H)
                                v.tensor_tensor(sum_dst[:, at, :], sum_dst[:, at, :],
                                                ps_sum[b][:, q * P:(q + 1) * P].rearrange("p (o d) -> p o d", o=1),
                                                ALU.add).then_inc(dst_added, 1)
                                v.wait_ge(deg_added, H * n + q + 2 * H)
                                v.tensor_tensor(deg[:, at, :], deg[:, at, :],
                                                ps_deg[b][:, 2 * q:2 * q + 2].rearrange("p (o d) -> p o d", o=1),
                                                ALU.add).then_inc(deg_added, 1)

                        front(0, 0)
                        with v.Fori(0, NI - 1) as i:
                            front(i, 1)
                            back(i, 0)
                            front(i + 1, 0)
                            back(i, 1)
                        front(NI - 1, 1)
                        back(NI - 1, 0)
                        back(NI - 1, 1)

                    @block.scalar
                    def _(s):
                        s.sem_inc(row_ready, H)

                        def half(i, b):
                            n = 2 * i + b
                            s.wait_ge(summed, n + 1)
                            s.wait_ge(oh_ready, n + 1)
                            for q in range(H):
                                last = s.activation(ohw[:, b, q, :], oh[:, b, q, :], ACT.Copy, scale=cur[:, b, q, 2:3])
                            last.then_inc(ohw_ready, 1)
                            s.wait_ge(mix_made, n + 1)
                            s.copy(mix[:, b, :, :].rearrange("p q d -> p (q d)"), ps_mix[:, :]).then_inc(mix_ready, 1)
                            for q in range(H):
                                s.wait_ge(rows_made, H * n + q // 2 * 2 + 2)
                                s.wait_ge(src_added[q], 16 * (n + 1))
                                s.copy(rows[:, q, :], ps_rows[q // 2][:, (q % 2) * 256:(q % 2) * 256 + D + 1]).then_inc(row_ready, 1)

                        with s.Fori(0, NI) as i:
                            half(i, 0)
                            half(i, 1)

                    @block.tensor
                    def _(pe):
                        pe.sem_inc(summed, 2)

                        def front(i, b):
                            n = 2 * i + b
                            pe.wait_ge(cur_ready, n + 1)
                            if not (isinstance(n, int) and n == 0):
                                pe.wait_ge(same_ready, n)
                            for q in range(H):
                                last = pe.transpose(ps_src[:, q * P:(q + 1) * P], cur[:, b, q, 0:1].to_broadcast([P, P]), ident[:, :])
                            last.then_inc(srcrow_ready, 1)

                        def middle(i, b):
                            n = 2 * i + b
                            if not (isinstance(n, int) and n == 0):
                                pe.wait_ge(mix_ready, n)
                            pe.wait_ge(ohw_ready, n + 1)
                            pe.wait_ge(same_ready, n + 1)
                            for q in range(H):
                                last = pe.matmul(ps_mix[:, q * P:(q + 1) * P], ohw[:, b, q, :], same[:, b, q, :], start=True, stop=True)
                            last.then_inc(mix_made, 1)
                            bucket = buckets_of(pe, n)
                            pe.wait_ge(mix_ready, n + 1)
                            for q in range(H):
                                pe.wait_ge(row_ready, H * n + q // 2 * 2 + 2)
                                pe.matmul(ps_rows[q // 2][:, (q % 2) * 256:(q % 2) * 256 + D + 1], mix[:, b, q, :],
                                          h[:, bass.ds(bucket[q], 1), :].rearrange("p o d -> p (o d)"), start=True, stop=True).then_inc(rows_made, 1)

                        def back(i, b):
                            n = 2 * i + b
                            pe.wait_ge(deg_added, H * n + H)
                            pe.wait_ge(dst_added, H * n + H)
                            for q in range(H):
                                s = H * b + q
                                pe.matmul(ps_deg[b][:, 2 * q:2 * q + 2], oh[:, b, q, :], cur[:, b, q, 2:4], start=True, stop=True)
                                pe.wait_ge(gathered[s], 16 * (i + 1))
                                last = pe.matmul(ps_sum[b][:, q * P:(q + 1) * P], ohw[:, b, q, :], G[:, s, :], start=True, stop=True)
                            last.then_inc(summed, 1)

                        front(0, 0)
                        middle(0, 0)
                        with pe.Fori(0, NI - 1) as i:
                            front(i, 1)
                            back(i, 0)
                            middle(i, 1)
                            front(i + 1, 0)
                            back(i, 1)
                            middle(i + 1, 0)
                        front(NI - 1, 1)
                        back(NI - 1, 0)
                        middle(NI - 1, 1)
                        back(NI - 1, 1)

        def chunk(c):
            return bass.ds(c * CT, CT)

        def spread(ap):
            return ap.unsqueeze(2).to_broadcast([P, CT, D])

        def across(ap):
            return ap.unsqueeze(1).to_broadcast([P, CT, D])

        def by_tile(ap):
            return ap.rearrange("p (t d) -> p t d", t=CT)

        def loader(sp, loaded, pairs):
            for dst, src in pairs:
                sp.dma_start(dst, src).then_inc(loaded, 16)

        def stage_gru_nodes(sum_dst):
            with ExitStack() as ctx:
                w12 = sb("u_w12", [P, 2, D], F32, ctx)
                wih = sb("u_wih", [P, 2, 3 * D], F32, ctx)
                whh = sb("u_whh", [P, 3 * D], F32, ctx)
                bias = sb("u_bias", [P, 2, 3], F32, ctx)
                brz = sb("u_brz", [P, 2], F32, ctx)
                wf = sb("u_wf", [P, 2, 3 * D], F32, ctx)
                inv1 = sb("u_inv1", [P, NT], F32, ctx)
                has1 = sb("u_has1", [P, NT], F32, ctx)
                inv2 = sb("u_inv2", [P, CT], F32, ctx)
                has2 = sb("u_has2", [P, CT], F32, ctx)
                parts = sb("u_parts", [P, SUMS, CT, D + 1], F32, ctx)
                tot = sb("u_tot", [P, 2, CT, D + 1], F32, ctx)
                nodes = sb("u_nodes", [P, 3, CT, D], F32, ctx)
                fm = sb("u_fm", [P, 3, CH], F32, ctx)
                rz = sb("u_rz", [P, 2, CH], F32, ctx)
                cand = sb("u_cand", [P, CH], F32, ctx)
                upd = sb("u_upd", [P, CH], F32, ctx)
                ps_turn = [ps(f"u_ps_turn{k}", ctx) for k in range(3)]
                ps_rz = [ps(f"u_ps_rz{k}", ctx) for k in range(2)]
                ps_in, ps_hn, ps_back = ps("u_ps_in", ctx), ps("u_ps_hn", ctx), ps("u_ps_back", ctx)
                loaded, folded, ready = sem("u_loaded"), sem("u_folded"), sem("u_ready")
                parts_in = sem("u_parts_in")
                T = Steps(sem("u_tensor_steps"), "turned gates turned_back")
                V = Steps(sem("u_vector_steps"), "sum01 sum23 total has less safe recip inv mean_dst mean_src h hn in diff gated out added")
                S = Steps(sem("u_scalar_steps"), "fm r z cand")

                with nc.Block() as block:
                    @block.sync
                    def _(sp):
                        loader(sp, loaded, [(w12[:, :, :], a["l0_w12"]), (wih[:, :, :], a["l0_wih"]), (whh[:, :], a["l0_whh"]),
                                            (bias[:, :, :], a["l0_bias"])])
                        with sp.Fori(0, NCH) as c:
                            sp.wait_ge(*V.before("sum23", c))
                            for q in range(SUMS):
                                sp.dma_start(parts[:, q, :, :], tiles(srcsum[q][0:NP])[:, chunk(c), :]).then_inc(parts_in, 16)

                    @block.tensor
                    def _(pe):
                        T.start(pe)
                        pe.wait_ge(loaded, 64)
                        for k in range(2):
                            last = pe.matmul(ps_rz[k][:, 0:3 * D], w12[:, k, :], wih[:, k, :], start=True, stop=True)
                        last.then_inc(folded, 1)
                        pe.wait_ge(ready, 2)
                        with pe.Fori(0, NCH) as c:
                            pe.wait_ge(*V.now("h", c))
                            pe.wait_ge(*S.before("fm", c))
                            for k in range(3):
                                for t in range(CT):
                                    last = pe.transpose(ps_turn[k][:, t * P:(t + 1) * P], nodes[:, k, t, :], ident[:, :])
                            last.then_inc(T.sem, 1)
                            pe.wait_ge(*S.now("fm", c))
                            pe.wait_ge(*V.before("in", c))
                            for g in range(2):
                                for k, w in enumerate((wf[:, 0, :], wf[:, 1, :], whh[:, :])):
                                    pe.matmul(ps_rz[g][:, :], w[:, g * D:(g + 1) * D], fm[:, k, :], start=k == 0, stop=k == 2)
                            for k in range(2):
                                pe.matmul(ps_in[:, :], wf[:, k, 2 * D:3 * D], fm[:, k, :], start=k == 0, stop=k == 1)
                            pe.matmul(ps_hn[:, :], whh[:, 2 * D:3 * D], fm[:, 2, :], start=True, stop=True).then_inc(T.sem, 1)
                            pe.wait_ge(*V.now("out", c))
                            for t in range(CT):
                                last = pe.transpose(ps_back[:, t * P:(t + 1) * P], upd[:, t * P:(t + 1) * P], ident[:, :])
                            last.then_inc(T.sem, 1)

                    @block.vector
                    def _(v):
                        V.start(v)
                        v.tensor_scalar(has1[:, :], deg[:, :, 0], 0.0, None, ALU.is_gt).then_inc(ready, 1)
                        v.wait_ge(loaded, 64)
                        v.tensor_tensor(brz[:, :], bias[:, 0, 0:2], bias[:, 1, 0:2], ALU.add)
                        v.wait_ge(folded, 1)
                        v.tensor_copy(wf[:, 0, :], ps_rz[0][:, 0:3 * D])
                        v.tensor_copy(wf[:, 1, :], ps_rz[1][:, 0:3 * D]).then_inc(ready, 1)
                        v.wait_ge(ready, 2)
                        v.scalar_tensor_tensor(out=inv1[:, :], in0=deg[:, :, 0], scalar=-1.0, in1=has1[:, :],
                                               op0=ALU.add, op1=ALU.mult).then_inc(ready, 1)
                        v.wait_ge(ready, 3)
                        v.tensor_scalar(inv1[:, :], inv1[:, :], 1.0, None, ALU.add).then_inc(ready, 1)
                        v.wait_ge(ready, 4)
                        v.reciprocal(inv1[:, :], inv1[:, :]).then_inc(ready, 1)
                        v.wait_ge(ready, 5)
                        v.tensor_tensor(inv1[:, :], inv1[:, :], has1[:, :], ALU.mult).then_inc(ready, 1)
                        v.wait_ge(ready, 6)
                        with v.Fori(0, NCH) as c:
                            v.wait_ge(parts_in, 16 * SUMS * (c + 1))
                            v.tensor_tensor(tot[:, 0, :, :], parts[:, 0, :, :], parts[:, 1, :, :], ALU.add).then_inc(V.sem, 1)
                            v.tensor_tensor(tot[:, 1, :, :], parts[:, 2, :, :], parts[:, 3, :, :], ALU.add).then_inc(V.sem, 1)
                            v.wait_ge(*V.now("sum23", c))
                            v.tensor_tensor(tot[:, 0, :, :], tot[:, 0, :, :], tot[:, 1, :, :], ALU.add).then_inc(V.sem, 1)
                            v.wait_ge(*V.now("total", c))
                            v.tensor_scalar(has2[:, :], tot[:, 0, :, D], 0.0, None, ALU.is_gt).then_inc(V.sem, 1)
                            v.wait_ge(*V.now("has", c))
                            v.scalar_tensor_tensor(out=inv2[:, :], in0=tot[:, 0, :, D], scalar=-1.0, in1=has2[:, :],
                                                   op0=ALU.add, op1=ALU.mult).then_inc(V.sem, 1)
                            v.wait_ge(*V.now("less", c))
                            v.tensor_scalar(inv2[:, :], inv2[:, :], 1.0, None, ALU.add).then_inc(V.sem, 1)
                            v.wait_ge(*V.now("safe", c))
                            v.reciprocal(inv2[:, :], inv2[:, :]).then_inc(V.sem, 1)
                            v.wait_ge(*V.now("recip", c))
                            v.tensor_tensor(inv2[:, :], inv2[:, :], has2[:, :], ALU.mult).then_inc(V.sem, 1)
                            v.wait_ge(*T.before("turned", c))
                            v.tensor_tensor(nodes[:, 0, :, :], sum_dst[:, chunk(c), :], spread(inv1[:, chunk(c)]), ALU.mult).then_inc(V.sem, 1)
                            v.wait_ge(*V.now("inv", c))
                            v.tensor_tensor(nodes[:, 1, :, :], tot[:, 0, :, 0:D], spread(inv2[:, :]), ALU.mult).then_inc(V.sem, 1)
                            v.tensor_copy(nodes[:, 2, :, :], h[:, chunk(c), 0:D]).then_inc(V.sem, 1)
                            v.wait_ge(*T.now("gates", c))
                            v.wait_ge(*S.now("r", c))
                            v.scalar_tensor_tensor(out=cand[:, :], in0=ps_hn[:, :], scalar=bias[:, 1, 2:3], in1=rz[:, 0, :],
                                                   op0=ALU.add, op1=ALU.mult).then_inc(V.sem, 1)
                            v.wait_ge(*V.now("hn", c))
                            v.tensor_tensor(cand[:, :], ps_in[:, :], cand[:, :], ALU.add).then_inc(V.sem, 1)
                            v.wait_ge(*S.now("cand", c))
                            v.wait_ge(*T.before("turned_back", c))
                            v.tensor_tensor(upd[:, :], fm[:, 2, :], cand[:, :], ALU.subtract).then_inc(V.sem, 1)
                            v.wait_ge(*V.now("diff", c))
                            v.tensor_tensor(upd[:, :], rz[:, 1, :], upd[:, :], ALU.mult).then_inc(V.sem, 1)
                            v.wait_ge(*V.now("gated", c))
                            v.tensor_tensor(upd[:, :], upd[:, :], cand[:, :], ALU.add).then_inc(V.sem, 1)
                            v.wait_ge(*T.now("turned_back", c))
                            v.tensor_tensor(x[:, chunk(c), :], x[:, chunk(c), :], by_tile(ps_back[:, :]), ALU.add).then_inc(V.sem, 1)

                    @block.scalar
                    def _(s):
                        S.start(s)
                        s.wait_ge(ready, 2)
                        with s.Fori(0, NCH) as c:
                            s.wait_ge(*T.now("turned", c))
                            s.wait_ge(*V.before("out", c))
                            for k in range(3):
                                last = s.copy(fm[:, k, :], ps_turn[k][:, :])
                            last.then_inc(S.sem, 1)
                            s.wait_ge(*T.now("gates", c))
                            for g in range(2):
                                s.activation(rz[:, g, :], ps_rz[g][:, :], ACT.Sigmoid, bias=brz[:, g:g + 1]).then_inc(S.sem, 1)
                            s.wait_ge(*V.now("in", c))
                            s.activation(cand[:, :], cand[:, :], ACT.Tanh, bias=bias[:, 0, 2:3]).then_inc(S.sem, 1)

        def stage_gcn_table(name, acc, w_name, dis, y=None, bn=None):
            with ExitStack() as ctx:
                w = sb(f"{name}_w", [P, D], F32, ctx)
                cur = sb(f"{name}_cur", [P, CT, D], F32, ctx)
                fm = sb(f"{name}_fm", [P, CH], F32, ctx)
                ps_turn, ps_out = ps(f"{name}_ps_turn", ctx), ps(f"{name}_ps_out", ctx)
                loaded, stored = sem(f"{name}_loaded"), sem(f"{name}_stored")
                T = Steps(sem(f"{name}_tensor_steps"), "turned product")
                V = Steps(sem(f"{name}_vector_steps"), "cur scaled")
                S = Steps(sem(f"{name}_scalar_steps"), "fm")
                with nc.Block() as block:
                    @block.sync
                    def _(sp):
                        sp.dma_start(w[:, :], a[w_name]).then_inc(loaded, 16)
                        with sp.Fori(0, NCH) as c:
                            sp.wait_ge(*V.now("scaled", c))
                            sp.dma_start(tiles(table)[:, chunk(c), :], acc[:, chunk(c), :]).then_inc(stored, 16)
                        sp.wait_ge(stored, 16 * NCH)

                    @block.tensor
                    def _(pe):
                        T.start(pe)
                        pe.wait_ge(loaded, 16)
                        with pe.Fori(0, NCH) as c:
                            pe.wait_ge(*V.now("cur", c))
                            pe.wait_ge(*S.before("fm", c))
                            for t in range(CT):
                                last = pe.transpose(ps_turn[:, t * P:(t + 1) * P], cur[:, t, :], ident[:, :])
                            last.then_inc(T.sem, 1)
                            pe.wait_ge(*S.now("fm", c))
                            pe.wait_ge(*V.before("scaled", c))
                            for t in range(CT):
                                last = pe.matmul(ps_out[:, t * P:(t + 1) * P], fm[:, t * P:(t + 1) * P], w[:, :], start=True, stop=True)
                            last.then_inc(T.sem, 1)

                    @block.vector
                    def _(v):
                        V.start(v)
                        with v.Fori(0, NCH) as c:
                            v.wait_ge(*T.before("turned", c))
                            v.tensor_copy(cur[:, :, :], h[:, chunk(c), 0:D]).then_inc(V.sem, 1)
                            v.wait_ge(*T.now("product", c))
                            v.tensor_tensor(acc[:, chunk(c), :], by_tile(ps_out[:, :]), spread(dis[:, chunk(c)]), ALU.mult).then_inc(V.sem, 1)

                    @block.scalar
                    def _(s):
                        S.start(s)
                        with s.Fori(0, NCH) as c:
                            s.wait_ge(*T.now("turned", c))
                            s.wait_ge(*T.before("product", c))
                            if y is None:
                                s.copy(fm[:, :], ps_turn[:, :]).then_inc(S.sem, 1)
                            else:
                                s.activation(fm[:, :], y[:, bass.ds(c * CH, CH)], ACT.Relu, scale=bn[:, 0:1], bias=bn[:, 1:2]).then_inc(S.sem, 1)

        def stage_sum_edges(name, acc):
            with ExitStack() as ctx:
                cur = sb(f"{name}_cur", [P, 2, H, 2], F32, ctx)
                gidx = sb(f"{name}_gidx", [P, 2, H], I32, ctx)
                G = sb(f"{name}_G", [P, U, D], F32, ctx)
                oh = sb(f"{name}_oh", [P, 2, H, P], F32, ctx)
                ps_sum = [ps(f"{name}_ps_sum{k}", ctx) for k in range(2)]
                cur_ready, gidx_ready, oh_ready = sem(f"{name}_cur_ready"), sem(f"{name}_gidx_ready"), sem(f"{name}_oh_ready")
                gathered = [sem(f"{name}_gathered{s}") for s in range(U)]
                summed, added = sem(f"{name}_summed"), sem(f"{name}_added")
                with nc.Block() as block:
                    @block.gpsimd
                    def _(g):
                        def half(i, b):
                            g.wait_ge(gidx_ready, 2 * i + b + 1)
                            g.nop(nofuse=True)
                            for q in range(H):
                                g.indirect_dma_start(G[:, H * b + q, :], None, table,
                                                     bass.IndirectOffsetOnAxis(ap=gidx[:, b, q:q + 1], axis=0)).then_inc(gathered[H * b + q], 16)

                        with g.Fori(0, NI) as i:
                            half(i, 0)
                            half(i, 1)

                    @block.vector
                    def _(v):
                        v.sem_inc(added, 2 * H)

                        def front(i, b):
                            n = 2 * i + b
                            v.wait_ge(summed, n + 1)
                            v.tensor_copy(cur[:, b, :, :], edge_tab[:, bass.ds(i * U + H * b, H), 0:2]).then_inc(cur_ready, 1)
                            v.wait_ge(cur_ready, n + 1)
                            v.tensor_copy(gidx[:, b, :], cur[:, b, :, 0]).then_inc(gidx_ready, 1)
                            for q in range(H):
                                last = v.tensor_scalar(oh[:, b, q, :], iota[:, :], cur[:, b, q, 1:2], None, ALU.is_equal)
                            last.then_inc(oh_ready, 1)

                        def back(i, b):
                            n = 2 * i + b
                            bucket = buckets_of(v, n)
                            v.wait_ge(summed, n + 3)
                            for q in range(H):
                                at = bass.ds(bucket[q], 1)
                                v.wait_ge(added, H * n + q + 2 * H)
                                v.tensor_tensor(acc[:, at, :], acc[:, at, :],
                                                ps_sum[b][:, q * P:(q + 1) * P].rearrange("p (o d) -> p o d", o=1),
                                                ALU.add).then_inc(added, 1)

                        front(0, 0)
                        with v.Fori(0, NI - 1) as i:
                            front(i, 1)
                            back(i, 0)
                            front(i + 1, 0)
                            back(i, 1)
                        front(NI - 1, 1)
                        back(NI - 1, 0)
                        back(NI - 1, 1)

                    @block.tensor
                    def _(pe):
                        pe.sem_inc(summed, 2)

                        def half(i, b):
                            n = 2 * i + b
                            pe.wait_ge(oh_ready, n + 1)
                            pe.wait_ge(added, H * n + H)
                            for q in range(H):
                                pe.wait_ge(gathered[H * b + q], 16 * (i + 1))
                                last = pe.matmul(ps_sum[b][:, q * P:(q + 1) * P], oh[:, b, q, :], G[:, H * b + q, :], start=True, stop=True)
                            last.then_inc(summed, 1)

                        with pe.Fori(0, NI) as i:
                            half(i, 0)
                            half(i, 1)

        def stage_gcn_norm(name, acc, dis, y, bn, par_name):
            with ExitStack() as ctx:
                par = sb(f"{name}_par", [P, 3], F32, ctx)
                cur = sb(f"{name}_cur", [P, CT, D], F32, ctx)
                bst = sb(f"{name}_bst", [P, NCH, 6], F32, ctx)
                agg = sb(f"{name}_agg", [P, 2], F32, ctx)
                dev = sb(f"{name}_dev", [P, 2], F32, ctx)
                ps_turn = ps(f"{name}_ps_turn", ctx)
                loaded, seen, dev_ready = sem(f"{name}_loaded"), sem(f"{name}_seen"), sem(f"{name}_dev_ready")
                T = Steps(sem(f"{name}_tensor_steps"), "turned")
                V = Steps(sem(f"{name}_vector_steps"), "cur")
                S = Steps(sem(f"{name}_scalar_steps"), "y")
                with nc.Block() as block:
                    @block.sync
                    def _(sp):
                        sp.dma_start(par[:, :], a[par_name]).then_inc(loaded, 16)

                    @block.tensor
                    def _(pe):
                        T.start(pe)
                        with pe.Fori(0, NCH) as c:
                            pe.wait_ge(*V.now("cur", c))
                            pe.wait_ge(*S.before("y", c))
                            for t in range(CT):
                                last = pe.transpose(ps_turn[:, t * P:(t + 1) * P], cur[:, t, :], ident[:, :])
                            last.then_inc(T.sem, 1)

                    @block.vector
                    def _(v):
                        V.start(v)
                        with v.Fori(0, NCH) as c:
                            v.wait_ge(*T.before("turned", c))
                            v.tensor_tensor(cur[:, :, :], acc[:, chunk(c), :], spread(dis[:, chunk(c)]), ALU.mult).then_inc(V.sem, 1)
                        for k in range(NCH):
                            v.wait_ge(*S.now("y", k))
                            v.bn_stats(bst[:, k, :], y[:, k * CH:min((k + 1) * CH, N)]).then_inc(seen, 1)
                        v.wait_ge(seen, NCH)
                        v.bn_aggr(agg[:, :], bst[:, :, :].rearrange("p k s -> p (k s)")).then_inc(seen, 1)
                        v.wait_ge(dev_ready, 1)
                        v.reciprocal(dev[:, 1:2], dev[:, 0:1]).then_inc(seen, 1)
                        v.wait_ge(seen, NCH + 2)
                        v.tensor_tensor(bn[:, 0:1], dev[:, 1:2], par[:, 1:2], ALU.mult).then_inc(seen, 1)
                        v.wait_ge(seen, NCH + 3)
                        v.tensor_tensor(bn[:, 1:2], agg[:, 0:1], bn[:, 0:1], ALU.mult).then_inc(seen, 1)
                        v.wait_ge(seen, NCH + 4)
                        v.tensor_tensor(bn[:, 1:2], par[:, 2:3], bn[:, 1:2], ALU.subtract)

                    @block.scalar
                    def _(s):
                        S.start(s)
                        s.wait_ge(loaded, 16)
                        with s.Fori(0, NCH) as c:
                            s.wait_ge(*T.now("turned", c))
                            s.activation(y[:, bass.ds(c * CH, CH)], ps_turn[:, :], ACT.Identity, bias=par[:, 0:1]).then_inc(S.sem, 1)
                        s.wait_ge(seen, NCH + 1)
                        s.activation(dev[:, 0:1], agg[:, 1:2], ACT.Sqrt, bias=eps[:, :]).then_inc(dev_ready, 1)

        def stage_gcn_out(y, bn):
            with ExitStack() as ctx:
                z = sb("o_z", [P, CH], F32, ctx)
                ps_back = ps("o_ps_back", ctx)
                T = Steps(sem("o_tensor_steps"), "turned")
                V = Steps(sem("o_vector_steps"), "added")
                S = Steps(sem("o_scalar_steps"), "z")
                with nc.Block() as block:
                    @block.tensor
                    def _(pe):
                        T.start(pe)
                        with pe.Fori(0, NCH) as c:
                            pe.wait_ge(*S.now("z", c))
                            pe.wait_ge(*V.before("added", c))
                            for t in range(CT):
                                last = pe.transpose(ps_back[:, t * P:(t + 1) * P], z[:, t * P:(t + 1) * P], ident[:, :])
                            last.then_inc(T.sem, 1)

                    @block.vector
                    def _(v):
                        V.start(v)
                        with v.Fori(0, NCH) as c:
                            v.wait_ge(*T.now("turned", c))
                            v.tensor_tensor(x[:, chunk(c), :], x[:, chunk(c), :], by_tile(ps_back[:, :]), ALU.add).then_inc(V.sem, 1)

                    @block.scalar
                    def _(s):
                        S.start(s)
                        with s.Fori(0, NCH) as c:
                            s.wait_ge(*T.before("turned", c))
                            s.activation(z[:, :], y[:, bass.ds(c * CH, CH)], ACT.Identity, scale=bn[:, 0:1], bias=bn[:, 1:2]).then_inc(S.sem, 1)

        def stage_dis(dis):
            root, known = sem("root"), sem("known")
            with nc.Block() as block:
                @block.scalar
                def _(s):
                    s.wait_ge(known, 1)
                    s.activation(dis[:, :], dis[:, :], ACT.Sqrt).then_inc(root, 1)

                @block.vector
                def _(v):
                    v.tensor_scalar(dis[:, :], deg[:, :, 1], 1.0, None, ALU.add).then_inc(known, 1)
                    v.wait_ge(root, 1)
                    v.reciprocal(dis[:, :], dis[:, :])

        def stage_mp_tables(own):
            with ExitStack() as ctx:
                w = sb("m_w", [P, 2, 2 * D], F32, ctx)
                be1 = sb("m_be1", [P, 2 * D], F32, ctx)
                cur = sb("m_cur", [P, CT, D], F32, ctx)
                fm = sb("m_fm", [P, CH], F32, ctx)
                rows = sb("m_rows", [P, CT, 2 * D], F32, ctx)
                ps_turn = ps("m_ps_turn", ctx)
                ps_src = [ps(f"m_ps_src{k}", ctx) for k in range(2)]
                ps_dst = [ps(f"m_ps_dst{k}", ctx) for k in range(2)]
                loaded, stored = sem("m_loaded"), sem("m_stored")
                T = Steps(sem("m_tensor_steps"), "turned src dst")
                V = Steps(sem("m_vector_steps"), "cur own")
                S = Steps(sem("m_scalar_steps"), "fm rows")
                with nc.Block() as block:
                    @block.sync
                    def _(sp):
                        loader(sp, loaded, [(w[:, :, :], a["l2_we1n"]), (be1[:, :], a["l2_be1"].to_broadcast([P, 2 * D]))])
                        with sp.Fori(0, NCH) as c:
                            sp.wait_ge(*S.now("rows", c))
                            sp.dma_start(tiles(table2)[:, chunk(c), :], rows[:, :, :]).then_inc(stored, 16)
                        sp.wait_ge(stored, 16 * NCH)

                    @block.tensor
                    def _(pe):
                        T.start(pe)
                        pe.wait_ge(loaded, 32)
                        with pe.Fori(0, NCH) as c:
                            pe.wait_ge(*V.now("cur", c))
                            pe.wait_ge(*S.before("fm", c))
                            for t in range(CT):
                                last = pe.transpose(ps_turn[:, t * P:(t + 1) * P], cur[:, t, :], ident[:, :])
                            last.then_inc(T.sem, 1)
                            pe.wait_ge(*S.now("fm", c))
                            pe.wait_ge(*S.before("rows", c))
                            pe.wait_ge(*V.before("own", c))
                            for k, out in enumerate((ps_src, ps_dst)):
                                for t in range(CT):
                                    last = pe.matmul(out[t // 2][:, t % 2 * 2 * D:(t % 2 + 1) * 2 * D], fm[:, t * P:(t + 1) * P],
                                                     w[:, k, :], start=True, stop=True)
                                last.then_inc(T.sem, 1)

                    @block.vector
                    def _(v):
                        V.start(v)
                        v.wait_ge(loaded, 32)
                        with v.Fori(0, NCH) as c:
                            v.wait_ge(*T.before("turned", c))
                            v.tensor_copy(cur[:, :, :], h[:, chunk(c), 0:D]).then_inc(V.sem, 1)
                            v.wait_ge(*T.now("dst", c))
                            for k in range(2):
                                last = v.tensor_tensor(own[:, bass.ds(c * CT + 2 * k, 2), :], ps_dst[k][:, :].rearrange("p (t d) -> p t d", t=2),
                                                       be1[:, :].unsqueeze(1).to_broadcast([P, 2, 2 * D]), ALU.add)
                            last.then_inc(V.sem, 1)

                    @block.scalar
                    def _(s):
                        S.start(s)
                        with s.Fori(0, NCH) as c:
                            s.wait_ge(*T.now("turned", c))
                            s.wait_ge(*T.before("dst", c))
                            s.copy(fm[:, :], ps_turn[:, :]).then_inc(S.sem, 1)
                            s.wait_ge(*T.now("src", c))
                            s.wait_ge(stored, 16 * c)
                            for k in range(2):
                                last = s.copy(rows[:, 2 * k:2 * k + 2, :].rearrange("p t d -> p (t d)"), ps_src[k][:, :])
                            last.then_inc(S.sem, 1)

        def stage_mp_edges(own, hid):
            with ExitStack() as ctx:
                w = sb("p_w", [DE2, 2 * D], F32, ctx)
                cur = sb("p_cur", [P, 2, H, 2], F32, ctx)
                gidx = sb("p_gidx", [P, 2, H], I32, ctx)
                G = sb("p_G", [P, U, 2 * D], F32, ctx)
                ed = sb("p_ed", [DE2, 2, H * P], F32, ctx)
                oh = sb("p_oh", [P, 2, H, P], F32, ctx)
                ohT = sb("p_ohT", [P, H, P], F32, ctx)
                ps_turn = ps("p_ps_turn", ctx)
                ps_pre = [ps(f"p_ps_pre{k}", ctx) for k in range(4)]
                ps_sum = [ps(f"p_ps_sum{k}", ctx) for k in range(2)]
                loaded = sem("p_loaded")
                cur_ready, gidx_ready, oh_ready = sem("p_cur_ready"), sem("p_gidx_ready"), sem("p_oh_ready")
                turned, ohT_ready, product = sem("p_turned"), sem("p_ohT_ready"), sem("p_product")
                total, hidden = sem("p_total"), sem("p_hidden")
                edges_in = [sem(f"p_edges_in{b}") for b in range(2)]
                gathered = [sem(f"p_gathered{s}") for s in range(U)]
                summed, added = sem("p_summed"), sem("p_added")
                with nc.Block() as block:
                    @block.sync
                    def _(sp):
                        sp.dma_start(w[:, :], a["l2_we1e"]).then_inc(loaded, 16)
                        sp.wait_ge(loaded, 16)

                        def half(i, b):
                            n = 2 * i + b
                            at = [sp.value_load(tile_row[0:1, bass.ds(i * U + H * b + q, 1)], min_val=0, max_val=(ET - 1) * P) for q in range(H)]
                            sp.wait_ge(product, n + 1)
                            sp.nop(nofuse=True)
                            for q in range(H):
                                sp.dma_start(ed[:, b, q * P:(q + 1) * P], a["edge32"][:, bass.ds(at[q], P)]).then_inc(edges_in[b], 16)

                        with sp.Fori(0, NI) as i:
                            half(i, 0)
                            half(i, 1)

                    @block.gpsimd
                    def _(g):
                        def half(i, b):
                            g.wait_ge(gidx_ready, 2 * i + b + 1)
                            g.nop(nofuse=True)
                            for q in range(H):
                                g.indirect_dma_start(G[:, H * b + q, :], None, table2,
                                                     bass.IndirectOffsetOnAxis(ap=gidx[:, b, q:q + 1], axis=0)).then_inc(gathered[H * b + q], 16)

                        with g.Fori(0, NI) as i:
                            half(i, 0)
                            half(i, 1)

                    @block.vector
                    def _(v):
                        v.memset(hid[:, :, :], 0.0).then_inc(added, 2 * H)
                        v.wait_ge(added, 2 * H)

                        def front(i, b):
                            n = 2 * i + b
                            v.wait_ge(summed, n + 1)
                            v.tensor_copy(cur[:, b, :, :], edge_tab[:, bass.ds(i * U + H * b, H), 0:2]).then_inc(cur_ready, 1)
                            v.wait_ge(cur_ready, n + 1)
                            v.tensor_copy(gidx[:, b, :], cur[:, b, :, 0]).then_inc(gidx_ready, 1)
                            for q in range(H):
                                last = v.tensor_scalar(oh[:, b, q, :], iota[:, :], cur[:, b, q, 1:2], None, ALU.is_equal)
                            last.then_inc(oh_ready, 1)

                        def middle(i, b):
                            n = 2 * i + b
                            v.wait_ge(product, n + 3)
                            for q in range(H):
                                s = H * b + q
                                v.wait_ge(gathered[s], 16 * (i + 1))
                                v.tensor_tensor(G[:, s, :], G[:, s, :], ps_pre[2 * b + q // 2][:, q % 2 * 2 * D:(q % 2 + 1) * 2 * D],
                                                ALU.add).then_inc(total, 1)

                        def back(i, b):
                            n = 2 * i + b
                            bucket = buckets_of(v, n)
                            v.wait_ge(summed, n + 3)
                            for q in range(H):
                                at = bass.ds(bucket[q], 1)
                                v.wait_ge(added, H * n + q + 2 * H)
                                v.tensor_tensor(hid[:, at, :], hid[:, at, :],
                                                ps_sum[q // 2][:, q % 2 * 2 * D:(q % 2 + 1) * 2 * D].rearrange("p (o d) -> p o d", o=1),
                                                ALU.add).then_inc(added, 1)

                        front(0, 0)
                        middle(0, 0)
                        with v.Fori(0, NI - 1) as i:
                            front(i, 1)
                            middle(i, 1)
                            back(i, 0)
                            front(i + 1, 0)
                            middle(i + 1, 0)
                            back(i, 1)
                        front(NI - 1, 1)
                        middle(NI - 1, 1)
                        back(NI - 1, 0)
                        back(NI - 1, 1)

                    @block.scalar
                    def _(s):
                        s.sem_inc(ohT_ready, 1)

                        def turn(i, b):
                            n = 2 * i + b
                            s.wait_ge(turned, n + 1)
                            s.wait_ge(product, n + 2)
                            s.copy(ohT[:, :, :].rearrange("p q d -> p (q d)"), ps_turn[:, :]).then_inc(ohT_ready, 1)

                        def act(i, b):
                            n = 2 * i + b
                            for q in range(0, H, 2):
                                s.wait_ge(total, H * n + q + 2)
                                v = G[:, H * b + q:H * b + q + 2, :].rearrange("p q d -> p (q d)")
                                s.activation(v, v, ACT.Silu).then_inc(hidden, 1)

                        with s.Fori(0, NI) as i:
                            turn(i, 0)
                            act(i, 0)
                            turn(i, 1)
                            act(i, 1)

                    @block.tensor
                    def _(pe):
                        pe.sem_inc(summed, 2)
                        pe.sem_inc(product, 2)
                        pe.wait_ge(loaded, 16)

                        def front(i, b):
                            n = 2 * i + b
                            bucket = buckets_of(pe, n)
                            pe.wait_ge(oh_ready, n + 1)
                            pe.wait_ge(ohT_ready, n + 1)
                            for q in range(H):
                                last = pe.transpose(ps_turn[:, q * P:(q + 1) * P], oh[:, b, q, :], ident[:, :])
                            last.then_inc(turned, 1)
                            pe.wait_ge(edges_in[b], 16 * H * (i + 1))
                            pe.wait_ge(ohT_ready, n + 2)
                            if not (isinstance(n, int) and n < 2):
                                pe.wait_ge(total, H * (n - 1))
                            for q in range(H):
                                out = ps_pre[2 * b + q // 2][:, q % 2 * 2 * D:(q % 2 + 1) * 2 * D]
                                pe.matmul(out, ohT[:, q, :], own[:, bass.ds(bucket[q], 1), :].rearrange("p o d -> p (o d)"), start=True, stop=False)
                                last = pe.matmul(out, ed[:, b, q * P:(q + 1) * P], w[:, :], start=False, stop=True)
                            last.then_inc(product, 1)

                        def back(i, b):
                            n = 2 * i + b
                            pe.wait_ge(added, H * n + 2 * H)
                            for q in range(H):
                                pe.wait_ge(hidden, 2 * n + q // 2 + 1)
                                last = pe.matmul(ps_sum[q // 2][:, q % 2 * 2 * D:(q % 2 + 1) * 2 * D], oh[:, b, q, :], G[:, H * b + q, :],
                                                 start=True, stop=True)
                            last.then_inc(summed, 1)

                        front(0, 0)
                        front(0, 1)
                        back(0, 0)
                        with pe.Fori(1, NI) as i:
                            front(i, 0)
                            back(i - 1, 1)
                            front(i, 1)
                            back(i, 0)
                        back(NI - 1, 1)

        def norm_vector(v, V, S, c, tag, src, st, mv4, rs, sh):
            for t in range(CT):
                last = v.bn_stats(st[:, t, :], src[:, t, :])
            last.then_inc(V.sem, 1)
            v.wait_ge(*V.now(tag + "stats", c))
            v.tensor_tensor(mv4[:, 0, :], st[:, :, 1], st[:, :, 4], ALU.add).then_inc(V.sem, 1)
            v.tensor_tensor(sh[:, :], st[:, :, 1], st[:, :, 4], ALU.subtract).then_inc(V.sem, 1)
            v.tensor_tensor(mv4[:, 1, :], st[:, :, 2], st[:, :, 5], ALU.add).then_inc(V.sem, 1)
            v.wait_ge(*V.now(tag + "squares", c))
            v.tensor_scalar(mv4[:, 0, :], mv4[:, 0, :], 0.5, None, ALU.mult).then_inc(V.sem, 1)
            v.tensor_scalar(mv4[:, 1, :], mv4[:, 1, :], 1.0 / D, None, ALU.mult).then_inc(V.sem, 1)
            v.scalar_tensor_tensor(out=sh[:, :], in0=sh[:, :], scalar=0.25, in1=sh[:, :], op0=ALU.mult, op1=ALU.mult).then_inc(V.sem, 1)
            v.wait_ge(*V.now(tag + "gap2", c))
            v.tensor_tensor(mv4[:, 1, :], mv4[:, 1, :], sh[:, :], ALU.add).then_inc(V.sem, 1)
            v.wait_ge(*S.now(tag + "std", c))
            v.reciprocal(rs[:, :], rs[:, :]).then_inc(V.sem, 1)
            v.wait_ge(*V.now(tag + "rstd", c))
            v.scalar_tensor_tensor(out=sh[:, :], in0=mv4[:, 0, :], scalar=-1.0, in1=rs[:, :], op0=ALU.mult, op1=ALU.mult).then_inc(V.sem, 1)

        def norm_steps(tag):
            return " ".join(tag + k for k in "stats means gap squares mean spread gap2 var rstd shift".split())

        def stage_mp_nodes(hid):
            with ExitStack() as ctx:
                we2 = sb("q_we2", [P, 2, D], F32, ctx)
                be2 = sb("q_be2", [P, D], F32, ctx)
                wn1 = sb("q_wn1", [P, 2, 2 * D], F32, ctx)
                bn1 = sb("q_bn1", [P, 2], F32, ctx)
                wn2 = sb("q_wn2", [P, 2, D], F32, ctx)
                rowp = sb("q_rowp", [P, 5, D], F32, ctx)
                mask = sb("q_mask", [P, NT], F32, ctx)
                cur = sb("q_cur", [P, CT, 2 * D], F32, ctx)
                hidT = sb("q_hidT", [P, 2, CH], F32, ctx)
                agg = sb("q_agg", [P, CT, D], F32, ctx)
                nod = sb("q_nod", [P, 2, CT, D], F32, ctx)
                nodT = sb("q_nodT", [P, 2, CH], F32, ctx)
                act = sb("q_act", [P, 2, CH], F32, ctx)
                nf = sb("q_nf", [P, CT, D], F32, ctx)
                st = sb("q_st", [P, CT, 6], F32, ctx)
                mv4 = sb("q_mv4", [P, 2, CT], F32, ctx)
                rs = sb("q_rs", [P, CT], F32, ctx)
                sh = sb("q_sh", [P, CT], F32, ctx)
                ps_a = [ps(f"q_ps_a{k}", ctx) for k in range(2)]
                ps_agg = ps("q_ps_agg", ctx)
                ps_b = [ps(f"q_ps_b{k}", ctx) for k in range(2)]
                ps_c = [ps(f"q_ps_c{k}", ctx) for k in range(2)]
                ps_nf = ps("q_ps_nf", ctx)
                loaded, ready = sem("q_loaded"), sem("q_ready")
                T = Steps(sem("q_tensor_steps"), "hid_turned agg nod_turned hidden nf")
                V = Steps(sem("q_vector_steps"), "cur h agg " + norm_steps("m_") + " m_g m_b m_mask bias res " + norm_steps("n_") +
                          " n_g n_b n_mask added")
                S = Steps(sem("q_scalar_steps"), "hidT m_std m_normed nodT act n_std n_normed")
                with nc.Block() as block:
                    @block.sync
                    def _(sp):
                        loader(sp, loaded, [
                            (we2[:, :, :], a["l2_we2"]), (be2[:, :], a["l2_be2"].to_broadcast([P, D])), (wn1[:, :, :], a["l2_wn1"]),
                            (bn1[:, :], a["l2_bn1"]), (wn2[:, :, :], a["l2_wn2"]),
                            (rowp[:, :, :], a["l2_rows"].unsqueeze(0).to_broadcast([P, 5, D])), (mask[:, :], a["mask"])])

                    @block.tensor
                    def _(pe):
                        T.start(pe)
                        pe.wait_ge(ready, 2)
                        with pe.Fori(0, NCH) as c:
                            pe.wait_ge(*V.now("cur", c))
                            pe.wait_ge(*S.before("hidT", c))
                            for t in range(CT):
                                for k in range(2):
                                    last = pe.transpose(ps_a[k][:, t * P:(t + 1) * P], cur[:, t, k * D:(k + 1) * D], ident[:, :])
                            last.then_inc(T.sem, 1)
                            pe.wait_ge(*S.now("hidT", c))
                            pe.wait_ge(*V.before("agg", c))
                            for t in range(CT):
                                for k in range(2):
                                    last = pe.matmul(ps_agg[:, t * P:(t + 1) * P], hidT[:, k, t * P:(t + 1) * P], we2[:, k, :], start=k == 0, stop=k == 1)
                            last.then_inc(T.sem, 1)
                            pe.wait_ge(*V.now("m_mask", c))
                            pe.wait_ge(*S.before("nodT", c))
                            for t in range(CT):
                                for k in range(2):
                                    last = pe.transpose(ps_b[k][:, t * P:(t + 1) * P], nod[:, k, t, :], ident[:, :])
                            last.then_inc(T.sem, 1)
                            pe.wait_ge(*S.now("nodT", c))
                            pe.wait_ge(*S.before("act", c))
                            for m in range(2):
                                for k in range(2):
                                    last = pe.matmul(ps_c[m][:, :], wn1[:, k, m * D:(m + 1) * D], nodT[:, k, :], start=k == 0, stop=k == 1)
                            last.then_inc(T.sem, 1)
                            pe.wait_ge(*S.now("act", c))
                            pe.wait_ge(*V.before("bias", c))
                            for t in range(CT):
                                for k in range(2):
                                    last = pe.matmul(ps_nf[:, t * P:(t + 1) * P], act[:, k, t * P:(t + 1) * P], wn2[:, k, :], start=k == 0, stop=k == 1)
                            last.then_inc(T.sem, 1)

                    @block.vector
                    def _(v):
                        V.start(v)
                        v.wait_ge(loaded, 7 * 16)
                        v.tensor_scalar(we2[:, :, :], we2[:, :, :], 1.0 / 16, None, ALU.mult).then_inc(ready, 1)
                        v.tensor_scalar(be2[:, :], be2[:, :], 1.0 / 16, None, ALU.mult).then_inc(ready, 1)
                        v.wait_ge(ready, 2)
                        with v.Fori(0, NCH) as c:
                            v.wait_ge(*T.before("hid_turned", c))
                            v.tensor_copy(cur[:, :, :], hid[:, chunk(c), :]).then_inc(V.sem, 1)
                            v.wait_ge(*T.before("nod_turned", c))
                            v.tensor_copy(nod[:, 0, :, :], h[:, chunk(c), 0:D]).then_inc(V.sem, 1)
                            v.wait_ge(*T.now("agg", c))
                            for t in range(CT):
                                last = v.scalar_tensor_tensor(out=agg[:, t, :], in0=be2[:, :], scalar=deg[:, bass.ds(c * CT + t, 1), 1],
                                                              in1=ps_agg[:, t * P:(t + 1) * P], op0=ALU.mult, op1=ALU.add)
                            last.then_inc(V.sem, 1)
                            v.wait_ge(*V.now("agg", c))
                            norm_vector(v, V, S, c, "m_", agg, st, mv4, rs, sh)
                            v.wait_ge(*S.now("m_normed", c))
                            v.tensor_tensor(nod[:, 1, :, :], nod[:, 1, :, :], across(rowp[:, 0, :]), ALU.mult).then_inc(V.sem, 1)
                            v.wait_ge(*V.now("m_g", c))
                            v.tensor_tensor(nod[:, 1, :, :], nod[:, 1, :, :], across(rowp[:, 1, :]), ALU.add).then_inc(V.sem, 1)
                            v.wait_ge(*V.now("m_b", c))
                            v.tensor_tensor(nod[:, 1, :, :], nod[:, 1, :, :], spread(mask[:, chunk(c)]), ALU.mult).then_inc(V.sem, 1)
                            v.wait_ge(*T.now("nf", c))
                            v.tensor_tensor(nf[:, :, :], by_tile(ps_nf[:, :]), across(rowp[:, 2, :]), ALU.add).then_inc(V.sem, 1)
                            v.wait_ge(*V.now("bias", c))
                            v.tensor_tensor(nf[:, :, :], nf[:, :, :], nod[:, 0, :, :], ALU.add).then_inc(V.sem, 1)
                            v.wait_ge(*V.now("res", c))
                            norm_vector(v, V, S, c, "n_", nf, st, mv4, rs, sh)
                            v.wait_ge(*S.now("n_normed", c))
                            v.tensor_tensor(nf[:, :, :], nf[:, :, :], across(rowp[:, 3, :]), ALU.mult).then_inc(V.sem, 1)
                            v.wait_ge(*V.now("n_g", c))
                            v.tensor_tensor(nf[:, :, :], nf[:, :, :], across(rowp[:, 4, :]), ALU.add).then_inc(V.sem, 1)
                            v.wait_ge(*V.now("n_b", c))
                            v.tensor_tensor(nf[:, :, :], nf[:, :, :], spread(mask[:, chunk(c)]), ALU.mult).then_inc(V.sem, 1)
                            v.wait_ge(*V.now("n_mask", c))
                            v.tensor_tensor(x[:, chunk(c), :], x[:, chunk(c), :], nf[:, :, :], ALU.add).then_inc(V.sem, 1)

                    @block.scalar
                    def _(s):
                        S.start(s)
                        s.wait_ge(loaded, 7 * 16)
                        with s.Fori(0, NCH) as c:
                            s.wait_ge(*T.now("hid_turned", c))
                            s.wait_ge(*T.before("agg", c))
                            for k in range(2):
                                last = s.copy(hidT[:, k, :], ps_a[k][:, :])
                            last.then_inc(S.sem, 1)
                            s.wait_ge(*V.now("m_var", c))
                            s.activation(rs[:, :], mv4[:, 1, :], ACT.Sqrt, bias=eps[:, :]).then_inc(S.sem, 1)
                            s.wait_ge(*V.now("m_shift", c))
                            for t in range(CT):
                                last = s.activation(nod[:, 1, t, :], agg[:, t, :], ACT.Identity, scale=rs[:, t:t + 1], bias=sh[:, t:t + 1])
                            last.then_inc(S.sem, 1)
                            s.wait_ge(*T.now("nod_turned", c))
                            for k in range(2):
                                last = s.copy(nodT[:, k, :], ps_b[k][:, :])
                            last.then_inc(S.sem, 1)
                            s.wait_ge(*T.now("hidden", c))
                            for k in range(2):
                                last = s.activation(act[:, k, :], ps_c[k][:, :], ACT.Silu, bias=bn1[:, k:k + 1])
                            last.then_inc(S.sem, 1)
                            s.wait_ge(*V.now("n_var", c))
                            s.activation(rs[:, :], mv4[:, 1, :], ACT.Sqrt, bias=eps[:, :]).then_inc(S.sem, 1)
                            s.wait_ge(*V.now("n_shift", c))
                            for t in range(CT):
                                last = s.activation(nf[:, t, :], nf[:, t, :], ACT.Identity, scale=rs[:, t:t + 1], bias=sh[:, t:t + 1])
                            last.then_inc(S.sem, 1)

        def stage_cutoff(fac):
            with ExitStack() as ctx:
                turns = sb("k_turns", [P, PG * P], F32, ctx)
                whole = sb("k_whole", [P, PG * P], I32, ctx)
                wholef = sb("k_wholef", [P, PG * P], F32, ctx)
                step, wave = sem("k_step"), sem("k_wave")
                with nc.Block() as block:
                    @block.vector
                    def _(v):
                        n = [0]

                        def then(ins):
                            n[0] += 1
                            ins.then_inc(step, 1)
                            v.wait_ge(step, n[0])

                        then(v.tensor_scalar(turns[:, :], edge_tab[:, :, 2], 0.5 / CUTOFF, 0.25, ALU.mult, ALU.add))
                        then(v.tensor_copy(whole[:, :], turns[:, :]))
                        then(v.tensor_copy(wholef[:, :], whole[:, :]))
                        then(v.tensor_tensor(turns[:, :], turns[:, :], wholef[:, :], ALU.subtract))
                        then(v.tensor_scalar(wholef[:, :], turns[:, :], 0.5, None, ALU.is_gt))
                        then(v.tensor_scalar(fac[:, :], turns[:, :], -0.5, None, ALU.is_lt))
                        then(v.tensor_tensor(turns[:, :], turns[:, :], wholef[:, :], ALU.subtract))
                        then(v.tensor_tensor(turns[:, :], turns[:, :], fac[:, :], ALU.add))
                        v.wait_ge(wave, 1)
                        v.tensor_scalar(fac[:, :], fac[:, :], 0.5, 0.5, ALU.mult, ALU.add)

                    @block.scalar
                    def _(s):
                        s.wait_ge(step, 8)
                        s.activation(fac[:, :], turns[:, :], ACT.Sin, scale=6.283185).then_inc(wave, 1)

        def stage_cf_edges(acc, fac):
            with ExitStack() as ctx:
                w1 = sb("c_w1", [DE3, D], F32, ctx)
                w2 = sb("c_w2", [P, D], F32, ctx)
                b1 = sb("c_b1", [P, 1], F32, ctx)
                b2 = sb("c_b2", [P, D], F32, ctx)
                cur = sb("c_cur", [P, 2, H, 3], F32, ctx)
                gidx = sb("c_gidx", [P, 2, H], I32, ctx)
                G = sb("c_G", [P, U, D], F32, ctx)
                ed = sb("c_ed", [DE3, 2, CH], F32, ctx)
                oh = sb("c_oh", [P, 2, H, P], F32, ctx)
                mag = sb("c_mag", [P, CH], F32, ctx)
                pos = sb("c_pos", [P, CH], F32, ctx)
                sp_ = sb("c_sp", [P, 2, CH], F32, ctx)
                filt = sb("c_filt", [P, H, D], F32, ctx)
                ps_lin = ps("c_ps_lin", ctx)
                ps_filt = ps("c_ps_filt", ctx)
                ps_sum = [ps(f"c_ps_sum{k}", ctx) for k in range(2)]
                loaded = sem("c_loaded")
                cur_ready, gidx_ready, oh_ready = sem("c_cur_ready"), sem("c_gidx_ready"), sem("c_oh_ready")
                linear, act_step, ssp_ready = sem("c_linear"), sem("c_act_step"), sem("c_ssp_ready")
                filtered, filt_ready, message = sem("c_filtered"), sem("c_filt_ready"), sem("c_message")
                edges_in = [sem(f"c_edges_in{b}") for b in range(2)]
                gathered = [sem(f"c_gathered{s}") for s in range(U)]
                summed, added = sem("c_summed"), sem("c_added")
                with nc.Block() as block:
                    @block.sync
                    def _(sp):
                        loader(sp, loaded, [(w1[:, :], a["l3_w1"]), (w2[:, :], a["l3_w2"]), (b1[:, :], a["l3_b1"]),
                                            (b2[:, :], a["l3_b2"].to_broadcast([P, D]))])

                        def half(i, b):
                            n = 2 * i + b
                            at = [sp.value_load(tile_row[0:1, bass.ds(i * U + H * b + q, 1)], min_val=0, max_val=(ET - 1) * P) for q in range(H)]
                            sp.wait_ge(linear, n + 1)
                            sp.nop(nofuse=True)
                            for q in range(H):
                                sp.dma_start(ed[:, b, q * P:(q + 1) * P], a["edge50"][:, bass.ds(at[q], P)]).then_inc(edges_in[b], 16)

                        with sp.Fori(0, NI) as i:
                            half(i, 0)
                            half(i, 1)

                    @block.gpsimd
                    def _(g):
                        def half(i, b):
                            g.wait_ge(gidx_ready, 2 * i + b + 1)
                            g.nop(nofuse=True)
                            for q in range(H):
                                g.indirect_dma_start(G[:, H * b + q, :], None, table,
                                                     bass.IndirectOffsetOnAxis(ap=gidx[:, b, q:q + 1], axis=0)).then_inc(gathered[H * b + q], 16)

                        with g.Fori(0, NI) as i:
                            half(i, 0)
                            half(i, 1)

                    @block.vector
                    def _(v):
                        v.memset(acc[:, :, :], 0.0).then_inc(added, 2 * H)
                        v.wait_ge(added, 2 * H)
                        v.wait_ge(loaded, 64)

                        def front(i, b):
                            n = 2 * i + b
                            v.wait_ge(summed, n + 1)
                            v.tensor_copy(cur[:, b, :, 2], fac[:, bass.ds(i * U + H * b, H)])
                            v.tensor_copy(cur[:, b, :, 0:2], edge_tab[:, bass.ds(i * U + H * b, H), 0:2]).then_inc(cur_ready, 1)
                            v.wait_ge(cur_ready, n + 1)
                            v.tensor_copy(gidx[:, b, :], cur[:, b, :, 0]).then_inc(gidx_ready, 1)
                            for q in range(H):
                                last = v.tensor_scalar(oh[:, b, q, :], iota[:, :], cur[:, b, q, 1:2], cur[:, b, q, 2:3], ALU.is_equal, ALU.mult)
                            last.then_inc(oh_ready, 1)

                        def middle(i, b):
                            n = 2 * i + b
                            v.wait_ge(act_step, 4 * n + 4)
                            v.scalar_tensor_tensor(out=sp_[:, b, :], in0=mag[:, :], scalar=-LOG2, in1=pos[:, :], op0=ALU.add,
                                                   op1=ALU.add).then_inc(ssp_ready, 1)
                            v.wait_ge(filtered, n + 1)
                            v.tensor_tensor(filt[:, :, :], by_tile(ps_filt[:, :]), across(b2[:, :]), ALU.add).then_inc(filt_ready, 1)
                            v.wait_ge(filt_ready, n + 2)
                            for q in range(H):
                                v.wait_ge(gathered[H * b + q], 16 * (i + 1))
                            v.tensor_tensor(G[:, H * b:H * b + H, :], G[:, H * b:H * b + H, :], filt[:, :, :], ALU.mult).then_inc(message, 1)

                        def back(i, b):
                            n = 2 * i + b
                            bucket = buckets_of(v, n)
                            v.wait_ge(summed, n + 3)
                            for q in range(H):
                                at = bass.ds(bucket[q], 1)
                                v.wait_ge(added, H * n + q + 2 * H)
                                v.tensor_tensor(acc[:, at, :], acc[:, at, :],
                                                ps_sum[b][:, q * P:(q + 1) * P].rearrange("p (o d) -> p o d", o=1),
                                                ALU.add).then_inc(added, 1)

                        v.sem_inc(ssp_ready, 1)
                        v.sem_inc(filt_ready, 1)
                        front(0, 0)
                        middle(0, 0)
                        with v.Fori(0, NI - 1) as i:
                            front(i, 1)
                            middle(i, 1)
                            back(i, 0)
                            front(i + 1, 0)
                            middle(i + 1, 0)
                            back(i, 1)
                        front(NI - 1, 1)
                        middle(NI - 1, 1)
                        back(NI - 1, 0)
                        back(NI - 1, 1)

                    @block.scalar
                    def _(s):
                        s.wait_ge(loaded, 64)

                        def half(i, b):
                            n = 2 * i + b
                            s.wait_ge(linear, n + 3)
                            s.wait_ge(ssp_ready, n + 1)
                            s.activation(pos[:, :], ps_lin[:, :], ACT.Relu, bias=b1[:, :]).then_inc(act_step, 1)
                            s.activation(mag[:, :], ps_lin[:, :], ACT.Abs, bias=b1[:, :]).then_inc(act_step, 1)
                            s.wait_ge(act_step, 4 * n + 2)
                            s.activation(mag[:, :], mag[:, :], ACT.Exp, scale=-1.0).then_inc(act_step, 1)
                            s.wait_ge(act_step, 4 * n + 3)
                            s.activation(mag[:, :], mag[:, :], ACT.Ln, bias=1.0).then_inc(act_step, 1)

                        with s.Fori(0, NI) as i:
                            half(i, 0)
                            half(i, 1)

                    @block.tensor
                    def _(pe):
                        pe.sem_inc(summed, 2)
                        pe.sem_inc(linear, 2)
                        pe.wait_ge(loaded, 64)

                        def front(i, b):
                            n = 2 * i + b
                            pe.wait_ge(edges_in[b], 16 * H * (i + 1))
                            pe.wait_ge(ssp_ready, n + 1)
                            pe.matmul(ps_lin[:, :], w1[:, :], ed[:, b, :], start=True, stop=True).then_inc(linear, 1)
                            pe.wait_ge(ssp_ready, n + 2)
                            pe.wait_ge(filt_ready, n + 1)
                            for q in range(H):
                                last = pe.matmul(ps_filt[:, q * P:(q + 1) * P], sp_[:, b, q * P:(q + 1) * P], w2[:, :], start=True, stop=True)
                            last.then_inc(filtered, 1)

                        def back(i, b):
                            n = 2 * i + b
                            pe.wait_ge(added, H * n + H)
                            pe.wait_ge(message, n + 1)
                            for q in range(H):
                                last = pe.matmul(ps_sum[b][:, q * P:(q + 1) * P], oh[:, b, q, :], G[:, H * b + q, :], start=True, stop=True)
                            last.then_inc(summed, 1)

                        with pe.Fori(0, NI) as i:
                            front(i, 0)
                            back(i, 0)
                            front(i, 1)
                            back(i, 1)

        def stage_cf_nodes(acc):
            with ExitStack() as ctx:
                w = sb("f_w", [P, D], F32, ctx)
                bias = sb("f_bias", [P, D], F32, ctx)
                cur = sb("f_cur", [P, CT, D], F32, ctx)
                fm = sb("f_fm", [P, CH], F32, ctx)
                lin = sb("f_lin", [P, CT, D], F32, ctx)
                mag = sb("f_mag", [P, CT, D], F32, ctx)
                pos = sb("f_pos", [P, CT, D], F32, ctx)
                ps_turn, ps_out = ps("f_ps_turn", ctx), ps("f_ps_out", ctx)
                loaded, stored = sem("f_loaded"), sem("f_stored")
                T = Steps(sem("f_tensor_steps"), "turned product")
                V = Steps(sem("f_vector_steps"), "cur lin ssp added")
                S = Steps(sem("f_scalar_steps"), "fm pos mag exp ln")
                with nc.Block() as block:
                    @block.sync
                    def _(sp):
                        loader(sp, loaded, [(w[:, :], a["l3_lin2"]), (bias[:, :], a["l3_lin2_b"].to_broadcast([P, D]))])
                        with sp.Fori(0, NCH) as c:
                            sp.wait_ge(*V.now("added", c))
                            sp.dma_start(out_x[:, chunk(c), :], x[:, chunk(c), :]).then_inc(stored, 16)
                        sp.wait_ge(stored, 16 * NCH)

                    @block.tensor
                    def _(pe):
                        T.start(pe)
                        pe.wait_ge(loaded, 32)
                        with pe.Fori(0, NCH) as c:
                            pe.wait_ge(*V.now("cur", c))
                            pe.wait_ge(*S.before("fm", c))
                            for t in range(CT):
                                last = pe.transpose(ps_turn[:, t * P:(t + 1) * P], cur[:, t, :], ident[:, :])
                            last.then_inc(T.sem, 1)
                            pe.wait_ge(*S.now("fm", c))
                            pe.wait_ge(*V.before("lin", c))
                            for t in range(CT):
                                last = pe.matmul(ps_out[:, t * P:(t + 1) * P], fm[:, t * P:(t + 1) * P], w[:, :], start=True, stop=True)
                            last.then_inc(T.sem, 1)

                    @block.vector
                    def _(v):
                        V.start(v)
                        v.wait_ge(loaded, 32)
                        with v.Fori(0, NCH) as c:
                            v.wait_ge(*T.before("turned", c))
                            v.tensor_copy(cur[:, :, :], acc[:, chunk(c), :]).then_inc(V.sem, 1)
                            v.wait_ge(*T.now("product", c))
                            v.wait_ge(*S.before("ln", c))
                            v.tensor_tensor(lin[:, :, :], by_tile(ps_out[:, :]), across(bias[:, :]), ALU.add).then_inc(V.sem, 1)
                            v.wait_ge(*S.now("ln", c))
                            v.scalar_tensor_tensor(out=pos[:, :, :], in0=mag[:, :, :], scalar=-LOG2, in1=pos[:, :, :], op0=ALU.add,
                                                   op1=ALU.add).then_inc(V.sem, 1)
                            v.wait_ge(*V.now("ssp", c))
                            v.tensor_tensor(x[:, chunk(c), :], x[:, chunk(c), :], pos[:, :, :], ALU.add).then_inc(V.sem, 1)

                    @block.scalar
                    def _(s):
                        S.start(s)
                        with s.Fori(0, NCH) as c:
                            s.wait_ge(*T.now("turned", c))
                            s.wait_ge(*T.before("product", c))
                            s.copy(fm[:, :], ps_turn[:, :]).then_inc(S.sem, 1)
                            s.wait_ge(*V.now("lin", c))
                            s.wait_ge(*V.before("added", c))
                            s.activation(pos[:, :, :], lin[:, :, :], ACT.Relu).then_inc(S.sem, 1)
                            s.activation(mag[:, :, :], lin[:, :, :], ACT.Abs).then_inc(S.sem, 1)
                            s.wait_ge(*S.now("mag", c))
                            s.activation(mag[:, :, :], mag[:, :, :], ACT.Exp, scale=-1.0).then_inc(S.sem, 1)
                            s.wait_ge(*S.now("exp", c))
                            s.activation(mag[:, :, :], mag[:, :, :], ACT.Ln, bias=1.0).then_inc(S.sem, 1)

        def stage_ones(one):
            with nc.Block() as block:
                @block.vector
                def _(v):
                    v.memset(one[:, :], 1.0)

        stage_tables()
        stage_done()
        stage_norm("norm0", True)
        stage_done()
        with ExitStack() as l0:
            sum_dst = sb("sum_dst", [P, NT, D], F32, l0)
            stage_gru_edges(sum_dst)
            stage_done()
            stage_gru_nodes(sum_dst)
            stage_done()
        stage_norm("norm1", False)
        stage_done()
        with ExitStack() as l1:
            acc = sb("acc", [P, NT, D], F32, l1)
            y = sb("y", [P, NP], F32, l1)
            dis = sb("dis", [P, NT], F32, l1)
            bn = sb("bn", [P, 2], F32, l1)
            stage_dis(dis)
            stage_done()
            stage_gcn_table("t1", acc, "l1_w1", dis)
            stage_done()
            stage_sum_edges("e1", acc)
            stage_done()
            stage_gcn_norm("n1", acc, dis, y, bn, "l1_par1")
            stage_done()
            stage_gcn_table("t2", acc, "l1_w2", dis, y, bn)
            stage_done()
            stage_sum_edges("e2", acc)
            stage_done()
            stage_gcn_norm("n2", acc, dis, y, bn, "l1_par2")
            stage_done()
            stage_gcn_out(y, bn)
            stage_done()
        stage_norm("norm2", False)
        stage_done()
        with ExitStack() as l2:
            hid = sb("hid", [P, NT, 2 * D], F32, l2)
            with ExitStack() as l2e:
                own = sb("own", [P, NT, 2 * D], F32, l2e)
                stage_mp_tables(own)
                stage_done()
                stage_mp_edges(own, hid)
                stage_done()
            stage_mp_nodes(hid)
            stage_done()
        stage_norm("norm3", False)
        stage_done()
        with ExitStack() as l3:
            acc3 = sb("acc3", [P, NT, D], F32, l3)
            one = sb("one3", [P, NT], F32, l3)
            fac = sb("fac", [P, PG * P], F32, l3)
            stage_ones(one)
            stage_done()
            stage_cutoff(fac)
            stage_done()
            stage_gcn_table("t3", acc3, "l3_lin1", one)
            stage_done()
            stage_cf_edges(acc3, fac)
            stage_done()
            stage_cf_nodes(acc3)
            stage_done()


def laid_out(inputs):
    f = {k: np.asarray(v) for k, v in inputs.items()}
    pad = ET * P - E

    def nm(v):
        v = np.pad(v, ((0, NP - N), (0, 0)))
        return np.ascontiguousarray(v.reshape(NT, P, -1).transpose(1, 0, 2))

    r = {"x": nm(f["x"]), "mask": nm(f["node_vec1"])[:, :, 0].copy()}
    dst = np.pad(f["dst"], (0, pad), constant_values=PAD_NODE).reshape(ET, P)
    r["dst"] = dst
    r["src"] = np.pad(f["src"], (0, pad)).reshape(ET, P)
    r["tile_ends"] = np.ascontiguousarray(dst[:, [0, -1]].T)
    r["edge_weight"] = np.pad(f["edge_weight"], (0, pad)).reshape(ET, P)
    r["edge32"] = np.ascontiguousarray(np.pad(f["edge_attr_32"], ((0, pad), (0, 0))).T)
    r["edge50"] = np.ascontiguousarray(np.pad(f["edge_attr_50"], ((0, pad), (0, 0))).T)
    c = np.ascontiguousarray

    def cut(v, k):
        return c(v.reshape(k, P, -1).transpose(1, 0, 2))

    def cols(*vs):
        return c(np.concatenate([v.reshape(-1, P).T for v in vs], 1))

    r["l0_w12"] = c(np.stack([f["L0_gnn_W1"], f["L0_gnn_W2"]], 1))
    r["l0_wih"] = cut(f["L0_gnn_w_ih"].T, 2)
    r["l0_whh"] = c(f["L0_gnn_w_hh"].T)
    r["l0_bias"] = c(np.stack([cols(f["L0_gnn_b_ih"]), cols(f["L0_gnn_b_hh"])], 1))
    r["l1_w1"], r["l1_w2"] = f["L1_gnn_W1"], f["L1_gnn_W2"]
    r["l1_par1"] = cols(f["L1_gnn_b1"], f["L1_gnn_g1"], f["L1_gnn_bt1"])
    r["l1_par2"] = cols(f["L1_gnn_b2"], f["L1_gnn_g2"], f["L1_gnn_bt2"])
    r["l2_we1n"] = cut(f["L2_gnn_We1"][:2 * D], 2)
    r["l2_we1e"] = c(f["L2_gnn_We1"][2 * D:])
    r["l2_be1"] = f["L2_gnn_be1"][None]
    r["l2_we2"] = cut(f["L2_gnn_We2"], 2)
    r["l2_be2"] = f["L2_gnn_be2"][None]
    r["l2_wn1"] = cut(f["L2_gnn_Wn1"], 2)
    r["l2_bn1"] = cols(f["L2_gnn_bn1"])
    r["l2_wn2"] = cut(f["L2_gnn_Wn2"], 2)
    r["l2_rows"] = c(np.stack([f["L2_gnn_" + k] for k in ("g_msg", "b_msg", "bn2", "g_node", "b_node")]))
    r["l3_w1"] = c(f["L3_gnn_mlp_w1"].T)
    r["l3_b1"] = cols(f["L3_gnn_mlp_b1"])
    r["l3_w2"] = c(f["L3_gnn_mlp_w2"].T)
    r["l3_b2"] = f["L3_gnn_mlp_b2"][None]
    r["l3_lin1"] = c(f["L3_gnn_lin1_w"].T)
    r["l3_lin2"] = c(f["L3_gnn_lin2_w"].T)
    r["l3_lin2_b"] = f["L3_gnn_lin2_b"][None]
    return r


def kernel(**inputs):
    import concourse.bacc as bacc
    from concourse.bass_utils import run_bass_kernel_spmd

    nc = bacc.Bacc("TRN2", target_bir_lowering=False, num_devices=1)
    arrays, args = {}, {}
    for name, v in laid_out(inputs).items():
        arrays[f"in_{name}_dram"] = v
        args[name] = nc.dram_tensor(f"in_{name}_dram", v.shape, mybir.dt.from_np(v.dtype), kind="ExternalInput").ap()
    out = nc.dram_tensor("out_0_dram", (P, NT, D), F32, kind="ExternalOutput").ap()
    build(nc, args, out)
    r = run_bass_kernel_spmd(nc, [arrays], core_ids=[0])
    return r.results[0]["out_0_dram"].transpose(1, 0, 2).reshape(NP, D)[:N]
```

```python
from contextlib import ExitStack

import numpy as np
import concourse.bass as bass
from concourse import mybir

F32 = mybir.dt.float32
I32 = mybir.dt.int32
ALU = mybir.AluOpType
ACT = mybir.ActivationFunctionType
AX_X = mybir.AxisListType.X

P = 128
N = 6250
D = 128
E = 200000
ET = -(-E // P)
BUCKETS = -(-N // P)
CH = 512
CT = CH // P
NCH = -(-N // CH)
NT = NCH * CT
NP = NT * P
PAD_NODE = BUCKETS * P - 1
H = 4
NB = 4
U = NB * H
NI = -(-(ET + BUCKETS - 1) // U)
PAIRS = NI * U
PG = -(-PAIRS // P)
SUMS = 4
EPS = 1e-5
DE2 = 32
DE3 = 50
PI = float(np.pi)
CUTOFF = 10.0
LOG2 = float(np.log(2.0))


def over_quads(eng, *steps):
    def turn(i, b):
        for step, lag in steps:
            at = i + (b - lag) // NB
            if not isinstance(at, int) or 0 <= at < NI:
                step(at, (b - lag) % NB)

    for b in range(NB):
        turn(0, b)
    with eng.Fori(1, NI) as i:
        for b in range(NB):
            turn(i, b)
    for b in range(max(lag for _, lag in steps)):
        turn(NI, b)


class Steps:

    def __init__(self, sem, names):
        self.sem, self.names = sem, names.split()

    def start(self, eng):
        eng.sem_inc(self.sem, len(self.names))

    def now(self, name, c):
        return self.sem, (c + 1) * len(self.names) + self.names.index(name) + 1

    def before(self, name, c):
        return self.sem, c * len(self.names) + self.names.index(name) + 1


def build(nc, a, out_x):
    es = ExitStack()

    def sb(name, shape, dt=F32, ctx=None):
        return (ctx or es).enter_context(nc.sbuf_tensor(name, shape, dt))

    def ps(name, ctx, shape=(P, 512)):
        return ctx.enter_context(nc.psum_tensor(name, list(shape), F32))

    stage_sems = []

    def sem(name):
        stage_sems.append(nc.alloc_semaphore(name))
        return stage_sems[-1]

    def stage_done():
        nc.clear_and_free_semaphores(stage_sems)
        stage_sems.clear()
        nc.all_engine_barrier()

    def dram(name, shape, dt=F32):
        return nc.dram_tensor(name, shape, dt, kind="Internal").ap()

    def tiles(ap):
        return ap.rearrange("(t p) w -> p t w", p=P)

    table = dram("table", (NP, D))
    x_save = dram("x_save", (P, NT, D))
    table2 = dram("table2", (NP, 2 * D))
    srcsum = [dram(f"srcsum{q}", (NP + P, D + 1)) for q in range(SUMS)]
    row_scratch = dram("row_scratch", (2, PG * P), I32)

    with es:
        x = sb("x", [P, NT, D])
        h = sb("h", [P, NT, D + 1])
        ident = sb("ident", [P, P])
        iota = sb("iota", [P, P])
        earlier = sb("earlier", [P, P])
        trash_row = sb("trash_row", [P, 1])
        edge_tab = sb("edge_tab", [P, PG * P, 3])
        tile_row = sb("tile_row", [1, PG * P], I32)
        bucket_row = sb("bucket_row", [1, PG * P // H], I32)
        deg = sb("deg", [P, NT, 2])
        stat = sb("stat", [P, NT, 6])
        mv = sb("mv", [P, NT, 2])
        rstd = sb("rstd", [P, NT])
        nmr = sb("nmr", [P, NT])
        eps = sb("eps", [P, 1])

        def stage_tables():
            with ExitStack() as ctx:
                lo_i = sb("lo_i", [P, 2, ET], I32, ctx)
                lo = sb("lo", [P, ET], F32, ctx)
                hi = sb("hi", [P, ET], F32, ctx)
                extra = sb("extra", [P, ET], F32, ctx)
                one = sb("one", [P, ET], F32, ctx)
                incl = sb("incl", [P, ET], F32, ctx)
                first = sb("first", [P, ET], F32, ctx)
                off = sb("off", [P, ET], F32, ctx)
                doff = sb("doff", [P, ET], F32, ctx)
                tno = sb("tno", [P, ET], F32, ctx)
                mask = sb("mask", [P, ET], F32, ctx)
                prod = sb("prod", [P, ET], F32, ctx)
                pair_no = sb("pair_no", [P, PG], F32, ctx)
                cnt = sb("cnt", [P, PG], F32, ctx)
                tix = sb("tix", [P, PG], F32, ctx)
                tix_i = sb("tix_i", [P, PG], I32, ctx)
                tfe_i = sb("tfe_i", [P, PG], I32, ctx)
                bno = sb("bno", [P, PG], F32, ctx)
                bst = sb("bst", [P, PG], F32, ctx)
                bcl_i = sb("bcl_i", [P, PG], I32, ctx)
                buckets = sb("buckets", [1, PG * P], I32, ctx)
                rows = [sb(f"rows{k}", [P, PG, P], dt, ctx) for k, dt in enumerate((I32, I32, F32))]
                rowf = sb("rowf", [P, 2, PG, P], F32, ctx)
                pt = [ps(f"pt{k}", ctx) for k in range(2)]
                loaded, x_loaded = sem("loaded"), sem("x_loaded")
                consts, vec = sem("consts"), sem("vec")
                pairs_known, rows_in, rows_ready = sem("pairs_known"), sem("rows_in"), sem("rows_ready")
                turned, taken, rows_out, rows_back = sem("turned"), sem("taken"), sem("rows_out"), sem("rows_back")

                with nc.Block() as block:
                    @block.sync
                    def _(sp):
                        sp.dma_start(lo_i[:, :, :], a["tile_ends"].rearrange("(o k) t -> o k t", o=1).to_broadcast([P, 2, ET])).then_inc(loaded, 16)
                        sp.dma_start(x[:, :, :], a["x"]).then_inc(x_loaded, 16)
                        sp.wait_ge(pairs_known, 1)
                        with nc.allow_non_contiguous_dma(reason="two columns of 13 values a partition"):
                            sp.dma_start(row_scratch[0].rearrange("(g p) -> p g", p=P), tfe_i[:, :]).then_inc(rows_out, 16)
                            sp.dma_start(row_scratch[1].rearrange("(g p) -> p g", p=P), bcl_i[:, :]).then_inc(rows_out, 16)
                        sp.wait_ge(rows_out, 32)
                        sp.dma_start(tile_row[:, :], row_scratch[0:1, :]).then_inc(rows_back, 16)
                        sp.dma_start(buckets[:, :], row_scratch[1:2, :]).then_inc(rows_back, 16)
                        sp.wait_ge(rows_back, 32)
                        sp.wait_ge(x_loaded, 16)

                    @block.gpsimd
                    def _(g):
                        g.memset(ident[:, :], 0.0).then_inc(consts, 1)
                        g.memset(earlier[:, :], 1.0).then_inc(consts, 1)
                        g.iota(iota[:, :], [[1, P]], 0, 0, allow_small_or_imprecise_dtypes=True).then_inc(consts, 1)
                        g.iota(pair_no[:, :], [[P, PG]], 0, 1, allow_small_or_imprecise_dtypes=True).then_inc(consts, 1)
                        g.iota(tno[:, :], [[1, ET]], 0, 0, allow_small_or_imprecise_dtypes=True).then_inc(consts, 1)
                        g.iota(trash_row[:, :], [[0, 1]], NP, 1, allow_small_or_imprecise_dtypes=True).then_inc(consts, 1)
                        g.wait_ge(consts, 6)
                        g.affine_select(out=ident[:, :], in_=ident[:, :], compare_op=ALU.not_equal, fill=1.0, base=0,
                                        pattern=[[-1, P]], channel_multiplier=1).then_inc(consts, 1)
                        g.affine_select(out=earlier[:, :], in_=earlier[:, :], compare_op=ALU.is_gt, fill=0.0, base=0,
                                        pattern=[[-1, P]], channel_multiplier=1).then_inc(consts, 1)
                        g.wait_ge(pairs_known, 1)
                        for k, name in enumerate(("src", "dst", "edge_weight")):
                            for gr in range(PG):
                                g.indirect_dma_start(rows[k][:, gr, :], None, a[name],
                                                     bass.IndirectOffsetOnAxis(ap=tix_i[:, gr:gr + 1], axis=0)).then_inc(rows_in, 16)
                        g.wait_ge(rows_in, 16 * 3 * PG)

                    @block.vector
                    def _(v):
                        n = [0]

                        def then(ins):
                            n[0] += 1
                            ins.then_inc(vec, 1)
                            v.wait_ge(vec, n[0])

                        v.memset(one[:, :], 1.0)
                        v.memset(eps[:, :], EPS)
                        v.memset(deg[:, :, :], 0.0)
                        v.memset(h[:, :, D:D + 1], 1.0)
                        v.wait_ge(loaded, 16)
                        then(v.tensor_scalar(lo_i[:, :, :], lo_i[:, :, :], 7, None, ALU.arith_shift_right))
                        v.tensor_copy(lo[:, :], lo_i[:, 0, :])
                        then(v.tensor_copy(hi[:, :], lo_i[:, 1, :]))
                        then(v.tensor_tensor(extra[:, :], hi[:, :], lo[:, :], ALU.subtract))
                        then(v.tensor_tensor_scan(incl[:, :], one[:, :], extra[:, :], 0.0, ALU.mult, ALU.add))
                        then(v.tensor_tensor(first[:, :], incl[:, :], extra[:, :], ALU.subtract))
                        v.wait_ge(consts, 8)
                        then(v.tensor_tensor(first[:, :], first[:, :], tno[:, :], ALU.add))
                        then(v.tensor_tensor(off[:, :], lo[:, :], first[:, :], ALU.subtract))
                        v.tensor_copy(doff[:, 0:1], off[:, 0:1])
                        then(v.tensor_tensor(doff[:, 1:ET], off[:, 1:ET], off[:, 0:ET - 1], ALU.subtract))
                        for gr in range(PG):
                            then(v.tensor_scalar(mask[:, :], first[:, :], pair_no[:, gr:gr + 1], None, ALU.is_le, ALU.add,
                                                 accum_out=cnt[:, gr:gr + 1]))
                            then(v.tensor_tensor_reduce(prod[:, :], mask[:, :], doff[:, :], 1.0, 0.0, ALU.mult, ALU.add,
                                                        bno[:, gr:gr + 1]))
                        v.tensor_scalar(tix_i[:, :], cnt[:, :], -1.0, None, ALU.add)
                        then(v.tensor_scalar(tix[:, :], cnt[:, :], -1.0, None, ALU.add))
                        v.tensor_scalar(tfe_i[:, :], tix[:, :], float(P), None, ALU.mult)
                        then(v.tensor_tensor(bno[:, :], bno[:, :], pair_no[:, :], ALU.add))
                        v.tensor_scalar(bst[:, :], bno[:, :], float(P), None, ALU.mult)
                        v.tensor_scalar(bcl_i[:, :], bno[:, :], float(BUCKETS - 1), None, ALU.min).then_inc(pairs_known, 1)
                        v.wait_ge(rows_in, 16 * 3 * PG)
                        v.tensor_copy(rowf[:, 0, :, :], rows[0][:, :, :])
                        for gr in range(PG):
                            last = v.tensor_scalar(rowf[:, 1, gr, :], rows[1][:, gr, :], bst[:, gr:gr + 1], None, ALU.subtract)
                        last.then_inc(rows_ready, 1)
                        v.wait_ge(rows_back, 32)
                        four = buckets[:, :].rearrange("o (n q) -> o q n", q=H)
                        for q in range(1, H):
                            last = v.tensor_scalar(four[:, q, :], four[:, q, :], 8 * q, None, ALU.logical_shift_left)
                        then(last)
                        then(v.tensor_tensor(bucket_row[:, :], four[:, 0, :], four[:, 1, :], ALU.bitwise_or))
                        then(v.tensor_tensor(bucket_row[:, :], bucket_row[:, :], four[:, 2, :], ALU.bitwise_or))
                        v.tensor_tensor(bucket_row[:, :], bucket_row[:, :], four[:, 3, :], ALU.bitwise_or)

                    @block.tensor
                    def _(pe):
                        pe.wait_ge(consts, 8)
                        pe.wait_ge(rows_ready, 1)
                        for gr in range(PG):
                            if gr >= 2:
                                pe.wait_ge(taken, gr - 1)
                            for k, r in enumerate((rowf[:, 0, gr, :], rowf[:, 1, gr, :], rows[2][:, gr, :])):
                                last = pe.transpose(pt[gr % 2][:, k * P:(k + 1) * P], r, ident[:, :])
                            last.then_inc(turned, 1)

                    @block.scalar
                    def _(s):
                        for gr in range(PG):
                            s.wait_ge(turned, gr + 1)
                            last = s.copy(edge_tab[:, gr * P:(gr + 1) * P, :].rearrange("p t k -> p k t"),
                                          pt[gr % 2][:, 0:3 * P].rearrange("p (k t) -> p k t", k=3))
                            last.then_inc(taken, 1)

        def buckets_of(eng, n):
            word = eng.value_load(bucket_row[0:1, bass.ds(n, 1)], min_val=0, max_val=(1 << 30) - 1)
            return [nc.s_assert_within(eng.snap((word >> (8 * q)) & 127), 0, BUCKETS - 1,
                                       skip_runtime_bounds_check_because="buckets are held to this range when the words are made") for q in range(H)]

        def stage_norm(name, to_table):
            stats_in, merged, std_in, scaled, normed, stored = (
                sem(f"{name}_{k}") for k in ("stats", "merged", "std", "scaled", "normed", "stored"))
            with nc.Block() as block:
                @block.vector
                def _(v):
                    with v.Fori(0, NCH) as c:
                        for k in range(CT):
                            v.bn_stats(stat[:, bass.ds(c * CT + k, 1), :].rearrange("p t s -> p (t s)"),
                                       x[:, bass.ds(c * CT + k, 1), :].rearrange("p t d -> p (t d)")).then_inc(stats_in, 1)
                    v.wait_ge(stats_in, NT)
                    v.tensor_tensor(mv[:, :, 0], stat[:, :, 1], stat[:, :, 4], ALU.add).then_inc(merged, 1)
                    v.tensor_tensor(nmr[:, :], stat[:, :, 1], stat[:, :, 4], ALU.subtract).then_inc(merged, 1)
                    v.tensor_tensor(mv[:, :, 1], stat[:, :, 2], stat[:, :, 5], ALU.add).then_inc(merged, 1)
                    v.wait_ge(merged, 3)
                    v.tensor_scalar(mv[:, :, 1], mv[:, :, 1], 1.0 / D, None, ALU.mult).then_inc(merged, 1)
                    v.tensor_tensor(nmr[:, :], nmr[:, :], nmr[:, :], ALU.mult).then_inc(merged, 1)
                    v.wait_ge(merged, 5)
                    v.tensor_scalar(mv[:, :, 0], mv[:, :, 0], 0.5, None, ALU.mult).then_inc(merged, 1)
                    v.scalar_tensor_tensor(out=mv[:, :, 1], in0=nmr[:, :], scalar=0.25, in1=mv[:, :, 1],
                                           op0=ALU.mult, op1=ALU.add).then_inc(merged, 1)
                    v.wait_ge(std_in, 1)
                    v.reciprocal(rstd[:, :], rstd[:, :]).then_inc(scaled, 1)
                    v.wait_ge(scaled, 1)
                    v.scalar_tensor_tensor(out=nmr[:, :], in0=mv[:, :, 0], scalar=-1.0, in1=rstd[:, :],
                                           op0=ALU.mult, op1=ALU.mult).then_inc(scaled, 1)

                @block.scalar
                def _(s):
                    s.wait_ge(merged, 7)
                    s.activation(rstd[:, :], mv[:, :, 1], ACT.Sqrt, bias=eps[:, :]).then_inc(std_in, 1)
                    s.wait_ge(scaled, 2)
                    with s.Fori(0, NCH) as c:
                        for k in range(CT):
                            t = c * CT + k
                            s.activation(h[:, bass.ds(t, 1), 0:D], x[:, bass.ds(t, 1), :], ACT.Relu,
                                         bias=nmr[:, bass.ds(t, 1)], scale=rstd[:, bass.ds(t, 1)]).then_inc(normed, 1)

                @block.sync
                def _(sp):
                    if to_table:
                        sp.wait_ge(normed, NT)
                        sp.dma_start(tiles(table), h[:, :, 0:D]).then_inc(stored, 16)
                        sp.wait_ge(stored, 16)

        def stage_gru_edges(sum_dst):
            with ExitStack() as ctx:
                cur = sb("g_cur", [P, NB, H, 4], F32, ctx)
                gidx = sb("g_gidx", [P, NB, H], I32, ctx)
                sidx = sb("g_sidx", [P, NB, H], I32, ctx)
                dup = sb("g_dup", [P, H], F32, ctx)
                away = sb("g_away", [P, H], F32, ctx)
                G = sb("g_G", [P, U, D], F32, ctx)
                oh = sb("g_oh", [P, NB, H, P], F32, ctx)
                ohw = sb("g_ohw", [P, NB, H, P], F32, ctx)
                same = sb("g_same", [P, 2, H, P], F32, ctx)
                junk = sb("g_junk", [P, H, P], F32, ctx)
                mix = sb("g_mix", [P, 2, H, P], F32, ctx)
                rows = sb("g_rows", [P, H, D + 1], F32, ctx)
                zero = sb("g_zero", [P, (NP + P) * (D + 1) // P], F32, ctx)
                ps_src = ps("g_ps_src", ctx)
                ps_sum = [ps(f"g_ps_sum{k}", ctx) for k in range(2)]
                ps_deg = [ps(f"g_ps_deg{k}", ctx) for k in range(2)]
                ps_mix = ps("g_ps_mix", ctx)
                ps_rows = [ps(f"g_ps_rows{k}", ctx) for k in range(2)]
                zeroed, cur_ready, gidx_ready = sem("g_zeroed"), sem("g_cur_ready"), sem("g_gidx_ready")
                oh_ready, ohw_ready = sem("g_oh_ready"), sem("g_ohw_ready")
                srcrow_ready, same_ready = sem("g_srcrow_ready"), sem("g_same_ready")
                mix_made, mix_ready = sem("g_mix_made"), sem("g_mix_ready")
                dup_step, sidx_ready = sem("g_dup_step"), sem("g_sidx_ready")
                rows_made, row_ready = sem("g_rows_made"), sem("g_row_ready")
                gathered = [sem(f"g_gathered{b}") for b in range(NB)]
                src_added = [sem(f"g_src_added{q}") for q in range(SUMS)]
                summed, dst_added, deg_added = sem("g_summed"), sem("g_dst_added"), sem("g_deg_added")

                with nc.Block() as block:
                    @block.gpsimd
                    def _(g):
                        g.memset(zero[:, :], 0.0).then_inc(zeroed, 1)
                        g.wait_ge(zeroed, 1)
                        for q in range(SUMS):
                            g.dma_start(srcsum[q].rearrange("(p r) c -> p (r c)", p=P), zero[:, :]).then_inc(src_added[q], 16)

                        def gather(i, b):
                            g.wait_ge(gidx_ready, NB * i + b + 1)
                            g.nop(nofuse=True)
                            for q in range(H):
                                g.indirect_dma_start(G[:, H * b + q, :], None, table,
                                                     bass.IndirectOffsetOnAxis(ap=gidx[:, b, q:q + 1], axis=0)).then_inc(gathered[b], 16)

                        def scatter(i, b):
                            n = NB * i + b
                            g.wait_ge(sidx_ready, n + 1)
                            for q in range(H):
                                g.wait_ge(row_ready, H * n + q + 1 + 2 * H)
                                g.nop(nofuse=True)
                                g.indirect_dma_start(srcsum[q], bass.IndirectOffsetOnAxis(ap=sidx[:, b, q:q + 1], axis=0),
                                                     rows[:, q, :], None, compute_op=ALU.add).then_inc(src_added[q], 16)

                        over_quads(g, (gather, 0), (scatter, 2))
                        for q in range(SUMS):
                            g.wait_ge(src_added[q], 16 * (NB * NI + 1))

                    @block.vector
                    def _(v):
                        v.memset(sum_dst[:, :, :], 0.0).then_inc(dst_added, 2 * H)
                        v.memset(cur[:, :, :, 3:4], 1.0).then_inc(deg_added, 2 * H)
                        v.wait_ge(dst_added, 2 * H)
                        v.wait_ge(deg_added, 2 * H)

                        def one_hot(i, b):
                            n = NB * i + b
                            v.wait_ge(summed, n + 1)
                            v.tensor_copy(cur[:, b, :, 0:3], edge_tab[:, bass.ds(i * U + H * b, H), :]).then_inc(cur_ready, 1)
                            v.wait_ge(cur_ready, n + 1)
                            v.tensor_copy(gidx[:, b, :], cur[:, b, :, 0]).then_inc(gidx_ready, 1)
                            for q in range(H):
                                last = v.tensor_scalar(oh[:, b, q, :], iota[:, :], cur[:, b, q, 1:2], None, ALU.is_equal)
                            last.then_inc(oh_ready, 1)

                        def same_src(i, b):
                            n = NB * i + b
                            v.wait_ge(srcrow_ready, n + 1)
                            for q in range(H):
                                last = v.tensor_scalar(same[:, b % 2, q, :], ps_src[:, q * P:(q + 1) * P], cur[:, b, q, 0:1], None,
                                                       ALU.is_equal)
                            last.then_inc(same_ready, 1)
                            v.tensor_scalar(away[:, :], cur[:, b, :, 0], -1.0, trash_row[:, :], ALU.mult, ALU.add).then_inc(dup_step, 1)
                            v.wait_ge(same_ready, n + 1)
                            for q in range(H):
                                last = v.tensor_tensor_reduce(junk[:, q, :], same[:, b % 2, q, :], earlier[:, :], 1.0, 0.0,
                                                              ALU.mult, ALU.add, dup[:, q:q + 1])
                            last.then_inc(dup_step, 1)
                            v.wait_ge(dup_step, 3 * n + 2)
                            v.scalar_tensor_tensor(out=away[:, :], in0=dup[:, :], scalar=0.5, in1=away[:, :],
                                                   op0=ALU.is_gt, op1=ALU.mult).then_inc(dup_step, 1)
                            v.wait_ge(dup_step, 3 * n + 3)
                            v.wait_ge(row_ready, H * n + H)
                            v.tensor_tensor(sidx[:, b, :], away[:, :], cur[:, b, :, 0], ALU.add).then_inc(sidx_ready, 1)

                        def add_up(i, b):
                            n = NB * i + b
                            bucket = buckets_of(v, n)
                            v.wait_ge(summed, n + 1 + NB)
                            for q in range(H):
                                at = bass.ds(bucket[q], 1)
                                v.wait_ge(dst_added, H * n + q + 2 * H)
                                v.tensor_tensor(sum_dst[:, at, :], sum_dst[:, at, :],
                                                ps_sum[b % 2][:, q * P:(q + 1) * P].rearrange("p (o d) -> p o d", o=1),
                                                ALU.add).then_inc(dst_added, 1)
                                v.wait_ge(deg_added, H * n + q + 2 * H)
                                v.tensor_tensor(deg[:, at, :], deg[:, at, :],
                                                ps_deg[b % 2][:, 2 * q:2 * q + 2].rearrange("p (o d) -> p o d", o=1),
                                                ALU.add).then_inc(deg_added, 1)

                        over_quads(v, (one_hot, 0), (same_src, 1), (add_up, 3))

                    @block.scalar
                    def _(s):
                        s.sem_inc(row_ready, 2 * H)
                        s.sem_inc(mix_ready, 1)

                        def weigh(i, b):
                            s.wait_ge(oh_ready, NB * i + b + 1)
                            for q in range(H):
                                last = s.activation(ohw[:, b, q, :], oh[:, b, q, :], ACT.Copy, scale=cur[:, b, q, 2:3])
                            last.then_inc(ohw_ready, 1)

                        def take_mix(i, b):
                            s.wait_ge(mix_made, NB * i + b + 1)
                            s.copy(mix[:, b % 2, :, :].rearrange("p q d -> p (q d)"), ps_mix[:, :]).then_inc(mix_ready, 1)

                        def take_rows(i, b):
                            n = NB * i + b
                            for q in range(H):
                                s.wait_ge(rows_made, H * n + q // 2 * 2 + 2)
                                s.wait_ge(src_added[q], 16 * (n + 1))
                                s.copy(rows[:, q, :], ps_rows[q // 2][:, (q % 2) * 256:(q % 2) * 256 + D + 1]).then_inc(row_ready, 1)

                        over_quads(s, (weigh, 0), (take_mix, 1), (take_rows, 2))

                    @block.tensor
                    def _(pe):
                        pe.sem_inc(summed, NB)

                        def turn_src(i, b):
                            n = NB * i + b
                            pe.wait_ge(cur_ready, n + 1)
                            if not (isinstance(n, int) and n == 0):
                                pe.wait_ge(same_ready, n)
                            for q in range(H):
                                last = pe.transpose(ps_src[:, q * P:(q + 1) * P], cur[:, b, q, 0:1].to_broadcast([P, P]), ident[:, :])
                            last.then_inc(srcrow_ready, 1)

                        def make_mix(i, b):
                            n = NB * i + b
                            pe.wait_ge(mix_ready, n + 1)
                            pe.wait_ge(ohw_ready, n + 1)
                            pe.wait_ge(same_ready, n + 1)
                            for q in range(H):
                                last = pe.matmul(ps_mix[:, q * P:(q + 1) * P], ohw[:, b, q, :], same[:, b % 2, q, :], start=True, stop=True)
                            last.then_inc(mix_made, 1)

                        def make_rows(i, b):
                            n = NB * i + b
                            bucket = buckets_of(pe, n)
                            pe.wait_ge(mix_ready, n + 2)
                            for q in range(H):
                                pe.wait_ge(row_ready, H * n + q // 2 * 2 + 2 + H)
                                pe.matmul(ps_rows[q // 2][:, (q % 2) * 256:(q % 2) * 256 + D + 1], mix[:, b % 2, q, :],
                                          h[:, bass.ds(bucket[q], 1), :].rearrange("p o d -> p (o d)"), start=True, stop=True).then_inc(rows_made, 1)

                        def make_sums(i, b):
                            n = NB * i + b
                            pe.wait_ge(deg_added, H * n + H)
                            pe.wait_ge(dst_added, H * n + H)
                            pe.wait_ge(gathered[b], 16 * H * (i + 1))
                            for q in range(H):
                                pe.matmul(ps_deg[b % 2][:, 2 * q:2 * q + 2], oh[:, b, q, :], cur[:, b, q, 2:4], start=True, stop=True)
                                last = pe.matmul(ps_sum[b % 2][:, q * P:(q + 1) * P], ohw[:, b, q, :], G[:, H * b + q, :], start=True, stop=True)
                            last.then_inc(summed, 1)

                        over_quads(pe, (turn_src, 0), (make_mix, 1), (make_rows, 2), (make_sums, 2))

        def chunk(c):
            return bass.ds(c * CT, CT)

        def spread(ap):
            return ap.unsqueeze(2).to_broadcast([P, CT, D])

        def across(ap):
            return ap.unsqueeze(1).to_broadcast([P, CT, D])

        def by_tile(ap):
            return ap.rearrange("p (t d) -> p t d", t=CT)

        def loader(sp, loaded, pairs):
            for dst, src in pairs:
                sp.dma_start(dst, src).then_inc(loaded, 16)

        def stage_gru_nodes(sum_dst):
            with ExitStack() as ctx:
                w12 = sb("u_w12", [P, 2, D], F32, ctx)
                wih = sb("u_wih", [P, 2, 3 * D], F32, ctx)
                whh = sb("u_whh", [P, 3 * D], F32, ctx)
                bias = sb("u_bias", [P, 2, 3], F32, ctx)
                brz = sb("u_brz", [P, 2], F32, ctx)
                wf = sb("u_wf", [P, 2, 3 * D], F32, ctx)
                inv1 = sb("u_inv1", [P, NT], F32, ctx)
                has1 = sb("u_has1", [P, NT], F32, ctx)
                inv2 = sb("u_inv2", [P, CT], F32, ctx)
                has2 = sb("u_has2", [P, CT], F32, ctx)
                parts = sb("u_parts", [P, SUMS, CT, D + 1], F32, ctx)
                tot = sb("u_tot", [P, 2, CT, D + 1], F32, ctx)
                nodes = sb("u_nodes", [P, 3, CT, D], F32, ctx)
                fm = sb("u_fm", [P, 3, CH], F32, ctx)
                rz = sb("u_rz", [P, 2, CH], F32, ctx)
                cand = sb("u_cand", [P, CH], F32, ctx)
                upd = sb("u_upd", [P, CH], F32, ctx)
                ps_turn = [ps(f"u_ps_turn{k}", ctx) for k in range(3)]
                ps_rz = [ps(f"u_ps_rz{k}", ctx) for k in range(2)]
                ps_in, ps_hn, ps_back = ps("u_ps_in", ctx), ps("u_ps_hn", ctx), ps("u_ps_back", ctx)
                loaded, folded, ready = sem("u_loaded"), sem("u_folded"), sem("u_ready")
                parts_in = sem("u_parts_in")
                T = Steps(sem("u_tensor_steps"), "turned gates turned_back")
                V = Steps(sem("u_vector_steps"), "sum01 sum23 total has less safe recip inv mean_dst mean_src h hn in diff gated out added")
                S = Steps(sem("u_scalar_steps"), "fm r z cand")

                with nc.Block() as block:
                    @block.sync
                    def _(sp):
                        loader(sp, loaded, [(w12[:, :, :], a["l0_w12"]), (wih[:, :, :], a["l0_wih"]), (whh[:, :], a["l0_whh"]),
                                            (bias[:, :, :], a["l0_bias"])])
                        with sp.Fori(0, NCH) as c:
                            sp.wait_ge(*V.before("sum23", c))
                            for q in range(SUMS):
                                sp.dma_start(parts[:, q, :, :], tiles(srcsum[q][0:NP])[:, chunk(c), :]).then_inc(parts_in, 16)

                    @block.tensor
                    def _(pe):
                        T.start(pe)
                        pe.wait_ge(loaded, 64)
                        for k in range(2):
                            last = pe.matmul(ps_rz[k][:, 0:3 * D], w12[:, k, :], wih[:, k, :], start=True, stop=True)
                        last.then_inc(folded, 1)
                        pe.wait_ge(ready, 2)
                        with pe.Fori(0, NCH) as c:
                            pe.wait_ge(*V.now("h", c))
                            pe.wait_ge(*S.before("fm", c))
                            for k in range(3):
                                for t in range(CT):
                                    last = pe.transpose(ps_turn[k][:, t * P:(t + 1) * P], nodes[:, k, t, :], ident[:, :])
                            last.then_inc(T.sem, 1)
                            pe.wait_ge(*S.now("fm", c))
                            pe.wait_ge(*V.before("in", c))
                            for g in range(2):
                                for k, w in enumerate((wf[:, 0, :], wf[:, 1, :], whh[:, :])):
                                    pe.matmul(ps_rz[g][:, :], w[:, g * D:(g + 1) * D], fm[:, k, :], start=k == 0, stop=k == 2)
                            for k in range(2):
                                pe.matmul(ps_in[:, :], wf[:, k, 2 * D:3 * D], fm[:, k, :], start=k == 0, stop=k == 1)
                            pe.matmul(ps_hn[:, :], whh[:, 2 * D:3 * D], fm[:, 2, :], start=True, stop=True).then_inc(T.sem, 1)
                            pe.wait_ge(*V.now("out", c))
                            for t in range(CT):
                                last = pe.transpose(ps_back[:, t * P:(t + 1) * P], upd[:, t * P:(t + 1) * P], ident[:, :])
                            last.then_inc(T.sem, 1)

                    @block.vector
                    def _(v):
                        V.start(v)
                        v.tensor_scalar(has1[:, :], deg[:, :, 0], 0.0, None, ALU.is_gt).then_inc(ready, 1)
                        v.wait_ge(loaded, 64)
                        v.tensor_tensor(brz[:, :], bias[:, 0, 0:2], bias[:, 1, 0:2], ALU.add)
                        v.wait_ge(folded, 1)
                        v.tensor_copy(wf[:, 0, :], ps_rz[0][:, 0:3 * D])
                        v.tensor_copy(wf[:, 1, :], ps_rz[1][:, 0:3 * D]).then_inc(ready, 1)
                        v.wait_ge(ready, 2)
                        v.scalar_tensor_tensor(out=inv1[:, :], in0=deg[:, :, 0], scalar=-1.0, in1=has1[:, :],
                                               op0=ALU.add, op1=ALU.mult).then_inc(ready, 1)
                        v.wait_ge(ready, 3)
                        v.tensor_scalar(inv1[:, :], inv1[:, :], 1.0, None, ALU.add).then_inc(ready, 1)
                        v.wait_ge(ready, 4)
                        v.reciprocal(inv1[:, :], inv1[:, :]).then_inc(ready, 1)
                        v.wait_ge(ready, 5)
                        v.tensor_tensor(inv1[:, :], inv1[:, :], has1[:, :], ALU.mult).then_inc(ready, 1)
                        v.wait_ge(ready, 6)
                        with v.Fori(0, NCH) as c:
                            v.wait_ge(parts_in, 16 * SUMS * (c + 1))
                            v.tensor_tensor(tot[:, 0, :, :], parts[:, 0, :, :], parts[:, 1, :, :], ALU.add).then_inc(V.sem, 1)
                            v.tensor_tensor(tot[:, 1, :, :], parts[:, 2, :, :], parts[:, 3, :, :], ALU.add).then_inc(V.sem, 1)
                            v.wait_ge(*V.now("sum23", c))
                            v.tensor_tensor(tot[:, 0, :, :], tot[:, 0, :, :], tot[:, 1, :, :], ALU.add).then_inc(V.sem, 1)
                            v.wait_ge(*V.now("total", c))
                            v.tensor_scalar(has2[:, :], tot[:, 0, :, D], 0.0, None, ALU.is_gt).then_inc(V.sem, 1)
                            v.wait_ge(*V.now("has", c))
                            v.scalar_tensor_tensor(out=inv2[:, :], in0=tot[:, 0, :, D], scalar=-1.0, in1=has2[:, :],
                                                   op0=ALU.add, op1=ALU.mult).then_inc(V.sem, 1)
                            v.wait_ge(*V.now("less", c))
                            v.tensor_scalar(inv2[:, :], inv2[:, :], 1.0, None, ALU.add).then_inc(V.sem, 1)
                            v.wait_ge(*V.now("safe", c))
                            v.reciprocal(inv2[:, :], inv2[:, :]).then_inc(V.sem, 1)
                            v.wait_ge(*V.now("recip", c))
                            v.tensor_tensor(inv2[:, :], inv2[:, :], has2[:, :], ALU.mult).then_inc(V.sem, 1)
                            v.wait_ge(*T.before("turned", c))
                            v.tensor_tensor(nodes[:, 0, :, :], sum_dst[:, chunk(c), :], spread(inv1[:, chunk(c)]), ALU.mult).then_inc(V.sem, 1)
                            v.wait_ge(*V.now("inv", c))
                            v.tensor_tensor(nodes[:, 1, :, :], tot[:, 0, :, 0:D], spread(inv2[:, :]), ALU.mult).then_inc(V.sem, 1)
                            v.tensor_copy(nodes[:, 2, :, :], h[:, chunk(c), 0:D]).then_inc(V.sem, 1)
                            v.wait_ge(*T.now("gates", c))
                            v.wait_ge(*S.now("r", c))
                            v.scalar_tensor_tensor(out=cand[:, :], in0=ps_hn[:, :], scalar=bias[:, 1, 2:3], in1=rz[:, 0, :],
                                                   op0=ALU.add, op1=ALU.mult).then_inc(V.sem, 1)
                            v.wait_ge(*V.now("hn", c))
                            v.tensor_tensor(cand[:, :], ps_in[:, :], cand[:, :], ALU.add).then_inc(V.sem, 1)
                            v.wait_ge(*S.now("cand", c))
                            v.wait_ge(*T.before("turned_back", c))
                            v.tensor_tensor(upd[:, :], fm[:, 2, :], cand[:, :], ALU.subtract).then_inc(V.sem, 1)
                            v.wait_ge(*V.now("diff", c))
                            v.tensor_tensor(upd[:, :], rz[:, 1, :], upd[:, :], ALU.mult).then_inc(V.sem, 1)
                            v.wait_ge(*V.now("gated", c))
                            v.tensor_tensor(upd[:, :], upd[:, :], cand[:, :], ALU.add).then_inc(V.sem, 1)
                            v.wait_ge(*T.now("turned_back", c))
                            v.tensor_tensor(x[:, chunk(c), :], x[:, chunk(c), :], by_tile(ps_back[:, :]), ALU.add).then_inc(V.sem, 1)

                    @block.scalar
                    def _(s):
                        S.start(s)
                        s.wait_ge(ready, 2)
                        with s.Fori(0, NCH) as c:
                            s.wait_ge(*T.now("turned", c))
                            s.wait_ge(*V.before("out", c))
                            for k in range(3):
                                last = s.copy(fm[:, k, :], ps_turn[k][:, :])
                            last.then_inc(S.sem, 1)
                            s.wait_ge(*T.now("gates", c))
                            for g in range(2):
                                s.activation(rz[:, g, :], ps_rz[g][:, :], ACT.Sigmoid, bias=brz[:, g:g + 1]).then_inc(S.sem, 1)
                            s.wait_ge(*V.now("in", c))
                            s.activation(cand[:, :], cand[:, :], ACT.Tanh, bias=bias[:, 0, 2:3]).then_inc(S.sem, 1)

        def stage_gcn_table(name, acc, w_name, dis, y=None, bn=None):
            with ExitStack() as ctx:
                w = sb(f"{name}_w", [P, D], F32, ctx)
                cur = sb(f"{name}_cur", [P, CT, D], F32, ctx)
                fm = sb(f"{name}_fm", [P, CH], F32, ctx)
                ps_turn, ps_out = ps(f"{name}_ps_turn", ctx), ps(f"{name}_ps_out", ctx)
                loaded, stored = sem(f"{name}_loaded"), sem(f"{name}_stored")
                T = Steps(sem(f"{name}_tensor_steps"), "turned product")
                V = Steps(sem(f"{name}_vector_steps"), "cur scaled")
                S = Steps(sem(f"{name}_scalar_steps"), "fm")
                with nc.Block() as block:
                    @block.sync
                    def _(sp):
                        sp.dma_start(w[:, :], a[w_name]).then_inc(loaded, 16)
                        with sp.Fori(0, NCH) as c:
                            sp.wait_ge(*V.now("scaled", c))
                            sp.dma_start(tiles(table)[:, chunk(c), :], acc[:, chunk(c), :]).then_inc(stored, 16)
                        sp.wait_ge(stored, 16 * NCH)

                    @block.tensor
                    def _(pe):
                        T.start(pe)
                        pe.wait_ge(loaded, 16)
                        with pe.Fori(0, NCH) as c:
                            pe.wait_ge(*V.now("cur", c))
                            pe.wait_ge(*S.before("fm", c))
                            for t in range(CT):
                                last = pe.transpose(ps_turn[:, t * P:(t + 1) * P], cur[:, t, :], ident[:, :])
                            last.then_inc(T.sem, 1)
                            pe.wait_ge(*S.now("fm", c))
                            pe.wait_ge(*V.before("scaled", c))
                            for t in range(CT):
                                last = pe.matmul(ps_out[:, t * P:(t + 1) * P], fm[:, t * P:(t + 1) * P], w[:, :], start=True, stop=True)
                            last.then_inc(T.sem, 1)

                    @block.vector
                    def _(v):
                        V.start(v)
                        with v.Fori(0, NCH) as c:
                            v.wait_ge(*T.before("turned", c))
                            v.tensor_copy(cur[:, :, :], h[:, chunk(c), 0:D]).then_inc(V.sem, 1)
                            v.wait_ge(*T.now("product", c))
                            v.tensor_tensor(acc[:, chunk(c), :], by_tile(ps_out[:, :]), spread(dis[:, chunk(c)]), ALU.mult).then_inc(V.sem, 1)

                    @block.scalar
                    def _(s):
                        S.start(s)
                        with s.Fori(0, NCH) as c:
                            s.wait_ge(*T.now("turned", c))
                            s.wait_ge(*T.before("product", c))
                            if y is None:
                                s.copy(fm[:, :], ps_turn[:, :]).then_inc(S.sem, 1)
                            else:
                                s.activation(fm[:, :], y[:, bass.ds(c * CH, CH)], ACT.Relu, scale=bn[:, 0:1], bias=bn[:, 1:2]).then_inc(S.sem, 1)

        def stage_sum_edges(name, acc):
            with ExitStack() as ctx:
                cur = sb(f"{name}_cur", [P, NB, H, 2], F32, ctx)
                gidx = sb(f"{name}_gidx", [P, NB, H], I32, ctx)
                G = sb(f"{name}_G", [P, U, D], F32, ctx)
                oh = sb(f"{name}_oh", [P, NB, H, P], F32, ctx)
                ps_sum = [ps(f"{name}_ps_sum{k}", ctx) for k in range(2)]
                cur_ready, gidx_ready, oh_ready = sem(f"{name}_cur_ready"), sem(f"{name}_gidx_ready"), sem(f"{name}_oh_ready")
                gathered = [sem(f"{name}_gathered{b}") for b in range(NB)]
                summed, added = sem(f"{name}_summed"), sem(f"{name}_added")
                with nc.Block() as block:
                    @block.gpsimd
                    def _(g):
                        def gather(i, b):
                            g.wait_ge(gidx_ready, NB * i + b + 1)
                            g.nop(nofuse=True)
                            for q in range(H):
                                g.indirect_dma_start(G[:, H * b + q, :], None, table,
                                                     bass.IndirectOffsetOnAxis(ap=gidx[:, b, q:q + 1], axis=0)).then_inc(gathered[b], 16)

                        over_quads(g, (gather, 0))

                    @block.vector
                    def _(v):
                        v.sem_inc(added, 2 * H)

                        def one_hot(i, b):
                            n = NB * i + b
                            v.wait_ge(summed, n + 1)
                            v.tensor_copy(cur[:, b, :, :], edge_tab[:, bass.ds(i * U + H * b, H), 0:2]).then_inc(cur_ready, 1)
                            v.wait_ge(cur_ready, n + 1)
                            v.tensor_copy(gidx[:, b, :], cur[:, b, :, 0]).then_inc(gidx_ready, 1)
                            for q in range(H):
                                last = v.tensor_scalar(oh[:, b, q, :], iota[:, :], cur[:, b, q, 1:2], None, ALU.is_equal)
                            last.then_inc(oh_ready, 1)

                        def add_up(i, b):
                            n = NB * i + b
                            bucket = buckets_of(v, n)
                            v.wait_ge(summed, n + 1 + NB)
                            for q in range(H):
                                at = bass.ds(bucket[q], 1)
                                v.wait_ge(added, H * n + q + 2 * H)
                                v.tensor_tensor(acc[:, at, :], acc[:, at, :],
                                                ps_sum[b % 2][:, q * P:(q + 1) * P].rearrange("p (o d) -> p o d", o=1),
                                                ALU.add).then_inc(added, 1)

                        over_quads(v, (one_hot, 0), (add_up, 2))

                    @block.tensor
                    def _(pe):
                        pe.sem_inc(summed, NB)

                        def make_sums(i, b):
                            n = NB * i + b
                            pe.wait_ge(oh_ready, n + 1)
                            pe.wait_ge(added, H * n + H)
                            pe.wait_ge(gathered[b], 16 * H * (i + 1))
                            for q in range(H):
                                last = pe.matmul(ps_sum[b % 2][:, q * P:(q + 1) * P], oh[:, b, q, :], G[:, H * b + q, :], start=True, stop=True)
                            last.then_inc(summed, 1)

                        over_quads(pe, (make_sums, 0))

        def stage_gcn_norm(name, acc, dis, y, bn, par_name):
            with ExitStack() as ctx:
                par = sb(f"{name}_par", [P, 3], F32, ctx)
                cur = sb(f"{name}_cur", [P, CT, D], F32, ctx)
                bst = sb(f"{name}_bst", [P, NCH, 6], F32, ctx)
                agg = sb(f"{name}_agg", [P, 2], F32, ctx)
                dev = sb(f"{name}_dev", [P, 2], F32, ctx)
                ps_turn = ps(f"{name}_ps_turn", ctx)
                loaded, seen, dev_ready = sem(f"{name}_loaded"), sem(f"{name}_seen"), sem(f"{name}_dev_ready")
                T = Steps(sem(f"{name}_tensor_steps"), "turned")
                V = Steps(sem(f"{name}_vector_steps"), "cur")
                S = Steps(sem(f"{name}_scalar_steps"), "y")
                with nc.Block() as block:
                    @block.sync
                    def _(sp):
                        sp.dma_start(par[:, :], a[par_name]).then_inc(loaded, 16)

                    @block.tensor
                    def _(pe):
                        T.start(pe)
                        with pe.Fori(0, NCH) as c:
                            pe.wait_ge(*V.now("cur", c))
                            pe.wait_ge(*S.before("y", c))
                            for t in range(CT):
                                last = pe.transpose(ps_turn[:, t * P:(t + 1) * P], cur[:, t, :], ident[:, :])
                            last.then_inc(T.sem, 1)

                    @block.vector
                    def _(v):
                        V.start(v)
                        with v.Fori(0, NCH) as c:
                            v.wait_ge(*T.before("turned", c))
                            v.tensor_tensor(cur[:, :, :], acc[:, chunk(c), :], spread(dis[:, chunk(c)]), ALU.mult).then_inc(V.sem, 1)
                        for k in range(NCH):
                            v.wait_ge(*S.now("y", k))
                            v.bn_stats(bst[:, k, :], y[:, k * CH:min((k + 1) * CH, N)]).then_inc(seen, 1)
                        v.wait_ge(seen, NCH)
                        v.bn_aggr(agg[:, :], bst[:, :, :].rearrange("p k s -> p (k s)")).then_inc(seen, 1)
                        v.wait_ge(dev_ready, 1)
                        v.reciprocal(dev[:, 1:2], dev[:, 0:1]).then_inc(seen, 1)
                        v.wait_ge(seen, NCH + 2)
                        v.tensor_tensor(bn[:, 0:1], dev[:, 1:2], par[:, 1:2], ALU.mult).then_inc(seen, 1)
                        v.wait_ge(seen, NCH + 3)
                        v.tensor_tensor(bn[:, 1:2], agg[:, 0:1], bn[:, 0:1], ALU.mult).then_inc(seen, 1)
                        v.wait_ge(seen, NCH + 4)
                        v.tensor_tensor(bn[:, 1:2], par[:, 2:3], bn[:, 1:2], ALU.subtract)

                    @block.scalar
                    def _(s):
                        S.start(s)
                        s.wait_ge(loaded, 16)
                        with s.Fori(0, NCH) as c:
                            s.wait_ge(*T.now("turned", c))
                            s.activation(y[:, bass.ds(c * CH, CH)], ps_turn[:, :], ACT.Identity, bias=par[:, 0:1]).then_inc(S.sem, 1)
                        s.wait_ge(seen, NCH + 1)
                        s.activation(dev[:, 0:1], agg[:, 1:2], ACT.Sqrt, bias=eps[:, :]).then_inc(dev_ready, 1)

        def stage_gcn_out(y, bn):
            with ExitStack() as ctx:
                z = sb("o_z", [P, CH], F32, ctx)
                ps_back = ps("o_ps_back", ctx)
                T = Steps(sem("o_tensor_steps"), "turned")
                V = Steps(sem("o_vector_steps"), "added")
                S = Steps(sem("o_scalar_steps"), "z")
                with nc.Block() as block:
                    @block.tensor
                    def _(pe):
                        T.start(pe)
                        with pe.Fori(0, NCH) as c:
                            pe.wait_ge(*S.now("z", c))
                            pe.wait_ge(*V.before("added", c))
                            for t in range(CT):
                                last = pe.transpose(ps_back[:, t * P:(t + 1) * P], z[:, t * P:(t + 1) * P], ident[:, :])
                            last.then_inc(T.sem, 1)

                    @block.vector
                    def _(v):
                        V.start(v)
                        with v.Fori(0, NCH) as c:
                            v.wait_ge(*T.now("turned", c))
                            v.tensor_tensor(x[:, chunk(c), :], x[:, chunk(c), :], by_tile(ps_back[:, :]), ALU.add).then_inc(V.sem, 1)

                    @block.scalar
                    def _(s):
                        S.start(s)
                        with s.Fori(0, NCH) as c:
                            s.wait_ge(*T.before("turned", c))
                            s.activation(z[:, :], y[:, bass.ds(c * CH, CH)], ACT.Identity, scale=bn[:, 0:1], bias=bn[:, 1:2]).then_inc(S.sem, 1)

        def stage_dis(dis):
            root, known = sem("root"), sem("known")
            with nc.Block() as block:
                @block.scalar
                def _(s):
                    s.wait_ge(known, 1)
                    s.activation(dis[:, :], dis[:, :], ACT.Sqrt).then_inc(root, 1)

                @block.vector
                def _(v):
                    v.tensor_scalar(dis[:, :], deg[:, :, 1], 1.0, None, ALU.add).then_inc(known, 1)
                    v.wait_ge(root, 1)
                    v.reciprocal(dis[:, :], dis[:, :])

        def stage_mp_tables(own):
            with ExitStack() as ctx:
                w = sb("m_w", [P, 2, 2 * D], F32, ctx)
                be1 = sb("m_be1", [P, 2 * D], F32, ctx)
                cur = sb("m_cur", [P, CT, D], F32, ctx)
                fm = sb("m_fm", [P, CH], F32, ctx)
                rows = sb("m_rows", [P, CT, 2 * D], F32, ctx)
                ps_turn = ps("m_ps_turn", ctx)
                ps_src = [ps(f"m_ps_src{k}", ctx) for k in range(2)]
                ps_dst = [ps(f"m_ps_dst{k}", ctx) for k in range(2)]
                loaded, stored, saved = sem("m_loaded"), sem("m_stored"), sem("m_saved")
                T = Steps(sem("m_tensor_steps"), "turned src dst")
                V = Steps(sem("m_vector_steps"), "cur own")
                S = Steps(sem("m_scalar_steps"), "fm rows")
                with nc.Block() as block:
                    @block.sync
                    def _(sp):
                        loader(sp, loaded, [(w[:, :, :], a["l2_we1n"]), (be1[:, :], a["l2_be1"].to_broadcast([P, 2 * D]))])
                        sp.dma_start(x_save, x[:, :, :]).then_inc(saved, 16)
                        sp.sem_inc(stored, 16)
                        with sp.Fori(0, NCH) as c:
                            sp.wait_ge(*S.now("rows", c))
                            sp.dma_start(tiles(table2)[:, chunk(c), :], rows[:, :, :]).then_inc(stored, 16)
                        sp.wait_ge(stored, 16 * (NCH + 1))
                        sp.wait_ge(saved, 16)

                    @block.tensor
                    def _(pe):
                        T.start(pe)
                        pe.wait_ge(loaded, 32)
                        with pe.Fori(0, NCH) as c:
                            pe.wait_ge(*V.now("cur", c))
                            pe.wait_ge(*S.before("fm", c))
                            for t in range(CT):
                                last = pe.transpose(ps_turn[:, t * P:(t + 1) * P], cur[:, t, :], ident[:, :])
                            last.then_inc(T.sem, 1)
                            pe.wait_ge(*S.now("fm", c))
                            pe.wait_ge(*S.before("rows", c))
                            pe.wait_ge(*V.before("own", c))
                            for k, out in enumerate((ps_src, ps_dst)):
                                for t in range(CT):
                                    last = pe.matmul(out[t // 2][:, t % 2 * 2 * D:(t % 2 + 1) * 2 * D], fm[:, t * P:(t + 1) * P],
                                                     w[:, k, :], start=True, stop=True)
                                last.then_inc(T.sem, 1)

                    @block.vector
                    def _(v):
                        V.start(v)
                        v.wait_ge(loaded, 32)
                        with v.Fori(0, NCH) as c:
                            v.wait_ge(*T.before("turned", c))
                            v.tensor_copy(cur[:, :, :], h[:, chunk(c), 0:D]).then_inc(V.sem, 1)
                            v.wait_ge(*T.now("dst", c))
                            for k in range(2):
                                last = v.tensor_tensor(own[:, bass.ds(c * CT + 2 * k, 2), :], ps_dst[k][:, :].rearrange("p (t d) -> p t d", t=2),
                                                       be1[:, :].unsqueeze(1).to_broadcast([P, 2, 2 * D]), ALU.add)
                            last.then_inc(V.sem, 1)

                    @block.scalar
                    def _(s):
                        S.start(s)
                        with s.Fori(0, NCH) as c:
                            s.wait_ge(*T.now("turned", c))
                            s.wait_ge(*T.before("dst", c))
                            s.copy(fm[:, :], ps_turn[:, :]).then_inc(S.sem, 1)
                            s.wait_ge(*T.now("src", c))
                            s.wait_ge(stored, 16 * (c + 1))
                            for k in range(2):
                                last = s.copy(rows[:, 2 * k:2 * k + 2, :].rearrange("p t d -> p (t d)"), ps_src[k][:, :])
                            last.then_inc(S.sem, 1)

        def stage_mp_edges(own, hid):
            with ExitStack() as ctx:
                w = sb("p_w", [DE2, 2 * D], F32, ctx)
                cur = sb("p_cur", [P, NB, H, 2], F32, ctx)
                gidx = sb("p_gidx", [P, NB, H], I32, ctx)
                G = x[:, 0:2 * U, :].rearrange("p (s k) d -> p s (k d)", k=2)
                oh = x[:, 2 * U:3 * U, :].rearrange("p (b q) d -> p b q d", q=H)
                ed = sb("p_ed", [DE2, 2, H * P], F32, ctx)
                ohT = sb("p_ohT", [P, 2, H, P], F32, ctx)
                ps_turn = ps("p_ps_turn", ctx)
                ps_pre = [ps(f"p_ps_pre{k}", ctx) for k in range(4)]
                ps_sum = [ps(f"p_ps_sum{k}", ctx) for k in range(2)]
                loaded = sem("p_loaded")
                cur_ready, gidx_ready, oh_ready = sem("p_cur_ready"), sem("p_gidx_ready"), sem("p_oh_ready")
                turned, ohT_ready, product = sem("p_turned"), sem("p_ohT_ready"), sem("p_product")
                total, hidden = sem("p_total"), sem("p_hidden")
                edges_in = [sem(f"p_edges_in{b}") for b in range(2)]
                gathered = [sem(f"p_gathered{b}") for b in range(NB)]
                summed, added = sem("p_summed"), sem("p_added")
                with nc.Block() as block:
                    @block.sync
                    def _(sp):
                        sp.dma_start(w[:, :], a["l2_we1e"]).then_inc(loaded, 16)
                        sp.wait_ge(loaded, 16)

                        def load(i, b):
                            n = NB * i + b
                            at = [sp.value_load(tile_row[0:1, bass.ds(i * U + H * b + q, 1)], min_val=0, max_val=(ET - 1) * P) for q in range(H)]
                            sp.wait_ge(product, n + 1)
                            sp.nop(nofuse=True)
                            for q in range(H):
                                sp.dma_start(ed[:, b % 2, q * P:(q + 1) * P], a["edge32"][:, bass.ds(at[q], P)]).then_inc(edges_in[b % 2], 16)

                        over_quads(sp, (load, 0))

                    @block.gpsimd
                    def _(g):
                        def gather(i, b):
                            g.wait_ge(gidx_ready, NB * i + b + 1)
                            g.nop(nofuse=True)
                            for q in range(H):
                                g.indirect_dma_start(G[:, H * b + q, :], None, table2,
                                                     bass.IndirectOffsetOnAxis(ap=gidx[:, b, q:q + 1], axis=0)).then_inc(gathered[b], 16)

                        over_quads(g, (gather, 0))

                    @block.vector
                    def _(v):
                        v.memset(hid[:, :, :], 0.0).then_inc(added, 2 * H)
                        v.sem_inc(total, 4)
                        v.wait_ge(added, 2 * H)

                        def one_hot(i, b):
                            n = NB * i + b
                            v.wait_ge(summed, n + 1)
                            v.tensor_copy(cur[:, b, :, :], edge_tab[:, bass.ds(i * U + H * b, H), 0:2]).then_inc(cur_ready, 1)
                            v.wait_ge(cur_ready, n + 1)
                            v.tensor_copy(gidx[:, b, :], cur[:, b, :, 0]).then_inc(gidx_ready, 1)
                            for q in range(H):
                                last = v.tensor_scalar(oh[:, b, q, :], iota[:, :], cur[:, b, q, 1:2], None, ALU.is_equal)
                            last.then_inc(oh_ready, 1)

                        def add_gathered(i, b):
                            v.wait_ge(product, NB * i + b + 3)
                            v.wait_ge(gathered[b], 16 * H * (i + 1))
                            for k in range(2):
                                two = G[:, H * b + 2 * k:H * b + 2 * k + 2, :].rearrange("p q d -> p (q d)")
                                v.tensor_tensor(two, two, ps_pre[b % 2 * 2 + k][:, :], ALU.add).then_inc(total, 1)

                        def add_up(i, b):
                            n = NB * i + b
                            bucket = buckets_of(v, n)
                            v.wait_ge(summed, n + 1 + NB)
                            for q in range(H):
                                at = bass.ds(bucket[q], 1)
                                v.wait_ge(added, H * n + q + 2 * H)
                                v.tensor_tensor(hid[:, at, :], hid[:, at, :],
                                                ps_sum[q // 2][:, q % 2 * 2 * D:(q % 2 + 1) * 2 * D].rearrange("p (o d) -> p o d", o=1),
                                                ALU.add).then_inc(added, 1)

                        over_quads(v, (one_hot, 0), (add_gathered, 2), (add_up, 3))

                    @block.scalar
                    def _(s):
                        s.sem_inc(ohT_ready, 1)

                        def take_ohT(i, b):
                            s.wait_ge(turned, NB * i + b + 1)
                            s.copy(ohT[:, b % 2, :, :].rearrange("p q d -> p (q d)"), ps_turn[:, :]).then_inc(ohT_ready, 1)

                        def silu(i, b):
                            for k in range(2):
                                s.wait_ge(total, 2 * (NB * i + b) + k + 1 + 4)
                                two = G[:, H * b + 2 * k:H * b + 2 * k + 2, :].rearrange("p q d -> p (q d)")
                                s.activation(two, two, ACT.Silu).then_inc(hidden, 1)

                        over_quads(s, (take_ohT, 0), (silu, 2))

                    @block.tensor
                    def _(pe):
                        pe.sem_inc(summed, NB)
                        pe.sem_inc(product, 2)
                        pe.wait_ge(loaded, 16)

                        def turn_oh(i, b):
                            n = NB * i + b
                            pe.wait_ge(oh_ready, n + 1)
                            pe.wait_ge(ohT_ready, n + 1)
                            for q in range(H):
                                last = pe.transpose(ps_turn[:, q * P:(q + 1) * P], oh[:, b, q, :], ident[:, :])
                            last.then_inc(turned, 1)

                        def products(i, b):
                            n = NB * i + b
                            bucket = buckets_of(pe, n)
                            pe.wait_ge(edges_in[b % 2], 16 * H * (NB // 2 * i + b // 2 + 1))
                            pe.wait_ge(ohT_ready, n + 2)
                            pe.wait_ge(total, 2 * n + 2)
                            for q in range(H):
                                out = ps_pre[b % 2 * 2 + q // 2][:, q % 2 * 2 * D:(q % 2 + 1) * 2 * D]
                                pe.matmul(out, ohT[:, b % 2, q, :], own[:, bass.ds(bucket[q], 1), :].rearrange("p o d -> p (o d)"), start=True, stop=False)
                                last = pe.matmul(out, ed[:, b % 2, q * P:(q + 1) * P], w[:, :], start=False, stop=True)
                            last.then_inc(product, 1)

                        def make_sums(i, b):
                            n = NB * i + b
                            pe.wait_ge(added, H * n + 2 * H)
                            for q in range(H):
                                pe.wait_ge(hidden, 2 * n + q // 2 + 1)
                                last = pe.matmul(ps_sum[q // 2][:, q % 2 * 2 * D:(q % 2 + 1) * 2 * D], oh[:, b, q, :], G[:, H * b + q, :],
                                                 start=True, stop=True)
                            last.then_inc(summed, 1)

                        over_quads(pe, (turn_oh, 0), (products, 1), (make_sums, 2))

        def norm_vector(v, V, S, c, tag, src, st, mv4, rs, sh):
            for t in range(CT):
                last = v.bn_stats(st[:, t, :], src[:, t, :])
            last.then_inc(V.sem, 1)
            v.wait_ge(*V.now(tag + "stats", c))
            v.tensor_tensor(mv4[:, 0, :], st[:, :, 1], st[:, :, 4], ALU.add).then_inc(V.sem, 1)
            v.tensor_tensor(sh[:, :], st[:, :, 1], st[:, :, 4], ALU.subtract).then_inc(V.sem, 1)
            v.tensor_tensor(mv4[:, 1, :], st[:, :, 2], st[:, :, 5], ALU.add).then_inc(V.sem, 1)
            v.wait_ge(*V.now(tag + "squares", c))
            v.tensor_scalar(mv4[:, 0, :], mv4[:, 0, :], 0.5, None, ALU.mult).then_inc(V.sem, 1)
            v.tensor_scalar(mv4[:, 1, :], mv4[:, 1, :], 1.0 / D, None, ALU.mult).then_inc(V.sem, 1)
            v.scalar_tensor_tensor(out=sh[:, :], in0=sh[:, :], scalar=0.25, in1=sh[:, :], op0=ALU.mult, op1=ALU.mult).then_inc(V.sem, 1)
            v.wait_ge(*V.now(tag + "gap2", c))
            v.tensor_tensor(mv4[:, 1, :], mv4[:, 1, :], sh[:, :], ALU.add).then_inc(V.sem, 1)
            v.wait_ge(*S.now(tag + "std", c))
            v.reciprocal(rs[:, :], rs[:, :]).then_inc(V.sem, 1)
            v.wait_ge(*V.now(tag + "rstd", c))
            v.scalar_tensor_tensor(out=sh[:, :], in0=mv4[:, 0, :], scalar=-1.0, in1=rs[:, :], op0=ALU.mult, op1=ALU.mult).then_inc(V.sem, 1)

        def norm_steps(tag):
            return " ".join(tag + k for k in "stats means gap squares mean spread gap2 var rstd shift".split())

        def stage_mp_nodes(hid):
            with ExitStack() as ctx:
                we2 = sb("q_we2", [P, 2, D], F32, ctx)
                be2 = sb("q_be2", [P, D], F32, ctx)
                wn1 = sb("q_wn1", [P, 2, 2 * D], F32, ctx)
                bn1 = sb("q_bn1", [P, 2], F32, ctx)
                wn2 = sb("q_wn2", [P, 2, D], F32, ctx)
                rowp = sb("q_rowp", [P, 5, D], F32, ctx)
                mask = sb("q_mask", [P, NT], F32, ctx)
                cur = sb("q_cur", [P, CT, 2 * D], F32, ctx)
                hidT = sb("q_hidT", [P, 2, CH], F32, ctx)
                agg = sb("q_agg", [P, CT, D], F32, ctx)
                nod = sb("q_nod", [P, 2, CT, D], F32, ctx)
                nodT = sb("q_nodT", [P, 2, CH], F32, ctx)
                act = sb("q_act", [P, 2, CH], F32, ctx)
                nf = sb("q_nf", [P, CT, D], F32, ctx)
                st = sb("q_st", [P, CT, 6], F32, ctx)
                mv4 = sb("q_mv4", [P, 2, CT], F32, ctx)
                rs = sb("q_rs", [P, CT], F32, ctx)
                sh = sb("q_sh", [P, CT], F32, ctx)
                ps_a = [ps(f"q_ps_a{k}", ctx) for k in range(2)]
                ps_agg = ps("q_ps_agg", ctx)
                ps_b = [ps(f"q_ps_b{k}", ctx) for k in range(2)]
                ps_c = [ps(f"q_ps_c{k}", ctx) for k in range(2)]
                ps_nf = ps("q_ps_nf", ctx)
                loaded, ready = sem("q_loaded"), sem("q_ready")
                T = Steps(sem("q_tensor_steps"), "hid_turned agg nod_turned hidden nf")
                V = Steps(sem("q_vector_steps"), "cur h agg " + norm_steps("m_") + " m_g m_b m_mask bias res " + norm_steps("n_") +
                          " n_g n_b n_mask added")
                S = Steps(sem("q_scalar_steps"), "hidT m_std m_normed nodT act n_std n_normed")
                with nc.Block() as block:
                    @block.sync
                    def _(sp):
                        loader(sp, loaded, [
                            (we2[:, :, :], a["l2_we2"]), (be2[:, :], a["l2_be2"].to_broadcast([P, D])), (wn1[:, :, :], a["l2_wn1"]),
                            (bn1[:, :], a["l2_bn1"]), (wn2[:, :, :], a["l2_wn2"]),
                            (rowp[:, :, :], a["l2_rows"].unsqueeze(0).to_broadcast([P, 5, D])), (mask[:, :], a["mask"]),
                            (x[:, :, :], x_save)])

                    @block.tensor
                    def _(pe):
                        T.start(pe)
                        pe.wait_ge(ready, 2)
                        with pe.Fori(0, NCH) as c:
                            pe.wait_ge(*V.now("cur", c))
                            pe.wait_ge(*S.before("hidT", c))
                            for t in range(CT):
                                for k in range(2):
                                    last = pe.transpose(ps_a[k][:, t * P:(t + 1) * P], cur[:, t, k * D:(k + 1) * D], ident[:, :])
                            last.then_inc(T.sem, 1)
                            pe.wait_ge(*S.now("hidT", c))
                            pe.wait_ge(*V.before("agg", c))
                            for t in range(CT):
                                for k in range(2):
                                    last = pe.matmul(ps_agg[:, t * P:(t + 1) * P], hidT[:, k, t * P:(t + 1) * P], we2[:, k, :], start=k == 0, stop=k == 1)
                            last.then_inc(T.sem, 1)
                            pe.wait_ge(*V.now("m_mask", c))
                            pe.wait_ge(*S.before("nodT", c))
                            for t in range(CT):
                                for k in range(2):
                                    last = pe.transpose(ps_b[k][:, t * P:(t + 1) * P], nod[:, k, t, :], ident[:, :])
                            last.then_inc(T.sem, 1)
                            pe.wait_ge(*S.now("nodT", c))
                            pe.wait_ge(*S.before("act", c))
                            for m in range(2):
                                for k in range(2):
                                    last = pe.matmul(ps_c[m][:, :], wn1[:, k, m * D:(m + 1) * D], nodT[:, k, :], start=k == 0, stop=k == 1)
                            last.then_inc(T.sem, 1)
                            pe.wait_ge(*S.now("act", c))
                            pe.wait_ge(*V.before("bias", c))
                            for t in range(CT):
                                for k in range(2):
                                    last = pe.matmul(ps_nf[:, t * P:(t + 1) * P], act[:, k, t * P:(t + 1) * P], wn2[:, k, :], start=k == 0, stop=k == 1)
                            last.then_inc(T.sem, 1)

                    @block.vector
                    def _(v):
                        V.start(v)
                        v.wait_ge(loaded, 8 * 16)
                        v.tensor_scalar(we2[:, :, :], we2[:, :, :], 1.0 / 16, None, ALU.mult).then_inc(ready, 1)
                        v.tensor_scalar(be2[:, :], be2[:, :], 1.0 / 16, None, ALU.mult).then_inc(ready, 1)
                        v.wait_ge(ready, 2)
                        with v.Fori(0, NCH) as c:
                            v.wait_ge(*T.before("hid_turned", c))
                            v.tensor_copy(cur[:, :, :], hid[:, chunk(c), :]).then_inc(V.sem, 1)
                            v.wait_ge(*T.before("nod_turned", c))
                            v.tensor_copy(nod[:, 0, :, :], h[:, chunk(c), 0:D]).then_inc(V.sem, 1)
                            v.wait_ge(*T.now("agg", c))
                            for t in range(CT):
                                last = v.scalar_tensor_tensor(out=agg[:, t, :], in0=be2[:, :], scalar=deg[:, bass.ds(c * CT + t, 1), 1],
                                                              in1=ps_agg[:, t * P:(t + 1) * P], op0=ALU.mult, op1=ALU.add)
                            last.then_inc(V.sem, 1)
                            v.wait_ge(*V.now("agg", c))
                            norm_vector(v, V, S, c, "m_", agg, st, mv4, rs, sh)
                            v.wait_ge(*S.now("m_normed", c))
                            v.tensor_tensor(nod[:, 1, :, :], nod[:, 1, :, :], across(rowp[:, 0, :]), ALU.mult).then_inc(V.sem, 1)
                            v.wait_ge(*V.now("m_g", c))
                            v.tensor_tensor(nod[:, 1, :, :], nod[:, 1, :, :], across(rowp[:, 1, :]), ALU.add).then_inc(V.sem, 1)
                            v.wait_ge(*V.now("m_b", c))
                            v.tensor_tensor(nod[:, 1, :, :], nod[:, 1, :, :], spread(mask[:, chunk(c)]), ALU.mult).then_inc(V.sem, 1)
                            v.wait_ge(*T.now("nf", c))
                            v.tensor_tensor(nf[:, :, :], by_tile(ps_nf[:, :]), across(rowp[:, 2, :]), ALU.add).then_inc(V.sem, 1)
                            v.wait_ge(*V.now("bias", c))
                            v.tensor_tensor(nf[:, :, :], nf[:, :, :], nod[:, 0, :, :], ALU.add).then_inc(V.sem, 1)
                            v.wait_ge(*V.now("res", c))
                            norm_vector(v, V, S, c, "n_", nf, st, mv4, rs, sh)
                            v.wait_ge(*S.now("n_normed", c))
                            v.tensor_tensor(nf[:, :, :], nf[:, :, :], across(rowp[:, 3, :]), ALU.mult).then_inc(V.sem, 1)
                            v.wait_ge(*V.now("n_g", c))
                            v.tensor_tensor(nf[:, :, :], nf[:, :, :], across(rowp[:, 4, :]), ALU.add).then_inc(V.sem, 1)
                            v.wait_ge(*V.now("n_b", c))
                            v.tensor_tensor(nf[:, :, :], nf[:, :, :], spread(mask[:, chunk(c)]), ALU.mult).then_inc(V.sem, 1)
                            v.wait_ge(*V.now("n_mask", c))
                            v.tensor_tensor(x[:, chunk(c), :], x[:, chunk(c), :], nf[:, :, :], ALU.add).then_inc(V.sem, 1)

                    @block.scalar
                    def _(s):
                        S.start(s)
                        s.wait_ge(loaded, 8 * 16)
                        with s.Fori(0, NCH) as c:
                            s.wait_ge(*T.now("hid_turned", c))
                            s.wait_ge(*T.before("agg", c))
                            for k in range(2):
                                last = s.copy(hidT[:, k, :], ps_a[k][:, :])
                            last.then_inc(S.sem, 1)
                            s.wait_ge(*V.now("m_var", c))
                            s.activation(rs[:, :], mv4[:, 1, :], ACT.Sqrt, bias=eps[:, :]).then_inc(S.sem, 1)
                            s.wait_ge(*V.now("m_shift", c))
                            for t in range(CT):
                                last = s.activation(nod[:, 1, t, :], agg[:, t, :], ACT.Identity, scale=rs[:, t:t + 1], bias=sh[:, t:t + 1])
                            last.then_inc(S.sem, 1)
                            s.wait_ge(*T.now("nod_turned", c))
                            for k in range(2):
                                last = s.copy(nodT[:, k, :], ps_b[k][:, :])
                            last.then_inc(S.sem, 1)
                            s.wait_ge(*T.now("hidden", c))
                            for k in range(2):
                                last = s.activation(act[:, k, :], ps_c[k][:, :], ACT.Silu, bias=bn1[:, k:k + 1])
                            last.then_inc(S.sem, 1)
                            s.wait_ge(*V.now("n_var", c))
                            s.activation(rs[:, :], mv4[:, 1, :], ACT.Sqrt, bias=eps[:, :]).then_inc(S.sem, 1)
                            s.wait_ge(*V.now("n_shift", c))
                            for t in range(CT):
                                last = s.activation(nf[:, t, :], nf[:, t, :], ACT.Identity, scale=rs[:, t:t + 1], bias=sh[:, t:t + 1])
                            last.then_inc(S.sem, 1)

        def stage_cutoff(fac):
            with ExitStack() as ctx:
                turns = sb("k_turns", [P, PG * P], F32, ctx)
                whole = sb("k_whole", [P, PG * P], I32, ctx)
                wholef = sb("k_wholef", [P, PG * P], F32, ctx)
                step, wave = sem("k_step"), sem("k_wave")
                with nc.Block() as block:
                    @block.vector
                    def _(v):
                        n = [0]

                        def then(ins):
                            n[0] += 1
                            ins.then_inc(step, 1)
                            v.wait_ge(step, n[0])

                        then(v.tensor_scalar(turns[:, :], edge_tab[:, :, 2], 0.5 / CUTOFF, 0.25, ALU.mult, ALU.add))
                        then(v.tensor_copy(whole[:, :], turns[:, :]))
                        then(v.tensor_copy(wholef[:, :], whole[:, :]))
                        then(v.tensor_tensor(turns[:, :], turns[:, :], wholef[:, :], ALU.subtract))
                        then(v.tensor_scalar(wholef[:, :], turns[:, :], 0.5, None, ALU.is_gt))
                        then(v.tensor_scalar(fac[:, :], turns[:, :], -0.5, None, ALU.is_lt))
                        then(v.tensor_tensor(turns[:, :], turns[:, :], wholef[:, :], ALU.subtract))
                        then(v.tensor_tensor(turns[:, :], turns[:, :], fac[:, :], ALU.add))
                        v.wait_ge(wave, 1)
                        v.tensor_scalar(fac[:, :], fac[:, :], 0.5, 0.5, ALU.mult, ALU.add)

                    @block.scalar
                    def _(s):
                        s.wait_ge(step, 8)
                        s.activation(fac[:, :], turns[:, :], ACT.Sin, scale=6.283185).then_inc(wave, 1)

        def stage_cf_edges(acc, fac):
            with ExitStack() as ctx:
                w1 = sb("c_w1", [DE3, D], F32, ctx)
                w2 = sb("c_w2", [P, D], F32, ctx)
                b1 = sb("c_b1", [P, 1], F32, ctx)
                b2 = sb("c_b2", [P, D], F32, ctx)
                filt = sb("c_filt", [P, CT, D], F32, ctx)
                cur = sb("c_cur", [P, NB, H, 2], F32, ctx)
                gidx = sb("c_gidx", [P, NB, H], I32, ctx)
                G = sb("c_G", [P, U, D], F32, ctx)
                ed = sb("c_ed", [DE3, 2, CH], F32, ctx)
                oh = sb("c_oh", [P, NB, H, P], F32, ctx)
                mag = sb("c_mag", [P, 2, CH], F32, ctx)
                pos = sb("c_pos", [P, 2, CH], F32, ctx)
                ssp = sb("c_ssp", [P, 2, CH], F32, ctx)
                ps_lin = [ps(f"c_ps_lin{k}", ctx) for k in range(2)]
                ps_filt = [ps(f"c_ps_filt{k}", ctx) for k in range(2)]
                ps_sum = [ps(f"c_ps_sum{k}", ctx) for k in range(2)]
                loaded = sem("c_loaded")
                cur_ready, gidx_ready, oh_ready = sem("c_cur_ready"), sem("c_gidx_ready"), sem("c_oh_ready")
                linear, act_step, ssp_ready = sem("c_linear"), sem("c_act_step"), sem("c_ssp_ready")
                filtered, filt_ready, message = sem("c_filtered"), sem("c_filt_ready"), sem("c_message")
                edges_in = [sem(f"c_edges_in{b}") for b in range(2)]
                gathered = [sem(f"c_gathered{b}") for b in range(NB)]
                summed, added = sem("c_summed"), sem("c_added")
                with nc.Block() as block:
                    @block.sync
                    def _(sp):
                        loader(sp, loaded, [(w1[:, :], a["l3_w1"]), (w2[:, :], a["l3_w2"]), (b1[:, :], a["l3_b1"]),
                                            (b2[:, :], a["l3_b2"].to_broadcast([P, D]))])

                        def load(i, b):
                            n = NB * i + b
                            at = [sp.value_load(tile_row[0:1, bass.ds(i * U + H * b + q, 1)], min_val=0, max_val=(ET - 1) * P) for q in range(H)]
                            sp.wait_ge(linear, n + 1)
                            sp.nop(nofuse=True)
                            for q in range(H):
                                sp.dma_start(ed[:, b % 2, q * P:(q + 1) * P], a["edge50"][:, bass.ds(at[q], P)]).then_inc(edges_in[b % 2], 16)

                        over_quads(sp, (load, 0))

                    @block.gpsimd
                    def _(g):
                        def gather(i, b):
                            g.wait_ge(gidx_ready, NB * i + b + 1)
                            g.nop(nofuse=True)
                            for q in range(H):
                                g.indirect_dma_start(G[:, H * b + q, :], None, table,
                                                     bass.IndirectOffsetOnAxis(ap=gidx[:, b, q:q + 1], axis=0)).then_inc(gathered[b], 16)

                        over_quads(g, (gather, 0))

                    @block.vector
                    def _(v):
                        v.sem_inc(ssp_ready, 2)
                        v.memset(acc[:, :, :], 0.0).then_inc(added, 2 * H)
                        v.sem_inc(filt_ready, 2)
                        v.sem_inc(message, 1)
                        v.wait_ge(loaded, 64)
                        v.wait_ge(added, 2 * H)

                        def one_hot(i, b):
                            n = NB * i + b
                            v.wait_ge(cur_ready, n + 1)
                            for q in range(H):
                                last = v.tensor_scalar(oh[:, b, q, :], iota[:, :], cur[:, b, q, 0:1], cur[:, b, q, 1:2], ALU.is_equal, ALU.mult)
                            last.then_inc(oh_ready, 1)

                        def make_ssp(i, b):
                            v.wait_ge(act_step, 4 * (NB * i + b) + 4)
                            v.scalar_tensor_tensor(out=ssp[:, b % 2, :], in0=mag[:, b % 2, :], scalar=-LOG2, in1=pos[:, b % 2, :],
                                                   op0=ALU.add, op1=ALU.add).then_inc(ssp_ready, 1)

                        def messages(i, b):
                            n = NB * i + b
                            v.wait_ge(filtered, n + 1)
                            v.wait_ge(message, n + 1)
                            v.tensor_tensor(filt[:, :, :], by_tile(ps_filt[b % 2][:, :]), across(b2[:, :]), ALU.add).then_inc(filt_ready, 1)
                            v.wait_ge(filt_ready, n + 3)
                            v.wait_ge(gathered[b], 16 * H * (i + 1))
                            v.tensor_tensor(G[:, H * b:H * b + H, :], G[:, H * b:H * b + H, :], filt[:, :, :], ALU.mult).then_inc(message, 1)

                        def add_up(i, b):
                            n = NB * i + b
                            bucket = buckets_of(v, n)
                            v.wait_ge(summed, n + 1 + NB)
                            for q in range(H):
                                at = bass.ds(bucket[q], 1)
                                v.wait_ge(added, H * n + q + 2 * H)
                                v.tensor_tensor(acc[:, at, :], acc[:, at, :],
                                                ps_sum[b % 2][:, q * P:(q + 1) * P].rearrange("p (o d) -> p o d", o=1),
                                                ALU.add).then_inc(added, 1)

                        over_quads(v, (one_hot, 0), (make_ssp, 1), (messages, 2), (add_up, 3))

                    @block.scalar
                    def _(s):
                        s.wait_ge(loaded, 64)
                        s.preload_act_table_set("natural_log_exp_and_others")

                        def fetch(i, b):
                            n = NB * i + b
                            s.wait_ge(summed, n + 1)
                            s.copy(gidx[:, b, :], edge_tab[:, bass.ds(i * U + H * b, H), 0]).then_inc(gidx_ready, 1)
                            s.copy(cur[:, b, :, 1], fac[:, bass.ds(i * U + H * b, H)])
                            s.copy(cur[:, b, :, 0], edge_tab[:, bass.ds(i * U + H * b, H), 1]).then_inc(cur_ready, 1)

                        def softplus(i, b):
                            n = NB * i + b
                            u, m, p = ps_lin[b % 2][:, :], mag[:, b % 2, :], pos[:, b % 2, :]
                            s.wait_ge(linear, n + 3)
                            s.wait_ge(ssp_ready, n + 1)
                            s.activation(p, u, ACT.Relu, bias=b1[:, :]).then_inc(act_step, 1)
                            s.activation(m, u, ACT.Abs, bias=b1[:, :]).then_inc(act_step, 1)
                            s.wait_ge(act_step, 4 * n + 2)
                            s.activation(m, m, ACT.Exp, scale=-1.0).then_inc(act_step, 1)
                            s.wait_ge(act_step, 4 * n + 3)
                            s.activation(m, m, ACT.Ln, bias=1.0).then_inc(act_step, 1)

                        over_quads(s, (fetch, 0), (softplus, 0))

                    @block.tensor
                    def _(pe):
                        pe.sem_inc(summed, NB)
                        pe.sem_inc(linear, 2)
                        pe.wait_ge(loaded, 64)

                        def line(i, b):
                            n = NB * i + b
                            pe.wait_ge(edges_in[b % 2], 16 * H * (NB // 2 * i + b // 2 + 1))
                            pe.wait_ge(ssp_ready, n + 1)
                            pe.matmul(ps_lin[b % 2][:, :], w1[:, :], ed[:, b % 2, :], start=True, stop=True).then_inc(linear, 1)

                        def filters(i, b):
                            n = NB * i + b
                            pe.wait_ge(ssp_ready, n + 3)
                            pe.wait_ge(filt_ready, n + 1)
                            for q in range(H):
                                last = pe.matmul(ps_filt[b % 2][:, q * P:(q + 1) * P], ssp[:, b % 2, q * P:(q + 1) * P], w2[:, :],
                                                 start=True, stop=True)
                            last.then_inc(filtered, 1)

                        def make_sums(i, b):
                            n = NB * i + b
                            pe.wait_ge(added, H * n + H)
                            pe.wait_ge(message, n + 2)
                            for q in range(H):
                                last = pe.matmul(ps_sum[b % 2][:, q * P:(q + 1) * P], oh[:, b, q, :], G[:, H * b + q, :], start=True, stop=True)
                            last.then_inc(summed, 1)

                        over_quads(pe, (line, 0), (filters, 1), (make_sums, 2))

        def stage_cf_nodes(acc):
            with ExitStack() as ctx:
                w = sb("f_w", [P, D], F32, ctx)
                bias = sb("f_bias", [P, D], F32, ctx)
                cur = sb("f_cur", [P, CT, D], F32, ctx)
                fm = sb("f_fm", [P, CH], F32, ctx)
                lin = sb("f_lin", [P, CT, D], F32, ctx)
                mag = sb("f_mag", [P, CT, D], F32, ctx)
                pos = sb("f_pos", [P, CT, D], F32, ctx)
                ps_turn, ps_out = ps("f_ps_turn", ctx), ps("f_ps_out", ctx)
                loaded, stored = sem("f_loaded"), sem("f_stored")
                T = Steps(sem("f_tensor_steps"), "turned product")
                V = Steps(sem("f_vector_steps"), "cur lin ssp added")
                S = Steps(sem("f_scalar_steps"), "fm pos mag exp ln")
                with nc.Block() as block:
                    @block.sync
                    def _(sp):
                        loader(sp, loaded, [(w[:, :], a["l3_lin2"]), (bias[:, :], a["l3_lin2_b"].to_broadcast([P, D]))])
                        with sp.Fori(0, NCH) as c:
                            sp.wait_ge(*V.now("added", c))
                            sp.dma_start(out_x[:, chunk(c), :], x[:, chunk(c), :]).then_inc(stored, 16)
                        sp.wait_ge(stored, 16 * NCH)

                    @block.tensor
                    def _(pe):
                        T.start(pe)
                        pe.wait_ge(loaded, 32)
                        with pe.Fori(0, NCH) as c:
                            pe.wait_ge(*V.now("cur", c))
                            pe.wait_ge(*S.before("fm", c))
                            for t in range(CT):
                                last = pe.transpose(ps_turn[:, t * P:(t + 1) * P], cur[:, t, :], ident[:, :])
                            last.then_inc(T.sem, 1)
                            pe.wait_ge(*S.now("fm", c))
                            pe.wait_ge(*V.before("lin", c))
                            for t in range(CT):
                                last = pe.matmul(ps_out[:, t * P:(t + 1) * P], fm[:, t * P:(t + 1) * P], w[:, :], start=True, stop=True)
                            last.then_inc(T.sem, 1)

                    @block.vector
                    def _(v):
                        V.start(v)
                        v.wait_ge(loaded, 32)
                        with v.Fori(0, NCH) as c:
                            v.wait_ge(*T.before("turned", c))
                            v.tensor_copy(cur[:, :, :], acc[:, chunk(c), :]).then_inc(V.sem, 1)
                            v.wait_ge(*T.now("product", c))
                            v.wait_ge(*S.before("ln", c))
                            v.tensor_tensor(lin[:, :, :], by_tile(ps_out[:, :]), across(bias[:, :]), ALU.add).then_inc(V.sem, 1)
                            v.wait_ge(*S.now("ln", c))
                            v.scalar_tensor_tensor(out=pos[:, :, :], in0=mag[:, :, :], scalar=-LOG2, in1=pos[:, :, :], op0=ALU.add,
                                                   op1=ALU.add).then_inc(V.sem, 1)
                            v.wait_ge(*V.now("ssp", c))
                            v.tensor_tensor(x[:, chunk(c), :], x[:, chunk(c), :], pos[:, :, :], ALU.add).then_inc(V.sem, 1)

                    @block.scalar
                    def _(s):
                        S.start(s)
                        s.preload_act_table_set("natural_log_exp_and_others")
                        with s.Fori(0, NCH) as c:
                            s.wait_ge(*T.now("turned", c))
                            s.wait_ge(*T.before("product", c))
                            s.copy(fm[:, :], ps_turn[:, :]).then_inc(S.sem, 1)
                            s.wait_ge(*V.now("lin", c))
                            s.wait_ge(*V.before("added", c))
                            s.activation(pos[:, :, :], lin[:, :, :], ACT.Relu).then_inc(S.sem, 1)
                            s.activation(mag[:, :, :], lin[:, :, :], ACT.Abs).then_inc(S.sem, 1)
                            s.wait_ge(*S.now("mag", c))
                            s.activation(mag[:, :, :], mag[:, :, :], ACT.Exp, scale=-1.0).then_inc(S.sem, 1)
                            s.wait_ge(*S.now("exp", c))
                            s.activation(mag[:, :, :], mag[:, :, :], ACT.Ln, bias=1.0).then_inc(S.sem, 1)

        def stage_ones(one):
            with nc.Block() as block:
                @block.vector
                def _(v):
                    v.memset(one[:, :], 1.0)

        stage_tables()
        stage_done()
        stage_norm("norm0", True)
        stage_done()
        with ExitStack() as l0:
            sum_dst = sb("sum_dst", [P, NT, D], F32, l0)
            stage_gru_edges(sum_dst)
            stage_done()
            stage_gru_nodes(sum_dst)
            stage_done()
        stage_norm("norm1", False)
        stage_done()
        with ExitStack() as l1:
            acc = sb("acc", [P, NT, D], F32, l1)
            y = sb("y", [P, NP], F32, l1)
            dis = sb("dis", [P, NT], F32, l1)
            bn = sb("bn", [P, 2], F32, l1)
            stage_dis(dis)
            stage_done()
            stage_gcn_table("t1", acc, "l1_w1", dis)
            stage_done()
            stage_sum_edges("e1", acc)
            stage_done()
            stage_gcn_norm("n1", acc, dis, y, bn, "l1_par1")
            stage_done()
            stage_gcn_table("t2", acc, "l1_w2", dis, y, bn)
            stage_done()
            stage_sum_edges("e2", acc)
            stage_done()
            stage_gcn_norm("n2", acc, dis, y, bn, "l1_par2")
            stage_done()
            stage_gcn_out(y, bn)
            stage_done()
        stage_norm("norm2", False)
        stage_done()
        with ExitStack() as l2:
            hid = sb("hid", [P, NT, 2 * D], F32, l2)
            with ExitStack() as l2e:
                own = sb("own", [P, NT, 2 * D], F32, l2e)
                stage_mp_tables(own)
                stage_done()
                stage_mp_edges(own, hid)
                stage_done()
            stage_mp_nodes(hid)
            stage_done()
        stage_norm("norm3", False)
        stage_done()
        with ExitStack() as l3:
            acc3 = sb("acc3", [P, NT, D], F32, l3)
            one = sb("one3", [P, NT], F32, l3)
            fac = sb("fac", [P, PG * P], F32, l3)
            stage_ones(one)
            stage_done()
            stage_cutoff(fac)
            stage_done()
            stage_gcn_table("t3", acc3, "l3_lin1", one)
            stage_done()
            stage_cf_edges(acc3, fac)
            stage_done()
            stage_cf_nodes(acc3)
            stage_done()


def laid_out(inputs):
    f = {k: np.asarray(v) for k, v in inputs.items()}
    pad = ET * P - E

    def nm(v):
        v = np.pad(v, ((0, NP - N), (0, 0)))
        return np.ascontiguousarray(v.reshape(NT, P, -1).transpose(1, 0, 2))

    r = {"x": nm(f["x"]), "mask": nm(f["node_vec1"])[:, :, 0].copy()}
    dst = np.pad(f["dst"], (0, pad), constant_values=PAD_NODE).reshape(ET, P)
    r["dst"] = dst
    r["src"] = np.pad(f["src"], (0, pad)).reshape(ET, P)
    r["tile_ends"] = np.ascontiguousarray(dst[:, [0, -1]].T)
    r["edge_weight"] = np.pad(f["edge_weight"], (0, pad)).reshape(ET, P)
    r["edge32"] = np.ascontiguousarray(np.pad(f["edge_attr_32"], ((0, pad), (0, 0))).T)
    r["edge50"] = np.ascontiguousarray(np.pad(f["edge_attr_50"], ((0, pad), (0, 0))).T)
    c = np.ascontiguousarray

    def cut(v, k):
        return c(v.reshape(k, P, -1).transpose(1, 0, 2))

    def cols(*vs):
        return c(np.concatenate([v.reshape(-1, P).T for v in vs], 1))

    r["l0_w12"] = c(np.stack([f["L0_gnn_W1"], f["L0_gnn_W2"]], 1))
    r["l0_wih"] = cut(f["L0_gnn_w_ih"].T, 2)
    r["l0_whh"] = c(f["L0_gnn_w_hh"].T)
    r["l0_bias"] = c(np.stack([cols(f["L0_gnn_b_ih"]), cols(f["L0_gnn_b_hh"])], 1))
    r["l1_w1"], r["l1_w2"] = f["L1_gnn_W1"], f["L1_gnn_W2"]
    r["l1_par1"] = cols(f["L1_gnn_b1"], f["L1_gnn_g1"], f["L1_gnn_bt1"])
    r["l1_par2"] = cols(f["L1_gnn_b2"], f["L1_gnn_g2"], f["L1_gnn_bt2"])
    r["l2_we1n"] = cut(f["L2_gnn_We1"][:2 * D], 2)
    r["l2_we1e"] = c(f["L2_gnn_We1"][2 * D:])
    r["l2_be1"] = f["L2_gnn_be1"][None]
    r["l2_we2"] = cut(f["L2_gnn_We2"], 2)
    r["l2_be2"] = f["L2_gnn_be2"][None]
    r["l2_wn1"] = cut(f["L2_gnn_Wn1"], 2)
    r["l2_bn1"] = cols(f["L2_gnn_bn1"])
    r["l2_wn2"] = cut(f["L2_gnn_Wn2"], 2)
    r["l2_rows"] = c(np.stack([f["L2_gnn_" + k] for k in ("g_msg", "b_msg", "bn2", "g_node", "b_node")]))
    r["l3_w1"] = c(f["L3_gnn_mlp_w1"].T)
    r["l3_b1"] = cols(f["L3_gnn_mlp_b1"])
    r["l3_w2"] = c(f["L3_gnn_mlp_w2"].T)
    r["l3_b2"] = f["L3_gnn_mlp_b2"][None]
    r["l3_lin1"] = c(f["L3_gnn_lin1_w"].T)
    r["l3_lin2"] = c(f["L3_gnn_lin2_w"].T)
    r["l3_lin2_b"] = f["L3_gnn_lin2_b"][None]
    return r


def kernel(**inputs):
    import concourse.bacc as bacc
    from concourse.bass_utils import run_bass_kernel_spmd

    nc = bacc.Bacc("TRN2", target_bir_lowering=False, num_devices=1)
    arrays, args = {}, {}
    for name, v in laid_out(inputs).items():
        arrays[f"in_{name}_dram"] = v
        args[name] = nc.dram_tensor(f"in_{name}_dram", v.shape, mybir.dt.from_np(v.dtype), kind="ExternalInput").ap()
    out = nc.dram_tensor("out_0_dram", (P, NT, D), F32, kind="ExternalOutput").ap()
    build(nc, args, out)
    r = run_bass_kernel_spmd(nc, [arrays], core_ids=[0])
    return r.results[0]["out_0_dram"].transpose(1, 0, 2).reshape(NP, D)[:N]
```
